# Optimizing a Trainium2 kernel written in Bass

```python
import numpy as np
import jax
import jax.numpy as jnp

def _softmax(x, axis=-1):
    return jax.nn.softmax(x, axis=axis)

def _gelu(x):
    return jax.nn.gelu(x, approximate=True)

def _silu(x):
    return jax.nn.silu(x)

def _sigmoid(x):
    return jax.nn.sigmoid(x)

def _layernorm(x, axis=-1, eps=1e-05):
    m = jnp.mean(x, axis=axis, keepdims=True)
    v = jnp.var(x, axis=axis, keepdims=True)
    return (x - m) / jnp.sqrt(v + eps)

def _scatter_add(tgt, idx, src, axis=0):
    return tgt.at[idx].add(src)

def _segment_sum(src, seg, n):
    return jax.ops.segment_sum(src, seg, n)
kernel_name = 'mk_xattn_seq_d4_seqx_r8_d12af2'

def setup_inputs(seed: int=0):
    np.random.seed(seed)
    _w = jnp.asarray

    def _rec_inputs():
        import jax
        import jax.numpy as jnp
        _rk = jax.random.key(seed)
        x = 7.22e-05 + 1 * jax.random.normal(jax.random.fold_in(_rk, 1), (16, 128, 256), jnp.float32)
        _lenS = 128 - jax.random.randint(jax.random.fold_in(_rk, 7), (16,), 0, max(1, 128 // 4) + 1, jnp.int32)
        _lenS2 = 128 - jax.random.randint(jax.random.fold_in(_rk, 8), (16,), 0, max(1, 128 // 4) + 1, jnp.int32)
        _ctx_2048P = jax.random.normal(jax.random.fold_in(_rk, 11), (16, 16, 256), jnp.float32)
        _ctx_2048c = jax.random.dirichlet(jax.random.fold_in(_rk, 511), 0.3 * jnp.ones((16,), jnp.float32), (16, 128))
        _ctx_2048t = jnp.einsum('bsk,bkd->bsd', _ctx_2048c, _ctx_2048P)
        _ctx_2048t = _ctx_2048t * jax.lax.rsqrt(jnp.mean(jnp.square(_ctx_2048t)) + 1e-12) * 0.953939
        ctx_2048 = 4.13588e-05 + 0.999923 * (_ctx_2048t + 0.3 * jax.random.normal(jax.random.fold_in(_rk, 611), (16, 128, 256), jnp.float32))
        _validS = jnp.arange(128)[None, :] < _lenS[:, None]
        _validS2 = jnp.arange(128)[None, :] < _lenS2[:, None]
        _causal = jnp.tril(jnp.ones((128, 128), dtype=bool))
        mask_Bx1xSxS2_ff0 = jnp.where(jnp.ones((16, 1, 128, 128), dtype=bool), 0.0, -1000000000.0).astype(jnp.float32)
        mask_Bx1x2048_bf1 = jnp.ones((16, 1, 256), dtype=bool)
        mask_BxS2_bf1 = jnp.ones((16, 128), dtype=bool)
        return (x, ctx_2048, mask_Bx1xSxS2_ff0, mask_Bx1x2048_bf1, mask_BxS2_bf1)
    x, ctx_2048, mask_Bx1xSxS2_ff0, mask_Bx1x2048_bf1, mask_BxS2_bf1 = _rec_inputs()

    def _L0_xattn_setup():
        import jax, jax.numpy as jnp
        import numpy as np
        H = 256
        NH = 32
        KVH = 8
        HD = H // NH
        GROUPS = NH // KVH
        EPS = 1e-06
        B, L, S = (4, 128, 128)

        def _gqa_forward(hidden_state, encoder_hidden_state, encoder_attention_mask, Wq, bq, Wk, bk, Wv, bv, Wo, bo, gamma, beta):
            b, l, _ = hidden_state.shape
            s = encoder_hidden_state.shape[1]
            q = hidden_state @ Wq + bq
            k = encoder_hidden_state @ Wk + bk
            v = encoder_hidden_state @ Wv + bv
            q = q.reshape(b, l, KVH, GROUPS, HD).transpose(0, 2, 3, 1, 4)
            k = k.reshape(b, s, KVH, HD).transpose(0, 2, 1, 3)
            v = v.reshape(b, s, KVH, HD).transpose(0, 2, 1, 3)
            scale = 1.0 / jnp.sqrt(jnp.asarray(HD, q.dtype))
            scores = jnp.einsum('bkgld,bksd->bkgls', q, k) * scale
            scores = scores + encoder_attention_mask[:, :, None, :, :]
            attn = jax.nn.softmax(scores, axis=-1)
            out = jnp.einsum('bkgls,bksd->bkgld', attn, v)
            out = out.transpose(0, 3, 1, 2, 4).reshape(b, l, H)
            out = out @ Wo + bo
            x = out + hidden_state
            mu = jnp.mean(x, axis=-1, keepdims=True)
            var = jnp.var(x, axis=-1, keepdims=True)
            return (x - mu) * jax.lax.rsqrt(var + EPS) * gamma + beta
        key = jax.random.key(seed)
        ks = jax.random.split(key, 12)
        sd = 0.02
        return {'hidden_state': jax.random.normal(ks[0], (B, L, H), jnp.float32), 'encoder_hidden_state': jax.random.normal(ks[1], (B, S, H), jnp.float32), 'encoder_attention_mask': jnp.zeros((B, 1, L, S), jnp.float32), 'Wq': jax.random.normal(ks[2], (H, H), jnp.float32) * sd, 'bq': jnp.zeros((H,), jnp.float32), 'Wk': jax.random.normal(ks[3], (H, KVH * HD), jnp.float32) * sd, 'bk': jnp.zeros((KVH * HD,), jnp.float32), 'Wv': jax.random.normal(ks[4], (H, KVH * HD), jnp.float32) * sd, 'bv': jnp.zeros((KVH * HD,), jnp.float32), 'Wo': jax.random.normal(ks[5], (H, H), jnp.float32) * sd, 'bo': jnp.zeros((H,), jnp.float32), 'gamma': jnp.ones((H,), jnp.float32), 'beta': jnp.zeros((H,), jnp.float32)}
    _L0_xattn_all = _L0_xattn_setup()
    _L0_xattn_in = {k: v for k, v in _L0_xattn_all.items() if k in ('Wq', 'bq', 'Wk', 'bk', 'Wv', 'bv', 'Wo', 'bo', 'gamma', 'beta')}
    del _L0_xattn_all

    def _L1_xattn_setup():
        import jax, jax.numpy as jnp
        import numpy as np
        import math
        N_HEADS = 16
        EPS = 1e-05

        def _masked_instance_norm(x, mask):
            m = mask.astype(x.dtype)
            x = x * m
            n_valid = jnp.sum(m, axis=-1, keepdims=True)
            mean = jnp.sum(x, axis=-1, keepdims=True) / n_valid
            var = jnp.sum(x * x, axis=-1, keepdims=True) / n_valid - mean * mean
            x = (x - mean) / jnp.sqrt(jax.nn.relu(var) + EPS)
            return x * m
        key = jax.random.key(seed)
        ks = jax.random.split(key, 8)
        bs, c, t1, t2 = (2, 128, 256, 256)
        s = 1.0 / math.sqrt(c)
        return {'x': jax.random.normal(ks[0], (bs, c, t1), jnp.float32), 'mask': jnp.ones((bs, 1, t1), jnp.bool_), 'kv': jax.random.normal(ks[1], (bs, c, t2), jnp.float32), 'kv_mask': jnp.ones((bs, 1, t2), jnp.bool_), 'Wq': jax.random.normal(ks[2], (c, c), jnp.float32) * s, 'bq': jnp.zeros((c,), jnp.float32), 'Wk': jax.random.normal(ks[3], (c, c), jnp.float32) * s, 'bk': jnp.zeros((c,), jnp.float32), 'Wv': jax.random.normal(ks[4], (c, c), jnp.float32) * s, 'bv': jnp.zeros((c,), jnp.float32)}
    _L1_xattn_all = _L1_xattn_setup()
    _L1_xattn_in = {k: v for k, v in _L1_xattn_all.items() if k in ('Wq', 'bq', 'Wk', 'bk', 'Wv', 'bv')}
    del _L1_xattn_all

    def _L2_xattn_setup():
        import jax, jax.numpy as jnp
        import numpy as np
        HIDDEN = 256
        HEADS = 16
        HEAD_DIM = HIDDEN // HEADS
        LN_EPS = 1e-05
        GATE_INIT = 0.5

        def _layer_norm(x, gamma, beta):
            mu = jnp.mean(x, axis=-1, keepdims=True)
            var = jnp.mean(jnp.square(x - mu), axis=-1, keepdims=True)
            return (x - mu) * jax.lax.rsqrt(var + LN_EPS) * gamma + beta
        key = jax.random.key(seed)
        ks = jax.random.split(key, 8)
        B, T_TEXT, T_AUDIO = (4, 256, 1500)
        s = 0.02
        return {'hidden_states': jax.random.normal(ks[0], (B, T_TEXT, HIDDEN), jnp.float32), 'audio_kv': jax.random.normal(ks[1], (B, T_AUDIO, HIDDEN), jnp.float32), 'audio_attention_mask': jnp.ones((B, T_AUDIO), dtype=bool), 'Wq': jax.random.normal(ks[2], (HIDDEN, HIDDEN), jnp.float32) * s, 'Wk': jax.random.normal(ks[3], (HIDDEN, HIDDEN), jnp.float32) * s, 'Wv': jax.random.normal(ks[4], (HIDDEN, HIDDEN), jnp.float32) * s, 'Wo': jax.random.normal(ks[5], (HIDDEN, HIDDEN), jnp.float32) * s, 'ln_gamma': jnp.ones((HIDDEN,), jnp.float32), 'ln_beta': jnp.zeros((HIDDEN,), jnp.float32), 'gate': jnp.array([GATE_INIT], jnp.float32)}
    _L2_xattn_all = _L2_xattn_setup()
    _L2_xattn_in = {k: v for k, v in _L2_xattn_all.items() if k in ('Wq', 'Wk', 'Wv', 'Wo', 'ln_gamma', 'ln_beta', 'gate')}
    del _L2_xattn_all

    def _L3_xattn_setup():
        import jax, jax.numpy as jnp
        import numpy as np
        B, L, E, H = (4, 64, 256, 32)
        S = E // H
        EXTRA_MAA, EXTRA_DECAY = (32, 64)
        EPS = 1e-05

        def _ln(x, w, b):
            m = jnp.mean(x, axis=-1, keepdims=True)
            v = jnp.mean((x - m) ** 2, axis=-1, keepdims=True)
            return (x - m) * jax.lax.rsqrt(v + EPS) * w + b

        def _token_shift(xn, prev_row):
            first = (prev_row - xn[:, 0])[:, None]
            rest = xn[:, :-1] - xn[:, 1:]
            return jnp.concatenate([first, rest], axis=1)
        key = jax.random.key(seed)
        ks = jax.random.split(key, 24)
        rn = lambda k, shp, s=1.0: jax.random.normal(k, shp, dtype=jnp.float32) * s
        return dict(x=rn(ks[0], (B, L, E)), state=rn(ks[1], (B, 2 + S, E), 0.1), ln1_w=jnp.ones((E,), jnp.float32), ln1_b=jnp.zeros((E,), jnp.float32), ln2_w=jnp.ones((E,), jnp.float32), ln2_b=jnp.zeros((E,), jnp.float32), maa_x=rn(ks[2], (E,), 0.02), maa_w1=rn(ks[3], (E, 5 * EXTRA_MAA), 0.02), maa_w2=rn(ks[4], (5, EXTRA_MAA, E), 0.02), maa_stack=rn(ks[5], (5, E), 0.02), time_decay=rn(ks[6], (E,), 0.5), decay_w1=rn(ks[7], (E, EXTRA_DECAY), 0.02), decay_w2=rn(ks[8], (EXTRA_DECAY, E), 0.02), faaaa=rn(ks[9], (H, S), 0.1), Wr=rn(ks[10], (E, E), 0.02), Wk=rn(ks[11], (E, E), 0.02), Wv=rn(ks[12], (E, E), 0.02), Wg=rn(ks[13], (E, E), 0.02), Wo=rn(ks[14], (E, E), 0.02), gn_w=jnp.ones((E,), jnp.float32), gn_b=jnp.zeros((E,), jnp.float32), ffn_maa_k=rn(ks[15], (E,), 0.02), ffn_maa_r=rn(ks[16], (E,), 0.02), ffn_Wk=rn(ks[17], (E, E), 0.02), ffn_Wr=rn(ks[18], (E, E), 0.02), ffn_Wv=rn(ks[19], (E, E), 0.02), i=0)
    _L3_xattn_all = _L3_xattn_setup()
    _L3_xattn_in = {k: v for k, v in _L3_xattn_all.items() if k in ('ln1_w', 'ln1_b', 'ln2_w', 'ln2_b', 'maa_x', 'maa_w1', 'maa_w2', 'maa_stack', 'time_decay', 'decay_w1', 'decay_w2', 'faaaa', 'Wr', 'Wk', 'Wv', 'Wg', 'Wo', 'gn_w', 'gn_b', 'ffn_maa_k', 'ffn_maa_r', 'ffn_Wk', 'ffn_Wr', 'ffn_Wv')}
    del _L3_xattn_all
    return {'x': x, 'ctx_2048': ctx_2048, 'mask_Bx1xSxS2_ff0': mask_Bx1xSxS2_ff0, 'mask_Bx1x2048_bf1': mask_Bx1x2048_bf1, 'mask_BxS2_bf1': mask_BxS2_bf1, 'L0_xattn_Wq': _L0_xattn_in['Wq'], 'L0_xattn_bq': _L0_xattn_in['bq'], 'L0_xattn_Wk': _L0_xattn_in['Wk'], 'L0_xattn_bk': _L0_xattn_in['bk'], 'L0_xattn_Wv': _L0_xattn_in['Wv'], 'L0_xattn_bv': _L0_xattn_in['bv'], 'L0_xattn_Wo': _L0_xattn_in['Wo'], 'L0_xattn_bo': _L0_xattn_in['bo'], 'L0_xattn_gamma': _L0_xattn_in['gamma'], 'L0_xattn_beta': _L0_xattn_in['beta'], 'L1_xattn_Wq': _L1_xattn_in['Wq'], 'L1_xattn_bq': _L1_xattn_in['bq'], 'L1_xattn_Wk': _L1_xattn_in['Wk'], 'L1_xattn_bk': _L1_xattn_in['bk'], 'L1_xattn_Wv': _L1_xattn_in['Wv'], 'L1_xattn_bv': _L1_xattn_in['bv'], 'L2_xattn_Wq': _L2_xattn_in['Wq'], 'L2_xattn_Wk': _L2_xattn_in['Wk'], 'L2_xattn_Wv': _L2_xattn_in['Wv'], 'L2_xattn_Wo': _L2_xattn_in['Wo'], 'L2_xattn_ln_gamma': _L2_xattn_in['ln_gamma'], 'L2_xattn_ln_beta': _L2_xattn_in['ln_beta'], 'L2_xattn_gate': _L2_xattn_in['gate'], 'L3_xattn_ln1_w': _L3_xattn_in['ln1_w'], 'L3_xattn_ln1_b': _L3_xattn_in['ln1_b'], 'L3_xattn_ln2_w': _L3_xattn_in['ln2_w'], 'L3_xattn_ln2_b': _L3_xattn_in['ln2_b'], 'L3_xattn_maa_x': _L3_xattn_in['maa_x'], 'L3_xattn_maa_w1': _L3_xattn_in['maa_w1'], 'L3_xattn_maa_w2': _L3_xattn_in['maa_w2'], 'L3_xattn_maa_stack': _L3_xattn_in['maa_stack'], 'L3_xattn_time_decay': _L3_xattn_in['time_decay'], 'L3_xattn_decay_w1': _L3_xattn_in['decay_w1'], 'L3_xattn_decay_w2': _L3_xattn_in['decay_w2'], 'L3_xattn_faaaa': _L3_xattn_in['faaaa'], 'L3_xattn_Wr': _L3_xattn_in['Wr'], 'L3_xattn_Wk': _L3_xattn_in['Wk'], 'L3_xattn_Wv': _L3_xattn_in['Wv'], 'L3_xattn_Wg': _L3_xattn_in['Wg'], 'L3_xattn_Wo': _L3_xattn_in['Wo'], 'L3_xattn_gn_w': _L3_xattn_in['gn_w'], 'L3_xattn_gn_b': _L3_xattn_in['gn_b'], 'L3_xattn_ffn_maa_k': _L3_xattn_in['ffn_maa_k'], 'L3_xattn_ffn_maa_r': _L3_xattn_in['ffn_maa_r'], 'L3_xattn_ffn_Wk': _L3_xattn_in['ffn_Wk'], 'L3_xattn_ffn_Wr': _L3_xattn_in['ffn_Wr'], 'L3_xattn_ffn_Wv': _L3_xattn_in['ffn_Wv']}

def reference(x, ctx_2048, mask_Bx1xSxS2_ff0, mask_Bx1x2048_bf1, mask_BxS2_bf1, L0_xattn_Wq, L0_xattn_bq, L0_xattn_Wk, L0_xattn_bk, L0_xattn_Wv, L0_xattn_bv, L0_xattn_Wo, L0_xattn_bo, L0_xattn_gamma, L0_xattn_beta, L1_xattn_Wq, L1_xattn_bq, L1_xattn_Wk, L1_xattn_bk, L1_xattn_Wv, L1_xattn_bv, L2_xattn_Wq, L2_xattn_Wk, L2_xattn_Wv, L2_xattn_Wo, L2_xattn_ln_gamma, L2_xattn_ln_beta, L2_xattn_gate, L3_xattn_ln1_w, L3_xattn_ln1_b, L3_xattn_ln2_w, L3_xattn_ln2_b, L3_xattn_maa_x, L3_xattn_maa_w1, L3_xattn_maa_w2, L3_xattn_maa_stack, L3_xattn_time_decay, L3_xattn_decay_w1, L3_xattn_decay_w2, L3_xattn_faaaa, L3_xattn_Wr, L3_xattn_Wk, L3_xattn_Wv, L3_xattn_Wg, L3_xattn_Wo, L3_xattn_gn_w, L3_xattn_gn_b, L3_xattn_ffn_maa_k, L3_xattn_ffn_maa_r, L3_xattn_ffn_Wk, L3_xattn_ffn_Wr, L3_xattn_ffn_Wv):
    import jax
    import jax.numpy as jnp

    def _L0_xattn_ref(hidden_state, encoder_hidden_state, encoder_attention_mask, Wq, bq, Wk, bk, Wv, bv, Wo, bo, gamma, beta):
        import jax, jax.numpy as jnp
        import numpy as np
        H = 256
        NH = 32
        KVH = 8
        HD = H // NH
        GROUPS = NH // KVH
        EPS = 1e-06
        B, L, S = (4, 128, 128)

        def _gqa_forward(hidden_state, encoder_hidden_state, encoder_attention_mask, Wq, bq, Wk, bk, Wv, bv, Wo, bo, gamma, beta):
            b, l, _ = hidden_state.shape
            s = encoder_hidden_state.shape[1]
            q = hidden_state @ Wq + bq
            k = encoder_hidden_state @ Wk + bk
            v = encoder_hidden_state @ Wv + bv
            q = q.reshape(b, l, KVH, GROUPS, HD).transpose(0, 2, 3, 1, 4)
            k = k.reshape(b, s, KVH, HD).transpose(0, 2, 1, 3)
            v = v.reshape(b, s, KVH, HD).transpose(0, 2, 1, 3)
            scale = 1.0 / jnp.sqrt(jnp.asarray(HD, q.dtype))
            scores = jnp.einsum('bkgld,bksd->bkgls', q, k) * scale
            scores = scores + encoder_attention_mask[:, :, None, :, :]
            attn = jax.nn.softmax(scores, axis=-1)
            out = jnp.einsum('bkgls,bksd->bkgld', attn, v)
            out = out.transpose(0, 3, 1, 2, 4).reshape(b, l, H)
            out = out @ Wo + bo
            x = out + hidden_state
            mu = jnp.mean(x, axis=-1, keepdims=True)
            var = jnp.var(x, axis=-1, keepdims=True)
            return (x - mu) * jax.lax.rsqrt(var + EPS) * gamma + beta
        return _gqa_forward(hidden_state, encoder_hidden_state, encoder_attention_mask, Wq, bq, Wk, bk, Wv, bv, Wo, bo, gamma, beta)

    def _L1_xattn_ref(x, mask, kv, kv_mask, Wq, bq, Wk, bk, Wv, bv):
        import jax, jax.numpy as jnp
        import numpy as np
        import math
        N_HEADS = 16
        EPS = 1e-05

        def _masked_instance_norm(x, mask):
            m = mask.astype(x.dtype)
            x = x * m
            n_valid = jnp.sum(m, axis=-1, keepdims=True)
            mean = jnp.sum(x, axis=-1, keepdims=True) / n_valid
            var = jnp.sum(x * x, axis=-1, keepdims=True) / n_valid - mean * mean
            x = (x - mean) / jnp.sqrt(jax.nn.relu(var) + EPS)
            return x * m
        bs, c, t1 = x.shape
        h = N_HEADS
        d = c // h
        scale = 1.0 / math.sqrt(d)
        q = jnp.einsum('oc,bct->bot', Wq, x) + bq[None, :, None]
        k = jnp.einsum('oc,bct->bot', Wk, kv) + bk[None, :, None]
        v = jnp.einsum('oc,bct->bot', Wv, kv) + bv[None, :, None]
        q = q.reshape(bs, h, d, t1).transpose(0, 1, 3, 2)
        k = k.reshape(bs, h, d, -1)
        v = v.reshape(bs, h, d, -1).transpose(0, 1, 3, 2)
        attn = jnp.einsum('bhqd,bhdk->bhqk', q * scale, k)
        attn = jnp.where(kv_mask[:, :, None, :], attn, -jnp.inf)
        attn = jax.nn.softmax(attn, axis=-1)
        mean = jnp.einsum('bhqk,bhkd->bhqd', attn, v)
        ex2 = jnp.einsum('bhqk,bhkd->bhqd', attn, v * v)
        std = jnp.sqrt(jax.nn.relu(ex2 - mean * mean))
        mean = mean.transpose(0, 1, 3, 2).reshape(bs, c, t1)
        std = std.transpose(0, 1, 3, 2).reshape(bs, c, t1)
        xn = _masked_instance_norm(x, mask)
        out = (xn * std + mean) * mask.astype(x.dtype)
        return out

    def _L2_xattn_ref(hidden_states, audio_kv, audio_attention_mask, Wq, Wk, Wv, Wo, ln_gamma, ln_beta, gate):
        import jax, jax.numpy as jnp
        import numpy as np
        HIDDEN = 256
        HEADS = 16
        HEAD_DIM = HIDDEN // HEADS
        LN_EPS = 1e-05
        GATE_INIT = 0.5

        def _layer_norm(x, gamma, beta):
            mu = jnp.mean(x, axis=-1, keepdims=True)
            var = jnp.mean(jnp.square(x - mu), axis=-1, keepdims=True)
            return (x - mu) * jax.lax.rsqrt(var + LN_EPS) * gamma + beta
        B, Tt, D = hidden_states.shape
        Ta = audio_kv.shape[1]
        scale = HEAD_DIM ** (-0.5)
        a = _layer_norm(audio_kv, ln_gamma, ln_beta)
        Q = (hidden_states @ Wq.T).reshape(B, Tt, HEADS, HEAD_DIM).transpose(0, 2, 1, 3)
        K = (a @ Wk.T).reshape(B, Ta, HEADS, HEAD_DIM).transpose(0, 2, 1, 3)
        V = (a @ Wv.T).reshape(B, Ta, HEADS, HEAD_DIM).transpose(0, 2, 1, 3)
        scores = jnp.einsum('bhtd,bhsd->bhts', Q, K) * scale
        mask = audio_attention_mask[:, None, None, :]
        scores = jnp.where(mask, scores, jnp.float32(-jnp.inf))
        attn = jax.nn.softmax(scores, axis=-1)
        out = jnp.einsum('bhts,bhsd->bhtd', attn, V)
        out = out.transpose(0, 2, 1, 3).reshape(B, Tt, D)
        out = out @ Wo.T
        return hidden_states + jnp.tanh(gate) * out

    def _L3_xattn_ref(x, state, ln1_w, ln1_b, ln2_w, ln2_b, maa_x, maa_w1, maa_w2, maa_stack, time_decay, decay_w1, decay_w2, faaaa, Wr, Wk, Wv, Wg, Wo, gn_w, gn_b, ffn_maa_k, ffn_maa_r, ffn_Wk, ffn_Wr, ffn_Wv, i):
        import jax, jax.numpy as jnp
        import numpy as np
        B, L, E, H = (4, 64, 256, 32)
        S = E // H
        EXTRA_MAA, EXTRA_DECAY = (32, 64)
        EPS = 1e-05

        def _ln(x, w, b):
            m = jnp.mean(x, axis=-1, keepdims=True)
            v = jnp.mean((x - m) ** 2, axis=-1, keepdims=True)
            return (x - m) * jax.lax.rsqrt(v + EPS) * w + b

        def _token_shift(xn, prev_row):
            first = (prev_row - xn[:, 0])[:, None]
            rest = xn[:, :-1] - xn[:, 1:]
            return jnp.concatenate([first, rest], axis=1)
        b, l = (x.shape[0], x.shape[1])
        i0 = (2 + S) * i + 0
        i1 = (2 + S) * i + 1
        xn = _ln(x, ln1_w, ln1_b)
        sx = _token_shift(xn, state[:, i1])
        xxx = jnp.tanh((xn + sx * maa_x) @ maa_w1).reshape(b, l, 5, 1, EXTRA_MAA)
        xxx = jnp.matmul(xxx, maa_w2).reshape(b, l, 5, E)
        x5 = xn[:, :, None] + sx[:, :, None] * (maa_stack + xxx)
        w = jnp.exp(-jnp.exp(time_decay + jnp.tanh(x5[:, :, 1] @ decay_w1) @ decay_w2))
        w = w.reshape(b, l, H, S)
        r = (x5[:, :, 3] @ Wr.T).reshape(b, l, H, S)
        k = (x5[:, :, 0] @ Wk.T).reshape(b, l, H, S)
        v = (x5[:, :, 2] @ Wv.T).reshape(b, l, H, S)
        g = jax.nn.silu(x5[:, :, 4] @ Wg.T)
        s0 = state[:, (2 + S) * i + 2:(2 + S) * (i + 1)].reshape(b, H, S, S)
        u = faaaa[None, :, :, None]

        def step(s, rkvw):
            r_t, k_t, v_t, w_t = rkvw
            a = k_t[:, :, :, None] * v_t[:, :, None, :]
            out = jnp.einsum('bhk,bhkd->bhd', r_t, u * a + s)
            return (a + w_t[:, :, :, None] * s, out)
        xs = tuple((jnp.moveaxis(t, 1, 0) for t in (r, k, v, w)))
        _, outs = jax.lax.scan(step, s0, xs)
        att = jnp.moveaxis(outs, 0, 1).reshape(b, l, E)
        a4 = att.reshape(b, l, H, S)
        m = jnp.mean(a4, axis=-1, keepdims=True)
        var = jnp.mean((a4 - m) ** 2, axis=-1, keepdims=True)
        att = ((a4 - m) * jax.lax.rsqrt(var + EPS)).reshape(b, l, E) * gn_w + gn_b
        x = x + att * g @ Wo.T
        xn2 = _ln(x, ln2_w, ln2_b)
        sx2 = _token_shift(xn2, state[:, i0])
        xk = xn2 + sx2 * ffn_maa_k
        xr = xn2 + sx2 * ffn_maa_r
        rr = jax.nn.sigmoid(xr @ ffn_Wr.T)
        kk = jnp.square(jax.nn.relu(xk @ ffn_Wk.T))
        x = x + rr * (kk @ ffn_Wv.T)
        return x
    x = _L0_xattn_ref(x, ctx_2048, mask_Bx1xSxS2_ff0, L0_xattn_Wq, L0_xattn_bq, L0_xattn_Wk, L0_xattn_bk, L0_xattn_Wv, L0_xattn_bv, L0_xattn_Wo, L0_xattn_bo, L0_xattn_gamma, L0_xattn_beta)
    x = _L1_xattn_ref(x, mask_Bx1x2048_bf1, ctx_2048, mask_Bx1x2048_bf1, L1_xattn_Wq, L1_xattn_bq, L1_xattn_Wk, L1_xattn_bk, L1_xattn_Wv, L1_xattn_bv)
    x = _L2_xattn_ref(x, ctx_2048, mask_BxS2_bf1, L2_xattn_Wq, L2_xattn_Wk, L2_xattn_Wv, L2_xattn_Wo, L2_xattn_ln_gamma, L2_xattn_ln_beta, L2_xattn_gate)
    x = _L3_xattn_ref(x, ctx_2048, L3_xattn_ln1_w, L3_xattn_ln1_b, L3_xattn_ln2_w, L3_xattn_ln2_b, L3_xattn_maa_x, L3_xattn_maa_w1, L3_xattn_maa_w2, L3_xattn_maa_stack, L3_xattn_time_decay, L3_xattn_decay_w1, L3_xattn_decay_w2, L3_xattn_faaaa, L3_xattn_Wr, L3_xattn_Wk, L3_xattn_Wv, L3_xattn_Wg, L3_xattn_Wo, L3_xattn_gn_w, L3_xattn_gn_b, L3_xattn_ffn_maa_k, L3_xattn_ffn_maa_r, L3_xattn_ffn_Wk, L3_xattn_ffn_Wr, L3_xattn_ffn_Wv, 0)
    return x

_drawn_inputs = setup_inputs


def setup_inputs(seed=0):
    import zlib

    import numpy as np

    out = dict(_drawn_inputs(seed))
    spreads = {'L0_xattn_bq': (0.0, 0.8),
     'L0_xattn_bk': (0.0, 0.8),
     'L0_xattn_bv': (0.0, 0.1),
     'L0_xattn_bo': (0.0, 0.1),
     'L0_xattn_gamma': (1.0, 0.2),
     'L0_xattn_beta': (0.0, 0.1),
     'L1_xattn_bq': (0.0, 0.1),
     'L1_xattn_bk': (0.0, 0.8),
     'L1_xattn_bv': (0.0, 0.1),
     'L2_xattn_ln_gamma': (1.0, 0.6),
     'L2_xattn_ln_beta': (0.0, 0.8),
     'L3_xattn_ln1_w': (1.0, 0.547),
     'L3_xattn_ln1_b': (0.0, 0.551),
     'L3_xattn_ln2_w': (1.0, 0.6),
     'L3_xattn_ln2_b': (0.0, 0.8),
     'L3_xattn_gn_w': (1.0, 0.6),
     'L3_xattn_gn_b': (0.0, 0.8)}
    factors = {'L0_xattn_Wq': 8.0,
     'L0_xattn_Wk': 8.0,
     'L2_xattn_Wq': 8.0,
     'L2_xattn_Wk': 8.0,
     'L3_xattn_maa_x': 8.0,
     'L3_xattn_maa_w1': 7.51,
     'L3_xattn_maa_w2': 7.495,
     'L3_xattn_maa_stack': 8.0,
     'L3_xattn_time_decay': 2.79,
     'L3_xattn_decay_w1': 8.0,
     'L3_xattn_decay_w2': 8.0,
     'L3_xattn_faaaa': 5.525,
     'L3_xattn_ffn_maa_k': 8.0,
     'L3_xattn_ffn_maa_r': 8.0,
     'L3_xattn_ffn_Wk': 2.801,
     'L3_xattn_ffn_Wr': 8.0}
    for name, (base, spread) in spreads.items():
        noise = np.random.default_rng([zlib.crc32(name.encode()), seed]).standard_normal(out[name].shape)
        drawn = base * np.exp(spread * noise) if base else spread * noise
        out[name] = jnp.asarray(drawn.astype(out[name].dtype))
    for name, factor in factors.items():
        out[name] = (out[name] * factor).astype(out[name].dtype)
    return out
```

```python
from contextlib import ExitStack


import concourse.bass as bass
from concourse import mybir

F32, F16, BF16, U8 = mybir.dt.float32, mybir.dt.float16, mybir.dt.bfloat16, mybir.dt.uint8
ALU = mybir.AluOpType
ACT = mybir.ActivationFunctionType
X_AXIS = mybir.AxisListType.X

P = 128
B, T, D = 16, 128, 256
NC = D // P
H0, KV0, HD0 = 32, 8, 8
H1, HD1 = 16, 8
H2, HD2 = 16, 16
H3, S3 = 32, 8
QB = 32
QB2 = 64
NEG = 60000.0

W_COLS = {}
_at = 0
for _name, _n in (("q0", 256), ("kv0", 128), ("o0", 256), ("kv2", 512), ("q2", 256), ("o2", 256),
                  ("maa1", 160), ("dec1", 64), ("r3", 256), ("k3", 256), ("v3", 256), ("g3", 256),
                  ("o3", 256), ("fk3", 256), ("fr3", 256), ("fv3", 256)):
    W_COLS[_name] = (_at, _at + _n)
    _at += _n
W_TOTAL = _at
R_COLS = {"bq0": (0, 256), "bkv0": (256, 384), "bo0": (384, 640), "bq1": (640, 768), "bkv1": (768, 1024)}
R_TOTAL = 1024
BC = {"gamma0": 0, "beta0": 1, "gnw": 2, "gnb": 3}
COL = {n: k for k, n in enumerate(("lng2", "lnb2", "ln1w", "ln1b", "ln2w", "ln2b", "maax", "st0", "st1", "st2",
                                   "st3", "st4", "td", "u", "fmk", "fmr"))}

PER = dict(
    x_in=16, c_in=16, m0_in=16, mx_in=16, s0_in=16, out_stored=16, batch_done=1,
    dve=54, act=3, pool=16,
    xc_t=1, xc_sb=1, proj0=1, hi0=4, lo0=2, packed0_t=2, qt_sb=3, kt_sb=3,
    scores=56, max_read=14, exp_done=14, pv_done=28, m_t=3, m_sb=3, nm=3, mxf=1, 
    o_norm=3, o_t=2, ot_sb=2, res=2,
    var_in=5, rstd=5,
    proj1=1, hi1=6, lo1=2, packed1_t=2, var1=1, std1=1, ms_t=1, xn1=1,
    x2=1, x2_t=1, x2_sb=1, c_hat=1, c_t=1, ct2_sb=2, proj2=1, hi2=4, lo2=2, packed2_t=2,
    mask_parts=1,
    xh_t=2, xnt=4, xm=1, xxx=1, xxt=2, mix=5, t5=5, x5=5, wd_ps=1, wd=1, w_ps=1, ws=1,
    kr_ps=1, v_ps=1, g_ps=1, krv_sb=4, vd=4, sc=4, pr=4, att_ps=1, ruk=1, gt=1,
    d8=1, sq=1, v8=1, r8=1, y=1, y_t=1, yt_sb=1, y_o=1, xkr=4, ff1=1, kk=1, tr=1, ff2=1,
    x3=1, x4=1, xh=2, x1=1,
)


def build(nc, x, ctx_in, mask0, mask1, mask2, wall, w1, maaw2, decw2, rows, bcast, cols, gate,
          ident, ident_h, ident_b, pick0, pick1, gsel, srep, out):
    with ExitStack() as ctx:
        def sb(name, shape, dt=F32):
            return ctx.enter_context(nc.sbuf_tensor(name, shape, dt))

        W = sb("W", [P, NC, W_TOTAL])
        W1 = sb("W1", [P, 3 * P])
        MAA2 = sb("MAA2", [P, D])
        MAA2b = sb("MAA2b", [32, D])
        DEC2 = sb("DEC2", [64, D])
        ROWS = sb("ROWS", [1, R_TOTAL])
        BCR = sb("BCR", [P, 4, D])
        CV = sb("CV", [P, NC, 16])
        ID = sb("ID", [P, P])
        IDH = sb("IDH", [P, P], F16)
        IDB = sb("IDB", [P, P], BF16)
        PICK0 = sb("PICK0", [P, 32], BF16)
        PICK1 = sb("PICK1", [P, 16], BF16)
        GSEL = sb("GSEL", [P, 16])
        SREP = sb("SREP", [P, 8, P])
        IDLE = sb("IDLE", [P, 2])
        GATE = sb("GATE", [P, 1])
        TG = sb("TG", [P, 1])
        ONES = sb("ONES", [1, P])
        NHALF = sb("NHALF", [P, 32])
        MRAW1 = sb("MRAW1", [16, 2 * P], U8)
        MRAW2 = sb("MRAW2", [16, P], U8)
        MF = sb("MF", [16, 3 * P], F16)
        KM1 = sb("KM1", [P, 16, 2], F16)
        KM2 = sb("KM2", [P, 16, 1], F16)
        X = sb("X", [P, D])
        C = sb("C", [P, D])
        M0 = sb("M0", [P, P])
        MXR = sb("MXR", [P, D], U8)
        S0 = sb("S0", [P, NC, S3])
        CXT = sb("CXT", [P, 4, P])
        MP = sb("MP", [P, 3, P], BF16)
        MR = sb("MR", [P, P])
        QN0 = sb("QN0", [P, H0, QB], F16)
        KN0 = sb("KN0", [P, KV0, 4, QB], F16)
        V0 = sb("V0", [P, KV0, HD0 + 1])
        QN1 = sb("QN1", [P, 2 * H1, QB], F16)
        KN1 = sb("KN1", [P, 2 * H1, QB], F16)
        V1 = sb("V1", [P, 2 * H1, 2 * HD1 + 1])
        QN2 = sb("QN2", [P, H2, QB2], F16)
        KN2 = sb("KN2", [P, H2, QB2], F16)
        V2 = sb("V2", [P, H2, HD2 + 1])
        QT = sb("QT", [P, 8, P], F16)
        KT = sb("KT", [P, 8, P], F16)
        NM = sb("NM", [P, 32])
        NR = sb("NR", [P, 32])
        MN = sb("MN", [P, 2, P], BF16)
        MT = sb("MT", [P, 2 * P], BF16)
        PR_ = sb("PR_", [P, 8, 512])
        RS = sb("RS", [P, 32])
        ON = sb("ON", [P, D])
        OT = sb("OT", [P, NC, P])
        X1 = sb("X1", [P, D])
        XH = sb("XH", [P, D])
        ST = sb("ST", [P, 6])
        MV = sb("MV", [P, 2])
        VE = sb("VE", [P, 32])
        RSTD = sb("RSTD", [P, 1])
        MXF = sb("MXF", [P, D])
        XM1 = sb("XM1", [P, D])
        XN1 = sb("XN1", [P, D])
        SM = sb("SM", [P, 8])
        MEAN = sb("MEAN", [P, 2, P])
        VAR = sb("VAR", [P, 2, P])
        EX2 = sb("EX2", [P, 2, P])
        STD = sb("STD", [P, 2, P])
        X2 = sb("X2", [P, D])
        X2T = sb("X2T", [P, NC, P])
        CH = sb("CH", [P, D])
        CT2 = sb("CT2", [P, NC, P])
        X3 = sb("X3", [P, D])
        XNT = sb("XNT", [P, NC, P + 1])
        SX = sb("SX", [P, NC, P])
        XM = sb("XM", [P, NC, P])
        XXT = sb("XXT", [P, P])
        XXT4 = sb("XXT4", [32, P])
        T5 = sb("T5", [P, 5, NC, P])
        X5 = sb("X5", [P, 5, NC, P])
        WD = sb("WD", [64, P])
        EW = sb("EW", [P, NC, P])
        WS = sb("WS", [P, 2, NC, P])
        KR = sb("KR", [P, 2, NC, P])
        VT3 = sb("VT3", [P, NC, P])
        VN3 = sb("VN3", [P, D])
        A3 = sb("A3", [P, 8, NC, P])
        SC3 = sb("SC3", [P, 8, NC, P])
        PR3 = sb("PR3", [P, 8, NC, P])
        RUK = sb("RUK", [P, NC, P])
        ATT = sb("ATT", [P, D])
        DD = sb("DD", [P, D])
        SQ = sb("SQ", [P, D])
        G8 = sb("G8", [P, 3, 32])
        GT = sb("GT", [P, D])
        Y = sb("Y", [P, D])
        YT = sb("YT", [P, NC, P])
        X4 = sb("X4", [P, D])
        XKR = sb("XKR", [P, 2, NC, P])
        KKR = sb("KKR", [P, NC, P])
        KK = sb("KK", [P, NC, P])
        TR = sb("TR", [P, D])
        OUT = sb("OUT", [P, D])

        PB = ctx.enter_context(nc.psum_tensor("PB", [P, 8, 512], F32))
        WA, WB, OA, OB = 0, 1, 6, 7

        sem = {n: ctx.enter_context(nc.semaphore(n)) for n in PER}
        w_in = ctx.enter_context(nc.semaphore("w_in"))
        masks_in = ctx.enter_context(nc.semaphore("masks_in"))
        set_dve = ctx.enter_context(nc.semaphore("set_dve"))
        set_act = ctx.enter_context(nc.semaphore("set_act"))
        set_pe = ctx.enter_context(nc.semaphore("set_pe"))
        block = ctx.enter_context(nc.Block())
        N_WEIGHTS = 17

        def at(i, name, k=None):
            return i * PER[name] + (PER[name] if k is None else k)

        class Count:

            def __init__(self):
                self.given = {}

            def __call__(self, i, name):
                self.given[name] = self.given.get(name, 0) + 1
                return at(i, name, self.given[name])

            def end(self):
                wrong = {n: (k, PER[n]) for n, k in self.given.items() if k != PER[n]}
                assert not wrong, wrong

        def wcol(name, c, a=0, b=None):
            lo, hi = W_COLS[name]
            return W[:, c, lo + a:(hi if b is None else lo + b)]

        def row(name):
            return ROWS[0:1, R_COLS[name][0]:R_COLS[name][1]]

        def vec(name, c):
            return CV[:, c, COL[name]:COL[name] + 1]

        def h16(bank):
            return PB[:, bank, :].bitcast(F16)

        @block.sync
        def _(sp):
            def load_x(b):
                sp.dma_start(X[:, :], x[b]).then_inc(sem["x_in"], 16)

            def load_rest(b):
                sp.dma_start(M0[:, :], mask0[b]).then_inc(sem["m0_in"], 16)
                sp.dma_start(MXR[:, :], mask1[b].broadcast_to([P, D])).then_inc(sem["mx_in"], 16)
                sp.dma_start(C[:, :], ctx_in[b]).then_inc(sem["c_in"], 16)
                sp.dma_start(S0[:, :, :], ctx_in[b, 2:2 + S3, :].rearrange("r (p d) -> (r p) d", d=S3)
                             .rearrange("(c p) d -> p c d", p=P)).then_inc(sem["s0_in"], 16)

            sp.sem_inc(sem["out_stored"], 16)
            load_x(0)
            sp.dma_start(ID[:, :], ident).then_inc(w_in, 16)
            load_rest(0)
            wv = wall.rearrange("(c p) n -> p c n", p=P)
            for a, b in ((0, 640), (640, 1664), (1664, W_TOTAL)):
                sp.dma_start(W[:, :, a:b], wv[:, :, a:b]).then_inc(w_in, 16)
            for dst, src in ((W1[:, :], w1), (MAA2[:, :], maaw2[0:P, :]), (MAA2b[:, :], maaw2[P:P + 32, :]),
                             (DEC2[:, :], decw2), (ROWS[:, :], rows),
                             (CV[:, :, :], cols.rearrange("(c p) n -> p c n", p=P)),
                             (IDH[:, :], ident_h), (IDB[:, :], ident_b), (PICK0[:, :], pick0),
                             (PICK1[:, :], pick1), (GSEL[:, :], gsel), (SREP[:, :, :], srep)):
                sp.dma_start(dst, src).then_inc(w_in, 16)
            sp.dma_start(BCR[:, :, :].rearrange("p a b -> p (a b)"), bcast.broadcast_to([P, 4 * D])).then_inc(w_in, 16)
            sp.dma_start(GATE[:, :], gate.broadcast_to([P, 1])).then_inc(masks_in, 16)
            sp.dma_start(MRAW1[:, :], mask1.rearrange("b o d -> (b o) d")).then_inc(masks_in, 16)
            sp.dma_start(MRAW2[:, :], mask2).then_inc(masks_in, 16)

            with sp.Fori(0, B - 1) as i:
                own = Count()
                sp.wait_ge(sem["batch_done"], at(i, "batch_done"))
                sp.dma_start(out[i], OUT[:, :]).then_inc(sem["out_stored"], 16)
                load_x(i + 1)
                load_rest(i + 1)
            sp.wait_ge(sem["batch_done"], B)
            sp.dma_start(out[B - 1], OUT[:, :]).then_inc(sem["out_stored"], 16)
            sp.wait_ge(sem["out_stored"], 16 * (B + 1))

        @block.tensor
        def _(pe):
            mm = pe.matmul
            pe.wait_ge(w_in, 16 * N_WEIGHTS)
            pe.wait_ge(set_dve, 1)
            for k in range(3):
                last = pe.transpose(h16(WA)[:, 16 * k:16 * k + 16], MF[:, P * k:P * k + P], IDH[0:16, 0:16])
            last.then_inc(set_pe, 1)
            pe.wait_ge(set_dve, 2)

            with pe.Fori(0, B) as i:
                own = Count()

                def pair_banks(n):
                    return 2 + 2 * (n % 2), 3 + 2 * (n % 2)

                def project(dst, lhs, weights, bias=None):
                    n = len(lhs)
                    for c in range(n):
                        last = mm(dst, lhs[c], weights[c], start=(c == 0), stop=(c == n - 1 and bias is None))
                    if bias is not None:
                        last = mm(dst, ONES[0:1, :], bias, start=False, stop=True)
                    return last

                def turn_two(bank, src, at=0):
                    for c in range(NC):
                        last = pe.transpose(PB[:, bank, at + P * c:at + P * c + P], src[:, P * c:P * c + P], ID[:, :])
                    return last

                def turn_packed(bank, src):
                    for k in range(8):
                        last = pe.transpose(h16(bank)[:, P * k:P * k + P], src[:, P * k:P * k + P], IDH[:, :])
                    return last

                pe.wait_ge(sem["c_in"], at(i, "c_in"))
                turn_two(WA, C)
                pe.wait_ge(sem["x_in"], at(i, "x_in"))
                turn_two(WA, X, 2 * P).then_inc(sem["xc_t"], 1)
                pe.wait_ge(sem["xc_sb"], at(i, "xc_sb"))
                project(PB[:, WB, 0:D], [CXT[:, 2 + c, :] for c in range(NC)], [wcol("q0", c) for c in range(NC)], row("bq0"))
                project(PB[:, WB, D:D + P], [CXT[:, c, :] for c in range(NC)],
                              [wcol("kv0", c) for c in range(NC)], row("bkv0")).then_inc(sem["proj0"], 1)
                pe.wait_ge(sem["lo0"], at(i, "lo0"))
                turn_packed(WA, QN0[:, :, :].rearrange("p a b -> p (a b)")).then_inc(sem["packed0_t"], 1)
                turn_packed(WB, KN0[:, :, :, :].rearrange("p a g b -> p (a g b)")).then_inc(sem["packed0_t"], 1)
                pe.wait_ge(sem["qt_sb"], at(i, "qt_sb", 1))
                pe.wait_ge(sem["kt_sb"], at(i, "kt_sb", 1))
                pe.wait_ge(sem["mask_parts"], at(i, "mask_parts"))
                K = 3 * HD0

                def l0_unit(bank, half, g, keys_out):
                    for n in range(3):
                        if keys_out:
                            mm(PB[:, bank, :], MP[:, n, :], IDB[:, None, :].broadcast_to([P, 4, P]), start=(n == 0), stop=False)
                        else:
                            mm(PB[:, bank, :], IDB[:, :], MP[:, n:n + 1, :].broadcast_to([P, 4, P]), start=(n == 0), stop=False)
                    for k in range(4):
                        kv = 4 * half + k
                        dst = PB[:, bank, P * k:P * k + P]
                        q, key = QT[32 * g:32 * g + K, kv, :], KT[32 * g:32 * g + K, kv, :]
                        if keys_out:
                            mm(dst, key, q, start=False, stop=False)
                            col = (4 * half + g) * 4 + k
                            last = mm(dst, PICK0[:, col:col + 1].broadcast_to([P, P]), MT[:, 0:P], start=False, stop=(k == 3))
                        else:
                            last = mm(dst, q, key, start=False, stop=(k == 3))
                    last.then_inc(sem["scores"], 1)

                units0 = [(half, g) for half in range(2) for g in range(4)]
                for n in range(4):
                    if n >= 2:
                        pe.wait_ge(sem["max_read"], at(i, "max_read", n - 1))
                    banks = pair_banks(n)
                    for k in range(2):
                        l0_unit(banks[k], *units0[2 * n + k], False)
                pe.wait_ge(sem["nm"], at(i, "nm", 1))
                pe.transpose(PB[:, WA, :].bitcast(BF16)[:, 0:P], MN[:, 0, :], IDB[:, :]).then_inc(sem["m_t"], 1)
                pe.wait_ge(sem["m_sb"], at(i, "m_sb", 1))

                def attend(n_pairs, score_unit, units, pv_unit, first_exp):
                    for n in range(n_pairs + 1):
                        if n < n_pairs:
                            banks = pair_banks(n)
                            for k in range(2):
                                score_unit(banks[k], *units[2 * n + k])
                        if n >= 1:
                            pe.wait_ge(sem["exp_done"], at(i, "exp_done", first_exp + n))
                            for k in range(2):
                                u = 2 * (n - 1) + k
                                last = pv_unit(PR_[:, (2 * first_exp + u) % 8, :], *units[u])
                                last.then_inc(sem["pv_done"], 1)

                def l0_pv(p, half, g):
                    for k in range(4):
                        kv = 4 * half + k
                        h = 4 * kv + g
                        last = mm(PB[:, OA, 9 * h:9 * h + 9], p[:, P * k:P * k + P], V0[:, kv, :], start=True, stop=True)
                    return last

                attend(4, lambda bank, half, g: l0_unit(bank, half, g, True), units0, l0_pv, 0)

                pe.wait_ge(sem["o_norm"], at(i, "o_norm", 1))
                turn_two(WA, ON).then_inc(sem["o_t"], 1)
                pe.wait_ge(sem["ot_sb"], at(i, "ot_sb", 1))
                project(PB[:, WB, 0:D], [OT[:, c, :] for c in range(NC)], [wcol("o0", c) for c in range(NC)], row("bo0")).then_inc(sem["res"], 1)

                pe.wait_ge(sem["x1"], at(i, "x1"))
                pe.wait_ge(sem["ot_sb"], at(i, "ot_sb", 1))
                for a in range(2):
                    mm(PB[:, WA, P * a:P * a + P], C[:, P * a:P * a + P], W1[:, P:2 * P], start=True, stop=False)
                    mm(PB[:, WA, P * a:P * a + P], ONES[0:1, :], row("bkv1")[:, 0:P], start=False, stop=True)
                    mm(PB[:, WA, D + P * a:D + P * a + P], C[:, P * a:P * a + P], W1[:, 2 * P:3 * P], start=True, stop=False)
                    mm(PB[:, WA, D + P * a:D + P * a + P], ONES[0:1, :], row("bkv1")[:, P:2 * P], start=False, stop=True)
                for a in range(2):
                    mm(PB[:, WB, P * a:P * a + P], X1[:, P * a:P * a + P], W1[:, 0:P], start=True, stop=False)
                    last = mm(PB[:, WB, P * a:P * a + P], ONES[0:1, :], row("bq1"), start=False, stop=True)
                last.then_inc(sem["proj1"], 1)
                pe.wait_ge(sem["lo1"], at(i, "lo1"))
                turn_packed(WA, QN1[:, :, :].rearrange("p a b -> p (a b)")).then_inc(sem["packed1_t"], 1)
                turn_packed(WB, KN1[:, :, :].rearrange("p a b -> p (a b)")).then_inc(sem["packed1_t"], 1)
                pe.wait_ge(sem["qt_sb"], at(i, "qt_sb", 2))
                pe.wait_ge(sem["kt_sb"], at(i, "kt_sb", 2))
                K1 = 3 * HD1 + 1

                def l1_max_unit(bank, a, j, p):
                    for k in range(2):
                        tt = 2 * p + k
                        rows_ = slice(32 * j, 32 * j + K1)
                        last = mm(PB[:, bank, D * k:D * k + D], QT[rows_, 4 * a + tt, :], KT[rows_, tt:8:4, :], start=True, stop=True)
                    last.then_inc(sem["scores"], 1)

                for a in range(2):
                    for j in range(4):
                        n = 4 * a + j
                        if n >= 2:
                            pe.wait_ge(sem["max_read"], at(i, "max_read", 4 + n - 1))
                        banks = pair_banks(n)
                        for p in range(2):
                            l1_max_unit(banks[p], a, j, p)
                pe.wait_ge(sem["nm"], at(i, "nm", 2))
                for a in range(2):
                    last = pe.transpose(PB[:, WA, :].bitcast(BF16)[:, P * a:P * a + P], MN[:, a, :], IDB[:, :])
                last.then_inc(sem["m_t"], 1)
                pe.wait_ge(sem["m_sb"], at(i, "m_sb", 2))

                def l1_unit(bank, j, tt):
                    rows_ = slice(32 * j, 32 * j + K1)
                    for c in range(2):
                        dst = PB[:, bank, D * c:D * c + D]
                        mm(dst, KT[rows_, 4 * c + tt, :], QT[rows_, tt:8:4, :], start=True, stop=False)
                        col = 4 * j + tt
                        last = mm(dst, PICK1[:, col:col + 1].broadcast_to([P, P]), MT[:, :], start=False, stop=True)
                    last.then_inc(sem["scores"], 1)

                def l1_pv(p, j, tt):
                    h = 4 * tt + j
                    for a in range(2):
                        for c in range(2):
                            last = mm(PB[:, OA + a, 17 * h:17 * h + 17], p[:, D * c + P * a:D * c + P * a + P],
                                      V1[:, H1 * c + h, :], start=(c == 0), stop=(c == 1))
                    return last

                units1 = [(j, tt) for j in range(4) for tt in range(4)]
                attend(8, l1_unit, units1, l1_pv, 4)
                pe.wait_ge(sem["std1"], at(i, "std1"))
                for a in range(2):
                    pe.transpose(PB[:, WA, P * a:P * a + P], MEAN[:, a, :], ID[:, :])
                    last = pe.transpose(PB[:, WA, D + P * a:D + P * a + P], STD[:, a, :], ID[:, :])
                last.then_inc(sem["ms_t"], 1)

                pe.wait_ge(sem["c_hat"], at(i, "c_hat"))
                turn_two(WB, CH).then_inc(sem["c_t"], 1)
                pe.wait_ge(sem["x2"], at(i, "x2"))
                turn_two(WA, X2).then_inc(sem["x2_t"], 1)
                pe.wait_ge(sem["x2_sb"], at(i, "x2_sb"))
                pe.wait_ge(sem["ct2_sb"], at(i, "ct2_sb"))
                project(PB[:, WA, 0:D], [X2T[:, c, :] for c in range(NC)], [wcol("q2", c) for c in range(NC)])
                project(PB[:, WB, :], [CT2[:, c, :] for c in range(NC)], [wcol("kv2", c) for c in range(NC)]).then_inc(sem["proj2"], 1)
                pe.wait_ge(sem["lo2"], at(i, "lo2"))
                turn_packed(WA, QN2[:, :, :].rearrange("p a b -> p (a b)")).then_inc(sem["packed2_t"], 1)
                turn_packed(WB, KN2[:, :, :].rearrange("p a b -> p (a b)")).then_inc(sem["packed2_t"], 1)
                pe.wait_ge(sem["qt_sb"], at(i, "qt_sb", 3))
                pe.wait_ge(sem["kt_sb"], at(i, "kt_sb", 3))
                K2 = 3 * HD2 + 1

                def l2_unit(bank, r, tg, keys_out):
                    rows_ = slice(64 * r, 64 * r + K2)
                    for k in range(4):
                        tt = 4 * tg + k
                        dst = PB[:, bank, P * k:P * k + P]
                        if keys_out:
                            mm(dst, KT[rows_, tt, :], QT[rows_, tt, :], start=True, stop=False)
                            col = 8 * r + tt
                            last = mm(dst, PICK1[:, col:col + 1].broadcast_to([P, P]), MT[:, 0:P], start=False, stop=True)
                        else:
                            last = mm(dst, QT[rows_, tt, :], KT[rows_, tt, :], start=True, stop=True)
                    last.then_inc(sem["scores"], 1)

                units2 = [(r, tg) for r in range(2) for tg in range(2)]
                for r in range(2):
                    banks = pair_banks(r)
                    for tg in range(2):
                        l2_unit(banks[tg], r, tg, False)
                pe.wait_ge(sem["nm"], at(i, "nm", 3))
                pe.transpose(PB[:, WA, :].bitcast(BF16)[:, 0:P], MN[:, 0, :], IDB[:, :]).then_inc(sem["m_t"], 1)
                pe.wait_ge(sem["m_sb"], at(i, "m_sb", 3))

                def l2_pv(p, r, tg):
                    for k in range(4):
                        h = 2 * (4 * tg + k) + r
                        last = mm(PB[:, OA, 17 * h:17 * h + 17], p[:, P * k:P * k + P], V2[:, h, :], start=True, stop=True)
                    return last

                attend(2, lambda bank, r, tg: l2_unit(bank, r, tg, True), units2, l2_pv, 12)
                pe.wait_ge(sem["o_norm"], at(i, "o_norm", 3))
                turn_two(WA, ON).then_inc(sem["o_t"], 1)
                pe.wait_ge(sem["ot_sb"], at(i, "ot_sb", 2))
                project(PB[:, WB, 0:D], [OT[:, c, :] for c in range(NC)], [wcol("o2", c) for c in range(NC)]).then_inc(sem["res"], 1)

                pe.wait_ge(sem["xh"], at(i, "xh", 1))
                turn_two(WA, XH).then_inc(sem["xh_t"], 1)
                pe.wait_ge(sem["xm"], at(i, "xm"))
                project(PB[:, WB, 0:P], [wcol("maa1", c, 0, P) for c in range(NC)], [XM[:, c, :] for c in range(NC)])
                project(PB[0:32, WB, P:2 * P], [wcol("maa1", c, P, P + 32) for c in range(NC)],
                              [XM[:, c, :] for c in range(NC)]).then_inc(sem["xxx"], 1)
                pe.wait_ge(sem["xxt"], at(i, "xxt"))
                for n in range(5):
                    for c in range(NC):
                        lhs = MAA2[32 * n:32 * n + 32, P * c:P * c + P] if n < 4 else MAA2b[:, P * c:P * c + P]
                        rhs = XXT[32 * n:32 * n + 32, :] if n < 4 else XXT4[:, :]
                        last = mm(PB[:, 2 + n, P * c:P * c + P], lhs, rhs, start=True, stop=True)
                    last.then_inc(sem["mix"], 1)

                def to_channels(bank, at, weights, src):
                    for co in range(NC):
                        last = project(PB[:, bank, at + P * co:at + P * co + P],
                                       [wcol(weights, c, P * co, P * co + P) for c in range(NC)],
                                       [src[:, c, :] for c in range(NC)])
                    return last

                def to_tokens(bank, at, weights, src):
                    return project(PB[:, bank, at:at + D], [src[:, c, :] for c in range(NC)],
                                   [wcol(weights, c) for c in range(NC)])

                pe.wait_ge(sem["x5"], at(i, "x5", 1))
                project(PB[0:64, WA, 0:P], [wcol("dec1", c) for c in range(NC)], [X5[:, 1, c, :] for c in range(NC)]).then_inc(sem["wd_ps"], 1)
                pe.wait_ge(sem["x5"], at(i, "x5", 2))
                to_channels(OB, 0, "k3", X5[:, 0])
                pe.wait_ge(sem["wd"], at(i, "wd"))
                for c in range(NC):
                    last = mm(PB[:, WA, P + P * c:2 * P + P * c], DEC2[:, P * c:P * c + P], WD[:, :], start=True, stop=True)
                last.then_inc(sem["w_ps"], 1)
                pe.wait_ge(sem["x5"], at(i, "x5", 3))
                to_channels(WB, D, "v3", X5[:, 2])
                to_tokens(WB, 0, "v3", X5[:, 2]).then_inc(sem["v_ps"], 1)
                pe.wait_ge(sem["x5"], at(i, "x5", 4))
                to_channels(OB, D, "r3", X5[:, 3]).then_inc(sem["kr_ps"], 1)
                pe.wait_ge(sem["x5"], at(i, "x5", 5))
                to_tokens(OA, 0, "g3", X5[:, 4]).then_inc(sem["g_ps"], 1)
                pe.wait_ge(sem["krv_sb"], at(i, "krv_sb", 3))
                for d in range(S3):
                    last = mm(PB[:, 2 + d // 2, D * (d % 2):D * (d % 2) + D], SREP[:, d, :],
                              VT3[:, :, :].rearrange("p c t -> p (c t)"), start=True, stop=True)
                    if d % 2:
                        last.then_inc(sem["vd"], 1)
                pe.wait_ge(sem["ruk"], at(i, "ruk"))
                pe.wait_ge(sem["krv_sb"], at(i, "krv_sb"))
                for c in range(NC):
                    mm(PB[:, OB, D + 16 * c:D + 16 * c + 16], RUK[:, c, :], GSEL[:, :], start=True, stop=True)
                for n in range(4):
                    pe.wait_ge(sem["pr"], at(i, "pr", n + 1))
                    for d in (2 * n, 2 * n + 1):
                        for c in range(NC):
                            last = mm(PB[:, OB, P * c + d:P * c + P:S3], PR3[:, d, c, :], GSEL[:, :], start=True, stop=True)
                last.then_inc(sem["att_ps"], 1)
                pe.wait_ge(sem["y"], at(i, "y"))
                turn_two(WA, Y).then_inc(sem["y_t"], 1)
                pe.wait_ge(sem["yt_sb"], at(i, "yt_sb"))
                to_tokens(WB, 0, "o3", YT).then_inc(sem["y_o"], 1)
                pe.wait_ge(sem["xh"], at(i, "xh", 2))
                turn_two(WA, XH).then_inc(sem["xh_t"], 1)
                pe.wait_ge(sem["xkr"], at(i, "xkr", 4))
                to_channels(2, 0, "fk3", XKR[:, 0])
                to_tokens(3, 0, "fr3", XKR[:, 1]).then_inc(sem["ff1"], 1)
                pe.wait_ge(sem["kk"], at(i, "kk"))
                to_tokens(4, 0, "fv3", KK).then_inc(sem["ff2"], 1)
                pe.wait_ge(sem["batch_done"], at(i, "batch_done"))
                own.end()

        @block.scalar
        def _(act):
            def copy(o, a, scale=1.0):
                return act.activation(o, a, ACT.Copy, scale=scale)

            act.wait_ge(masks_in, 48)
            act.activation(TG[:, :], GATE[:, :], ACT.Tanh).then_inc(set_act, 1)
            act.wait_ge(w_in, 16 * N_WEIGHTS)
            act.wait_ge(set_act, 1)
            act.wait_ge(set_dve, 2)

            with act.Fori(0, B) as i:
                own = Count()
                exps = [0]

                def exp_pair():
                    n = exps[0]
                    first = 8 + 2 * n if n < 4 else 24 + 2 * n if n < 12 else 28 + 2 * n
                    act.wait_ge(sem["scores"], at(i, "scores", first + 2))
                    if n >= 4:
                        act.wait_ge(sem["pv_done"], at(i, "pv_done", 2 * (n - 4) + 2))
                    bank = 2 + 2 * ((first // 2) % 2)
                    act.activation(PR_[:, (2 * n) % 8:(2 * n) % 8 + 2, :], PB[:, bank:bank + 2, :], ACT.Exp).then_inc(sem["exp_done"], 1)
                    act.wait_ge(sem["exp_done"], own(i, "exp_done"))
                    exps[0] += 1

                act.wait_ge(sem["xc_t"], at(i, "xc_t"))
                copy(CXT[:, :, :].rearrange("p a b -> p (a b)"), PB[:, WA, :]).then_inc(sem["xc_sb"], 1)
                act.wait_ge(sem["xc_sb"], own(i, "xc_sb"))
                act.wait_ge(sem["proj0"], at(i, "proj0"))
                scale0 = float(HD0) ** -0.5
                q = PB[:, WB, 0:D].rearrange("p (h d) -> p h d", d=HD0)
                k = PB[:, WB, D:D + 64].rearrange("p (h d) -> p h d", d=HD0)
                v = PB[:, WB, D + 64:D + P].rearrange("p (h d) -> p h d", d=HD0)
                copy(QN0[:, :, 0:16].rearrange("p h (a d) -> p h a d", a=2),
                            q[:, :, None, :].broadcast_to([P, H0, 2, HD0]), scale0).then_inc(sem["hi0"], 1)
                act.wait_ge(sem["hi0"], own(i, "hi0"))
                copy(KN0[:, :, :, 0:8], k[:, :, None, :].broadcast_to([P, KV0, 4, HD0])).then_inc(sem["hi0"], 1)
                act.wait_ge(sem["hi0"], own(i, "hi0"))
                copy(KN0[:, :, :, 16:24], k[:, :, None, :].broadcast_to([P, KV0, 4, HD0])).then_inc(sem["hi0"], 1)
                act.wait_ge(sem["hi0"], own(i, "hi0"))
                copy(V0[:, :, 0:HD0], v).then_inc(sem["hi0"], 1)
                act.wait_ge(sem["hi0"], own(i, "hi0"))
                act.wait_ge(sem["packed0_t"], at(i, "packed0_t", 2))
                copy(KT[:, :, :].rearrange("p a b -> p (a b)"), h16(WB)).then_inc(sem["kt_sb"], 1)
                act.wait_ge(sem["kt_sb"], own(i, "kt_sb"))
                act.wait_ge(sem["m_t"], at(i, "m_t", 1))
                copy(MT[:, 0:P], PB[:, WA, :].bitcast(BF16)[:, 0:P]).then_inc(sem["m_sb"], 1)
                act.wait_ge(sem["m_sb"], own(i, "m_sb"))
                for _n in range(4):
                    exp_pair()
                act.wait_ge(sem["o_t"], at(i, "o_t", 1))
                copy(OT[:, :, :].rearrange("p a b -> p (a b)"), PB[:, WA, 0:D]).then_inc(sem["ot_sb"], 1)
                act.wait_ge(sem["ot_sb"], own(i, "ot_sb"))

                act.wait_ge(sem["proj1"], at(i, "proj1"))
                q = PB[:, WB, 0:D].rearrange("p (h d) -> p h d", d=HD1)
                k = PB[:, WA, 0:D].rearrange("p (h d) -> p h d", d=HD1)
                v = PB[:, WA, D:2 * D].rearrange("p (h d) -> p h d", d=HD1)
                copy(QN1[:, :, 0:16].rearrange("p h (a d) -> p h a d", a=2),
                            q[:, :, None, :].broadcast_to([P, 2 * H1, 2, HD1]), float(HD1) ** -0.5).then_inc(sem["hi1"], 1)
                act.wait_ge(sem["hi1"], own(i, "hi1"))
                copy(KN1[:, :, 0:8], k).then_inc(sem["hi1"], 1)
                act.wait_ge(sem["hi1"], own(i, "hi1"))
                copy(KN1[:, :, 16:24], k).then_inc(sem["hi1"], 1)
                act.wait_ge(sem["hi1"], own(i, "hi1"))
                copy(V1[:, :, 0:HD1], v).then_inc(sem["hi1"], 1)
                act.wait_ge(sem["hi1"], own(i, "hi1"))
                act.activation(V1[:, :, HD1:2 * HD1], v, ACT.Square).then_inc(sem["hi1"], 1)
                act.wait_ge(sem["hi1"], own(i, "hi1"))
                act.wait_ge(sem["mxf"], at(i, "mxf", 1))
                act.activation(SQ[:, :], XM1[:, :], ACT.Square, accum_out=SM[:, 1:2]).then_inc(sem["hi1"], 1)
                act.wait_ge(sem["hi1"], own(i, "hi1"))
                act.wait_ge(sem["packed1_t"], at(i, "packed1_t", 2))
                copy(KT[:, :, :].rearrange("p a b -> p (a b)"), h16(WB)).then_inc(sem["kt_sb"], 1)
                act.wait_ge(sem["kt_sb"], own(i, "kt_sb"))
                act.wait_ge(sem["m_t"], at(i, "m_t", 2))
                copy(MT[:, :], PB[:, WA, :].bitcast(BF16)[:, 0:D]).then_inc(sem["m_sb"], 1)
                act.wait_ge(sem["m_sb"], own(i, "m_sb"))
                for _n in range(8):
                    exp_pair()
                act.wait_ge(sem["var1"], at(i, "var1"))
                act.activation(STD[:, :, :], VAR[:, :, :], ACT.Sqrt).then_inc(sem["std1"], 1)
                act.wait_ge(sem["std1"], own(i, "std1"))

                act.wait_ge(sem["c_t"], at(i, "c_t"))
                for c in range(NC):
                    act.activation(CT2[:, c, :], PB[:, WB, P * c:P * c + P], ACT.Identity,
                                          bias=vec("lnb2", c), scale=vec("lng2", c)).then_inc(sem["ct2_sb"], 1)
                    act.wait_ge(sem["ct2_sb"], own(i, "ct2_sb"))
                act.wait_ge(sem["x2_t"], at(i, "x2_t"))
                copy(X2T[:, :, :].rearrange("p a b -> p (a b)"), PB[:, WA, 0:D]).then_inc(sem["x2_sb"], 1)
                act.wait_ge(sem["x2_sb"], own(i, "x2_sb"))
                act.wait_ge(sem["proj2"], at(i, "proj2"))
                q = PB[:, WA, 0:D].rearrange("p (h d) -> p h d", d=HD2)
                k = PB[:, WB, 0:D].rearrange("p (h d) -> p h d", d=HD2)
                v = PB[:, WB, D:2 * D].rearrange("p (h d) -> p h d", d=HD2)
                copy(QN2[:, :, 0:32].rearrange("p h (a d) -> p h a d", a=2),
                            q[:, :, None, :].broadcast_to([P, H2, 2, HD2]), float(HD2) ** -0.5).then_inc(sem["hi2"], 1)
                act.wait_ge(sem["hi2"], own(i, "hi2"))
                copy(KN2[:, :, 0:16], k).then_inc(sem["hi2"], 1)
                act.wait_ge(sem["hi2"], own(i, "hi2"))
                copy(KN2[:, :, 32:48], k).then_inc(sem["hi2"], 1)
                act.wait_ge(sem["hi2"], own(i, "hi2"))
                copy(V2[:, :, 0:HD2], v).then_inc(sem["hi2"], 1)
                act.wait_ge(sem["hi2"], own(i, "hi2"))
                act.wait_ge(sem["packed2_t"], at(i, "packed2_t", 2))
                copy(KT[:, :, :].rearrange("p a b -> p (a b)"), h16(WB)).then_inc(sem["kt_sb"], 1)
                act.wait_ge(sem["kt_sb"], own(i, "kt_sb"))
                act.wait_ge(sem["m_t"], at(i, "m_t", 3))
                copy(MT[:, 0:P], PB[:, WA, :].bitcast(BF16)[:, 0:P]).then_inc(sem["m_sb"], 1)
                act.wait_ge(sem["m_sb"], own(i, "m_sb"))
                for _n in range(2):
                    exp_pair()
                act.wait_ge(sem["o_t"], at(i, "o_t", 2))
                copy(OT[:, :, :].rearrange("p a b -> p (a b)"), PB[:, WA, 0:D]).then_inc(sem["ot_sb"], 1)
                act.wait_ge(sem["ot_sb"], own(i, "ot_sb"))

                def affine(sem_k, w, b):
                    act.wait_ge(sem["xh_t"], at(i, "xh_t", sem_k))
                    for c in range(NC):
                        act.activation(XNT[:, c, 1:P + 1], PB[:, WA, P * c:P * c + P], ACT.Identity,
                                              bias=vec(b, c), scale=vec(w, c)).then_inc(sem["xnt"], 1)
                        act.wait_ge(sem["xnt"], own(i, "xnt"))

                affine(1, "ln1w", "ln1b")
                act.wait_ge(sem["xxx"], at(i, "xxx"))
                act.activation(XXT[:, :], PB[:, WB, 0:P], ACT.Tanh).then_inc(sem["xxt"], 1)
                act.wait_ge(sem["xxt"], own(i, "xxt"))
                act.activation(XXT4[:, :], PB[0:32, WB, P:2 * P], ACT.Tanh).then_inc(sem["xxt"], 1)
                act.wait_ge(sem["xxt"], own(i, "xxt"))
                act.wait_ge(sem["wd_ps"], at(i, "wd_ps"))
                act.activation(WD[:, :], PB[0:64, WA, 0:P], ACT.Tanh).then_inc(sem["wd"], 1)
                act.wait_ge(sem["wd"], own(i, "wd"))
                act.wait_ge(sem["w_ps"], at(i, "w_ps"))
                for c in range(NC):
                    act.activation(EW[:, c, :], PB[:, WA, P + P * c:2 * P + P * c], ACT.Exp, bias=vec("td", c)).then_inc(sem["act"], 1)
                    act.wait_ge(sem["act"], own(i, "act"))
                act.activation(WS[:, :, :, 1:P], EW[:, None, :, 0:P - 1].broadcast_to([P, 2, NC, P - 1]),
                                      ACT.Exp, scale=-1.0).then_inc(sem["ws"], 1)
                act.wait_ge(sem["ws"], own(i, "ws"))
                act.wait_ge(sem["v_ps"], at(i, "v_ps"))
                copy(VN3[:, :], PB[:, WB, 0:D]).then_inc(sem["krv_sb"], 1)
                act.wait_ge(sem["krv_sb"], own(i, "krv_sb"))
                copy(VT3[:, :, :].rearrange("p a b -> p (a b)"), PB[:, WB, D:2 * D]).then_inc(sem["krv_sb"], 1)
                act.wait_ge(sem["krv_sb"], own(i, "krv_sb"))
                act.wait_ge(sem["kr_ps"], at(i, "kr_ps"))
                copy(KR[:, :, :, :].rearrange("p n a b -> p (n a b)"), PB[:, OB, :]).then_inc(sem["krv_sb"], 1)
                act.wait_ge(sem["krv_sb"], own(i, "krv_sb"))
                act.wait_ge(sem["g_ps"], at(i, "g_ps"))
                act.activation(GT[:, :], PB[:, OA, 0:D], ACT.Tanh, scale=0.5).then_inc(sem["krv_sb"], 1)
                act.wait_ge(sem["krv_sb"], own(i, "krv_sb"))
                act.wait_ge(sem["d8"], at(i, "d8"))
                act.activation(SQ[:, :], DD[:, :], ACT.Square).then_inc(sem["sq"], 1)
                act.wait_ge(sem["sq"], own(i, "sq"))
                act.wait_ge(sem["y_t"], at(i, "y_t"))
                copy(YT[:, :, :].rearrange("p a b -> p (a b)"), PB[:, WA, 0:D]).then_inc(sem["yt_sb"], 1)
                act.wait_ge(sem["yt_sb"], own(i, "yt_sb"))
                affine(2, "ln2w", "ln2b")
                act.wait_ge(sem["ff1"], at(i, "ff1"))
                act.activation(KKR[:, :, :].rearrange("p a b -> p (a b)"), PB[:, 2, 0:D], ACT.Relu).then_inc(sem["act"], 1)
                act.wait_ge(sem["act"], own(i, "act"))
                act.activation(KK[:, :, :], KKR[:, :, :], ACT.Square).then_inc(sem["kk"], 1)
                act.wait_ge(sem["kk"], own(i, "kk"))
                act.activation(TR[:, :], PB[:, 3, 0:D], ACT.Tanh, scale=0.5).then_inc(sem["tr"], 1)
                act.wait_ge(sem["tr"], own(i, "tr"))
                act.wait_ge(sem["batch_done"], at(i, "batch_done"))
                own.end()

        @block.gpsimd
        def _(pool):
            tt = pool.tensor_tensor
            pool.wait_ge(set_dve, 2)

            with pool.Fori(0, B) as i:
                own = Count()

                def rsqrt(k, eps, n=1, scale=1.0, src=None, dst=None):
                    pool.wait_ge(sem["var_in"], at(i, "var_in", k))
                    src = MV[:, 1:2] if src is None else src
                    dst = RSTD[:, :] if dst is None else dst
                    tt(IDLE[:, 0:1], NHALF[:, 0:1], NHALF[:, 1:2], ALU.add)
                    pool.tensor_scalar(VE[:, 0:n], src, scale, eps, ALU.mult, ALU.add).then_inc(sem["pool"], 1)
                    pool.wait_ge(sem["pool"], own(i, "pool"))
                    tt(dst, VE[:, 0:n], NHALF[:, 0:n], ALU.pow).then_inc(sem["rstd"], 1)
                    pool.wait_ge(sem["rstd"], own(i, "rstd"))

                pool.wait_ge(sem["m0_in"], at(i, "m0_in"))
                tt(IDLE[:, 0:1], NHALF[:, 0:1], NHALF[:, 1:2], ALU.add)
                pool.tensor_copy(MP[:, 0, :], M0[:, :]).then_inc(sem["pool"], 1)
                pool.wait_ge(sem["pool"], own(i, "pool"))
                tt(MR[:, :], M0[:, :], MP[:, 0, :], ALU.subtract).then_inc(sem["pool"], 1)
                pool.wait_ge(sem["pool"], own(i, "pool"))
                tt(IDLE[:, 0:1], NHALF[:, 0:1], NHALF[:, 1:2], ALU.add)
                pool.tensor_copy(MP[:, 1, :], MR[:, :]).then_inc(sem["pool"], 1)
                pool.wait_ge(sem["pool"], own(i, "pool"))
                tt(MR[:, :], MR[:, :], MP[:, 1, :], ALU.subtract).then_inc(sem["pool"], 1)
                pool.wait_ge(sem["pool"], own(i, "pool"))
                tt(IDLE[:, 0:1], NHALF[:, 0:1], NHALF[:, 1:2], ALU.add)
                pool.tensor_copy(MP[:, 2, :], MR[:, :]).then_inc(sem["mask_parts"], 1)
                pool.wait_ge(sem["mask_parts"], own(i, "mask_parts"))
                rsqrt(1, 1e-6)
                pool.wait_ge(sem["hi1"], at(i, "hi1"))
                tt(IDLE[:, 0:1], NHALF[:, 0:1], NHALF[:, 1:2], ALU.add)
                pool.tensor_scalar(SM[:, 3:4], SM[:, 0:1], SM[:, 2:3], None, ALU.mult).then_inc(sem["pool"], 1)
                pool.wait_ge(sem["pool"], own(i, "pool"))
                tt(IDLE[:, 0:1], NHALF[:, 0:1], NHALF[:, 1:2], ALU.add)
                pool.tensor_scalar(SM[:, 4:5], SM[:, 1:2], SM[:, 2:3], None, ALU.mult).then_inc(sem["pool"], 1)
                pool.wait_ge(sem["pool"], own(i, "pool"))
                tt(SM[:, 5:6], SM[:, 3:4], SM[:, 3:4], ALU.mult).then_inc(sem["pool"], 1)
                pool.wait_ge(sem["pool"], own(i, "pool"))
                tt(SM[:, 6:7], SM[:, 4:5], SM[:, 5:6], ALU.subtract).then_inc(sem["pool"], 1)
                pool.wait_ge(sem["pool"], own(i, "pool"))
                tt(IDLE[:, 0:1], NHALF[:, 0:1], NHALF[:, 1:2], ALU.add)
                pool.tensor_scalar(SM[:, 7:8], SM[:, 6:7], 0.0, 1e-5, ALU.max, ALU.add).then_inc(sem["pool"], 1)
                pool.wait_ge(sem["pool"], own(i, "pool"))
                tt(RSTD[:, :], SM[:, 7:8], NHALF[:, 0:1], ALU.pow).then_inc(sem["pool"], 1)
                pool.wait_ge(sem["pool"], own(i, "pool"))
                tt(IDLE[:, 0:1], NHALF[:, 0:1], NHALF[:, 1:2], ALU.add)
                pool.tensor_scalar(XN1[:, :], XM1[:, :], SM[:, 3:4], RSTD[:, :], ALU.subtract, ALU.mult).then_inc(sem["pool"], 1)
                pool.wait_ge(sem["pool"], own(i, "pool"))
                tt(XN1[:, :], XN1[:, :], MXF[:, :], ALU.mult).then_inc(sem["xn1"], 1)
                pool.wait_ge(sem["xn1"], own(i, "xn1"))
                rsqrt(2, 1e-5)
                rsqrt(3, 1e-5)
                for k, n in enumerate((1, 0, 2, 3, 4)):
                    pool.wait_ge(sem["t5"], at(i, "t5", k + 1))
                    tt(X5[:, n], T5[:, n], XNT[:, :, 1:P + 1], ALU.add).then_inc(sem["x5"], 1)
                    pool.wait_ge(sem["x5"], own(i, "x5"))
                for n in range(4):
                    pool.wait_ge(sem["sc"], at(i, "sc", n + 1))
                    pool.wait_ge(sem["krv_sb"], at(i, "krv_sb", 3))
                    tt(PR3[:, 2 * n:2 * n + 2], SC3[:, 2 * n:2 * n + 2],
                              KR[:, 1:2].broadcast_to([P, 2, NC, P]), ALU.mult).then_inc(sem["pr"], 1)
                    pool.wait_ge(sem["pr"], own(i, "pr"))
                rsqrt(4, 1e-5, 32, 1.0 / S3, G8[:, 1, :], G8[:, 2, :])
                rsqrt(5, 1e-5)
                pool.wait_ge(sem["batch_done"], at(i, "batch_done"))
                own.end()

        @block.vector
        def _(dve):
            stt, tt, ts = dve.scalar_tensor_tensor, dve.tensor_tensor, dve.tensor_scalar
            for tile in (QN0, KN0, QN1, KN1, QN2, KN2, WS, MN):
                dve.memset(tile[:], 0.0)
            dve.memset(V0[:, :, HD0:HD0 + 1], 1.0)
            dve.memset(V1[:, :, 2 * HD1:2 * HD1 + 1], 1.0)
            dve.memset(V2[:, :, HD2:HD2 + 1], 1.0)
            dve.memset(ONES[:, :], 1.0)
            dve.memset(NHALF[:, :], -0.5)
            dve.wait_ge(masks_in, 48)
            ts(MF[:, 0:2 * P], MRAW1[:, :], 1.0, NEG, ALU.subtract, ALU.mult)
            ts(MF[:, 2 * P:3 * P], MRAW2[:, :], 1.0, NEG, ALU.subtract, ALU.mult).then_inc(set_dve, 1)
            dve.wait_ge(set_dve, 1)
            dve.memset(QN1[:, :, 24:25], NEG)
            dve.memset(QN2[:, :, 48:49], NEG)
            dve.wait_ge(set_pe, 1)
            dve.tensor_copy(KM1[:, :, :].rearrange("p b a -> p a b"), h16(WA)[:, 0:32].rearrange("p (a b) -> p a b", a=2)).then_inc(masks_in, 16)
            dve.tensor_copy(KM2[:, :, 0], h16(WA)[:, 32:48]).then_inc(set_dve, 1)
            dve.wait_ge(masks_in, 64)
            dve.wait_ge(set_dve, 2)
            dve.wait_ge(w_in, 16 * N_WEIGHTS)
            dve.wait_ge(set_act, 1)

            with dve.Fori(0, B) as i:
                own = Count()
                maxes = [0]

                def flat(tile):
                    return tile[:, :, :].rearrange("p a b -> p (a b)")

                def max_pair(dst, width):
                    n = maxes[0]
                    first = 2 * n if n < 4 else 8 + 2 * n if n < 12 else 24 + 2 * n
                    dve.wait_ge(sem["scores"], at(i, "scores", first + 2))
                    bank = 2 + 2 * ((first // 2) % 2)
                    dve.tensor_reduce(dst, PB[:, bank:bank + 2, :].rearrange("p b (h s) -> p (b h) s", s=width),
                                             X_AXIS, ALU.max, negate=True).then_inc(sem["max_read"], 1)
                    dve.wait_ge(sem["max_read"], own(i, "max_read"))
                    maxes[0] += 1

                def max_parts(n, parts):
                    nm = NM[:, 0:n]
                    if n == 32 and parts(0).shape[1:] != nm.shape[1:]:
                        nm = NM[:, :].rearrange("p (a h) -> p a h", a=2)
                        nr = NR[:, :].rearrange("p (a h) -> p a h", a=2)
                    else:
                        nr = NR[:, 0:n]
                    dve.tensor_copy(parts(0), nm).then_inc(sem["dve"], 1)
                    dve.wait_ge(sem["dve"], own(i, "dve"))
                    tt(nr, nm, parts(0), ALU.subtract).then_inc(sem["dve"], 1)
                    dve.wait_ge(sem["dve"], own(i, "dve"))
                    dve.tensor_copy(parts(1), nr).then_inc(sem["dve"], 1)
                    dve.wait_ge(sem["dve"], own(i, "dve"))
                    tt(parts(2), nr, parts(1), ALU.subtract).then_inc(sem["nm"], 1)
                    dve.wait_ge(sem["nm"], own(i, "nm"))

                def stats(src):
                    dve.bn_stats(ST[:, :], src).then_inc(sem["dve"], 1)
                    dve.wait_ge(sem["dve"], own(i, "dve"))
                    dve.memset(IDLE[:, 1:2], 0.0)
                    dve.bn_aggr(MV[:, :], ST[:, :]).then_inc(sem["var_in"], 1)
                    dve.wait_ge(sem["var_in"], own(i, "var_in"))

                dve.wait_ge(sem["hi0"], at(i, "hi0"))
                q = PB[:, WB, 0:D].rearrange("p (h d) -> p h d", d=HD0)
                k = PB[:, WB, D:D + 64].rearrange("p (h d) -> p h d", d=HD0)
                stt(QN0[:, :, 16:24], q, float(HD0) ** -0.5, QN0[:, :, 0:8], ALU.mult, ALU.subtract).then_inc(sem["lo0"], 1)
                dve.wait_ge(sem["lo0"], own(i, "lo0"))
                tt(KN0[:, :, :, 8:16], k[:, :, None, :].broadcast_to([P, KV0, 4, HD0]), KN0[:, :, :, 0:8], ALU.subtract).then_inc(sem["lo0"], 1)
                dve.wait_ge(sem["lo0"], own(i, "lo0"))
                dve.wait_ge(sem["packed0_t"], at(i, "packed0_t", 1))
                dve.tensor_copy(flat(QT), h16(WA)).then_inc(sem["qt_sb"], 1)
                dve.wait_ge(sem["qt_sb"], own(i, "qt_sb"))
                for n in range(4):
                    max_pair(NM[:, 8 * n:8 * n + 8], P)
                max_parts(32, lambda k: MN[:, 0, 32 * k:32 * k + 32])
                dve.wait_ge(sem["pv_done"], at(i, "pv_done", 8))
                o = PB[:, OA, 0:9 * H0].rearrange("p (h d) -> p h d", d=9)
                dve.reciprocal(RS[:, 0:H0], o[:, :, 8]).then_inc(sem["dve"], 1)
                dve.wait_ge(sem["dve"], own(i, "dve"))
                tt(ON[:, :].rearrange("p (h d) -> p h d", d=HD0), o[:, :, 0:8],
                          RS[:, 0:H0, None].broadcast_to([P, H0, HD0]), ALU.mult).then_inc(sem["o_norm"], 1)
                dve.wait_ge(sem["o_norm"], own(i, "o_norm"))
                dve.wait_ge(sem["res"], at(i, "res", 1))
                tt(XH[:, :], PB[:, WB, 0:D], X[:, :], ALU.add).then_inc(sem["dve"], 1)
                dve.wait_ge(sem["dve"], own(i, "dve"))
                stats(XH[:, :])
                dve.wait_ge(sem["rstd"], at(i, "rstd", 1))
                ts(XH[:, :], XH[:, :], MV[:, 0:1], RSTD[:, :], ALU.subtract, ALU.mult).then_inc(sem["dve"], 1)
                dve.wait_ge(sem["dve"], own(i, "dve"))
                tt(XH[:, :], XH[:, :], BCR[:, BC["gamma0"], :], ALU.mult).then_inc(sem["dve"], 1)
                dve.wait_ge(sem["dve"], own(i, "dve"))
                tt(X1[:, :], XH[:, :], BCR[:, BC["beta0"], :], ALU.add).then_inc(sem["x1"], 1)
                dve.wait_ge(sem["x1"], own(i, "x1"))

                dve.wait_ge(sem["mx_in"], at(i, "mx_in"))
                dve.tensor_copy(MXF[:, :], MXR[:, :]).then_inc(sem["dve"], 1)
                dve.wait_ge(sem["dve"], own(i, "dve"))
                dve.tensor_reduce(SM[:, 2:3], MXF[:, :], X_AXIS, ALU.add).then_inc(sem["dve"], 1)
                dve.wait_ge(sem["dve"], own(i, "dve"))
                dve.reciprocal(SM[:, 2:3], SM[:, 2:3]).then_inc(sem["dve"], 1)
                dve.wait_ge(sem["dve"], own(i, "dve"))
                tt(XM1[:, :], X1[:, :], MXF[:, :], ALU.mult).then_inc(sem["dve"], 1)
                dve.wait_ge(sem["dve"], own(i, "dve"))
                dve.tensor_reduce(SM[:, 0:1], XM1[:, :], X_AXIS, ALU.add).then_inc(sem["mxf"], 1)
                dve.wait_ge(sem["mxf"], own(i, "mxf"))
                km = KM1[:, i, :][:, :, None].broadcast_to([P, 2, H1])
                dve.tensor_copy(KN1[:, :, 24].rearrange("p (a h) -> p a h", a=2), km).then_inc(sem["dve"], 1)
                dve.wait_ge(sem["dve"], own(i, "dve"))
                dve.wait_ge(sem["hi1"], at(i, "hi1"))
                q = PB[:, WB, 0:D].rearrange("p (h d) -> p h d", d=HD1)
                k = PB[:, WA, 0:D].rearrange("p (h d) -> p h d", d=HD1)
                stt(QN1[:, :, 16:24], q, float(HD1) ** -0.5, QN1[:, :, 0:8], ALU.mult, ALU.subtract).then_inc(sem["lo1"], 1)
                dve.wait_ge(sem["lo1"], own(i, "lo1"))
                tt(KN1[:, :, 8:16], k, KN1[:, :, 0:8], ALU.subtract).then_inc(sem["lo1"], 1)
                dve.wait_ge(sem["lo1"], own(i, "lo1"))
                dve.wait_ge(sem["packed1_t"], at(i, "packed1_t", 1))
                dve.tensor_copy(flat(QT), h16(WA)).then_inc(sem["qt_sb"], 1)
                dve.wait_ge(sem["qt_sb"], own(i, "qt_sb"))
                for a in range(2):
                    for j in range(4):
                        max_pair(NM[:, 16 * a + 4 * j:16 * a + 4 * j + 4], D)
                max_parts(32, lambda k: MN[:, :, 16 * k:16 * k + 16])
                dve.wait_ge(sem["pv_done"], at(i, "pv_done", 24))
                dve.wait_ge(sem["xn1"], at(i, "xn1"))
                o = PB[:, OA:OB + 1, 0:17 * H1].rearrange("p a (h d) -> p a h d", d=17)
                rs = RS[:, :].rearrange("p (a h) -> p a h", a=2)
                rsb = rs[:, :, :, None].broadcast_to([P, 2, H1, HD1])
                v4 = lambda tile: tile[:, :, :].rearrange("p a (h d) -> p a h d", d=HD1)
                dve.reciprocal(rs, o[:, :, :, 16]).then_inc(sem["dve"], 1)
                dve.wait_ge(sem["dve"], own(i, "dve"))
                tt(v4(MEAN), o[:, :, :, 0:8], rsb, ALU.mult).then_inc(sem["dve"], 1)
                dve.wait_ge(sem["dve"], own(i, "dve"))
                tt(v4(EX2), o[:, :, :, 8:16], rsb, ALU.mult).then_inc(sem["o_norm"], 1)
                dve.wait_ge(sem["o_norm"], own(i, "o_norm"))
                tt(flat(VAR), flat(MEAN), flat(MEAN), ALU.mult).then_inc(sem["dve"], 1)
                dve.wait_ge(sem["dve"], own(i, "dve"))
                tt(flat(VAR), flat(EX2), flat(VAR), ALU.subtract).then_inc(sem["dve"], 1)
                dve.wait_ge(sem["dve"], own(i, "dve"))
                ts(flat(VAR), flat(VAR), 0.0, None, ALU.max).then_inc(sem["var1"], 1)
                dve.wait_ge(sem["var1"], own(i, "var1"))
                dve.bn_stats(ST[:, :], C[:, :]).then_inc(sem["dve"], 1)
                dve.wait_ge(sem["dve"], own(i, "dve"))
                dve.memset(IDLE[:, 1:2], 0.0)
                dve.bn_aggr(MV[:, :], ST[:, :]).then_inc(sem["var_in"], 1)
                dve.wait_ge(sem["var_in"], own(i, "var_in"))
                dve.wait_ge(sem["rstd"], at(i, "rstd", 2))
                ts(CH[:, :], C[:, :], MV[:, 0:1], RSTD[:, :], ALU.subtract, ALU.mult).then_inc(sem["c_hat"], 1)
                dve.wait_ge(sem["c_hat"], own(i, "c_hat"))
                dve.wait_ge(sem["ms_t"], at(i, "ms_t"))
                tt(X2[:, :], XN1[:, :], PB[:, WA, D:2 * D], ALU.mult).then_inc(sem["dve"], 1)
                dve.wait_ge(sem["dve"], own(i, "dve"))
                tt(X2[:, :], X2[:, :], PB[:, WA, 0:D], ALU.add).then_inc(sem["dve"], 1)
                dve.wait_ge(sem["dve"], own(i, "dve"))
                tt(X2[:, :], X2[:, :], MXF[:, :], ALU.mult).then_inc(sem["x2"], 1)
                dve.wait_ge(sem["x2"], own(i, "x2"))

                dve.tensor_copy(KN2[:, :, 48], KM2[:, i, :].broadcast_to([P, H2])).then_inc(sem["dve"], 1)
                dve.wait_ge(sem["dve"], own(i, "dve"))
                dve.wait_ge(sem["hi2"], at(i, "hi2"))
                q = PB[:, WA, 0:D].rearrange("p (h d) -> p h d", d=HD2)
                k = PB[:, WB, 0:D].rearrange("p (h d) -> p h d", d=HD2)
                stt(QN2[:, :, 32:48], q, float(HD2) ** -0.5, QN2[:, :, 0:16], ALU.mult, ALU.subtract).then_inc(sem["lo2"], 1)
                dve.wait_ge(sem["lo2"], own(i, "lo2"))
                tt(KN2[:, :, 16:32], k, KN2[:, :, 0:16], ALU.subtract).then_inc(sem["lo2"], 1)
                dve.wait_ge(sem["lo2"], own(i, "lo2"))
                dve.wait_ge(sem["packed2_t"], at(i, "packed2_t", 1))
                dve.tensor_copy(flat(QT), h16(WA)).then_inc(sem["qt_sb"], 1)
                dve.wait_ge(sem["qt_sb"], own(i, "qt_sb"))
                for r in range(2):
                    max_pair(NM[:, 8 * r:8 * r + 8], P)
                max_parts(16, lambda k: MN[:, 0, 16 * k:16 * k + 16])
                dve.wait_ge(sem["pv_done"], at(i, "pv_done", 28))
                o = PB[:, OA, 0:17 * H2].rearrange("p (h d) -> p h d", d=17)
                dve.reciprocal(RS[:, 0:H2], o[:, :, 16]).then_inc(sem["dve"], 1)
                dve.wait_ge(sem["dve"], own(i, "dve"))
                tt(ON[:, :].rearrange("p (h d) -> p h d", d=HD2), o[:, :, 0:16],
                          RS[:, 0:H2, None].broadcast_to([P, H2, HD2]), ALU.mult).then_inc(sem["o_norm"], 1)
                dve.wait_ge(sem["o_norm"], own(i, "o_norm"))
                dve.wait_ge(sem["res"], at(i, "res", 2))
                stt(X3[:, :], PB[:, WB, 0:D], TG[:, 0:1], X2[:, :], ALU.mult, ALU.add).then_inc(sem["x3"], 1)
                dve.wait_ge(sem["x3"], own(i, "x3"))

                stats(X3[:, :])
                dve.wait_ge(sem["rstd"], at(i, "rstd", 3))
                ts(XH[:, :], X3[:, :], MV[:, 0:1], RSTD[:, :], ALU.subtract, ALU.mult).then_inc(sem["xh"], 1)
                dve.wait_ge(sem["xh"], own(i, "xh"))
                dve.tensor_copy(XNT[:, :, 0], CXT[:, 0:NC, 1]).then_inc(sem["dve"], 1)
                dve.wait_ge(sem["dve"], own(i, "dve"))
                dve.wait_ge(sem["s0_in"], at(i, "s0_in"))
                dve.tensor_copy(A3[:, :, :, 0], S0[:, :, :].rearrange("p c d -> p d c")).then_inc(sem["dve"], 1)
                dve.wait_ge(sem["dve"], own(i, "dve"))
                dve.wait_ge(sem["xnt"], at(i, "xnt", 2))
                tt(SX[:, :, :], XNT[:, :, 0:P], XNT[:, :, 1:P + 1], ALU.subtract).then_inc(sem["dve"], 1)
                dve.wait_ge(sem["dve"], own(i, "dve"))
                stt(XM[:, 0, :], SX[:, 0, :], vec("maax", 0), XNT[:, 0, 1:P + 1], ALU.mult, ALU.add).then_inc(sem["dve"], 1)
                dve.wait_ge(sem["dve"], own(i, "dve"))
                stt(XM[:, 1, :], SX[:, 1, :], vec("maax", 1), XNT[:, 1, 1:P + 1], ALU.mult, ALU.add).then_inc(sem["xm"], 1)
                dve.wait_ge(sem["xm"], own(i, "xm"))
                for n in (1, 0, 2, 3, 4):
                    dve.wait_ge(sem["mix"], at(i, "mix"))
                    stt(T5[:, n, 0, :], PB[:, 2 + n, 0:P], vec(f"st{n}", 0), SX[:, 0, :], ALU.add, ALU.mult).then_inc(sem["dve"], 1)
                    dve.wait_ge(sem["dve"], own(i, "dve"))
                    stt(T5[:, n, 1, :], PB[:, 2 + n, P:2 * P], vec(f"st{n}", 1), SX[:, 1, :], ALU.add, ALU.mult).then_inc(sem["t5"], 1)
                    dve.wait_ge(sem["t5"], own(i, "t5"))
                dve.wait_ge(sem["krv_sb"], at(i, "krv_sb", 3))
                dve.wait_ge(sem["ws"], at(i, "ws"))
                stt(RUK[:, 0, :], KR[:, 1, 0, :], vec("u", 0), KR[:, 0, 0, :], ALU.mult, ALU.mult).then_inc(sem["dve"], 1)
                dve.wait_ge(sem["dve"], own(i, "dve"))
                stt(RUK[:, 1, :], KR[:, 1, 1, :], vec("u", 1), KR[:, 0, 1, :], ALU.mult, ALU.mult).then_inc(sem["ruk"], 1)
                dve.wait_ge(sem["ruk"], own(i, "ruk"))
                for n in range(4):
                    dve.wait_ge(sem["vd"], at(i, "vd", n + 1))
                    vd = PB[:, 2 + n, :].rearrange("p (d c t) -> p d c t", d=2, c=NC)
                    tt(A3[:, 2 * n:2 * n + 2, :, 1:P], vd[:, :, :, 0:P - 1],
                              KR[:, 0:1, :, 0:P - 1].broadcast_to([P, 2, NC, P - 1]), ALU.mult).then_inc(sem["dve"], 1)
                    dve.wait_ge(sem["dve"], own(i, "dve"))
                    dve.tensor_tensor_scan(SC3[:, 2 * n:2 * n + 2].rearrange("p d c t -> p (d c t)"),
                                                  WS[:, :, :, :].rearrange("p d c t -> p (d c t)"),
                                                  A3[:, 2 * n:2 * n + 2].rearrange("p d c t -> p (d c t)"),
                                                  0.0, ALU.mult, ALU.add).then_inc(sem["sc"], 1)
                    dve.wait_ge(sem["sc"], own(i, "sc"))
                h3 = lambda ap: ap.rearrange("p (h d) -> p h d", d=S3)
                b8 = lambda ap: ap[:, :, None].broadcast_to([P, H3, S3])
                dve.wait_ge(sem["krv_sb"], at(i, "krv_sb", 4))
                stt(GT[:, :], GT[:, :], 1.0, PB[:, OA, 0:D], ALU.add, ALU.mult).then_inc(sem["gt"], 1)
                dve.wait_ge(sem["gt"], own(i, "gt"))
                dve.wait_ge(sem["att_ps"], at(i, "att_ps"))
                tt(h3(ATT[:, :]), h3(VN3[:, :]), b8(PB[:, OB, D:D + H3]), ALU.mult).then_inc(sem["dve"], 1)
                dve.wait_ge(sem["dve"], own(i, "dve"))
                tt(ATT[:, :], ATT[:, :], PB[:, OB, 0:D], ALU.add).then_inc(sem["dve"], 1)
                dve.wait_ge(sem["dve"], own(i, "dve"))
                dve.tensor_reduce(G8[:, 0, :], h3(ATT[:, :]), X_AXIS, ALU.add).then_inc(sem["dve"], 1)
                dve.wait_ge(sem["dve"], own(i, "dve"))
                ts(G8[:, 0, :], G8[:, 0, :], 1.0 / S3, None, ALU.mult).then_inc(sem["dve"], 1)
                dve.wait_ge(sem["dve"], own(i, "dve"))
                tt(h3(DD[:, :]), h3(ATT[:, :]), b8(G8[:, 0, :]), ALU.subtract).then_inc(sem["d8"], 1)
                dve.wait_ge(sem["d8"], own(i, "d8"))
                dve.wait_ge(sem["sq"], at(i, "sq"))
                dve.tensor_reduce(G8[:, 1, :], h3(SQ[:, :]), X_AXIS, ALU.add).then_inc(sem["var_in"], 1)
                dve.wait_ge(sem["var_in"], own(i, "var_in"))
                dve.wait_ge(sem["rstd"], at(i, "rstd", 4))
                tt(h3(Y[:, :]), h3(DD[:, :]), b8(G8[:, 2, :]), ALU.mult).then_inc(sem["dve"], 1)
                dve.wait_ge(sem["dve"], own(i, "dve"))
                tt(Y[:, :], Y[:, :], BCR[:, BC["gnw"], :], ALU.mult).then_inc(sem["dve"], 1)
                dve.wait_ge(sem["dve"], own(i, "dve"))
                tt(Y[:, :], Y[:, :], BCR[:, BC["gnb"], :], ALU.add).then_inc(sem["dve"], 1)
                dve.wait_ge(sem["dve"], own(i, "dve"))
                stt(Y[:, :], Y[:, :], 0.5, GT[:, :], ALU.mult, ALU.mult).then_inc(sem["y"], 1)
                dve.wait_ge(sem["y"], own(i, "y"))
                dve.wait_ge(sem["y_o"], at(i, "y_o"))
                tt(X4[:, :], PB[:, WB, 0:D], X3[:, :], ALU.add).then_inc(sem["x4"], 1)
                dve.wait_ge(sem["x4"], own(i, "x4"))
                stats(X4[:, :])
                dve.wait_ge(sem["rstd"], at(i, "rstd", 5))
                ts(XH[:, :], X4[:, :], MV[:, 0:1], RSTD[:, :], ALU.subtract, ALU.mult).then_inc(sem["xh"], 1)
                dve.wait_ge(sem["xh"], own(i, "xh"))
                dve.tensor_copy(XNT[:, :, 0], CXT[:, 0:NC, 0]).then_inc(sem["dve"], 1)
                dve.wait_ge(sem["dve"], own(i, "dve"))
                dve.wait_ge(sem["xnt"], at(i, "xnt", 4))
                tt(SX[:, :, :], XNT[:, :, 0:P], XNT[:, :, 1:P + 1], ALU.subtract).then_inc(sem["dve"], 1)
                dve.wait_ge(sem["dve"], own(i, "dve"))
                for n, name in enumerate(("fmk", "fmr")):
                    for c in range(NC):
                        stt(XKR[:, n, c, :], SX[:, c, :], vec(name, c), XNT[:, c, 1:P + 1], ALU.mult, ALU.add).then_inc(sem["xkr"], 1)
                        dve.wait_ge(sem["xkr"], own(i, "xkr"))
                dve.wait_ge(sem["ff2"], at(i, "ff2"))
                dve.wait_ge(sem["tr"], at(i, "tr"))
                stt(TR[:, :], TR[:, :], 1.0, PB[:, 4, 0:D], ALU.add, ALU.mult).then_inc(sem["dve"], 1)
                dve.wait_ge(sem["dve"], own(i, "dve"))
                dve.wait_ge(sem["out_stored"], at(i, "out_stored"))
                stt(OUT[:, :], TR[:, :], 0.5, X4[:, :], ALU.mult, ALU.add).then_inc(sem["batch_done"], 1)
                dve.wait_ge(sem["batch_done"], own(i, "batch_done"))
                own.end()


def kernel(**inputs):
    import numpy as np
    import ml_dtypes
    import concourse.bacc as bacc
    from concourse.bass_utils import run_bass_kernel_spmd as run

    a = {k: np.asarray(v) for k, v in inputs.items()}
    L0, L1, L2, L3 = (lambda n, p=f"L{k}_xattn_": a[p + n] for k in range(4))
    cat = np.concatenate
    wall = cat([L0("Wq"), L0("Wk"), L0("Wv"), L0("Wo"), L2("Wk").T, L2("Wv").T, L2("Wq").T, L2("Wo").T,
                L3("maa_w1"), L3("decay_w1"), L3("Wr").T, L3("Wk").T, L3("Wv").T, L3("Wg").T, L3("Wo").T,
                L3("ffn_Wk").T, L3("ffn_Wr").T, L3("ffn_Wv").T], axis=1)
    w1 = cat([L1("Wq").T, L1("Wk").T, L1("Wv").T], axis=1)
    rows = cat([L0("bq"), L0("bk"), L0("bv"), L0("bo"), L1("bq"), L1("bk"), L1("bv")]).reshape(1, -1)
    bcast = cat([L0("gamma"), L0("beta"), L3("gn_w"), L3("gn_b")]).reshape(1, -1)
    st = L3("maa_stack")
    cols = np.stack([L2("ln_gamma"), L2("ln_beta"), L3("ln1_w"), L3("ln1_b"), L3("ln2_w"), L3("ln2_b"), L3("maa_x"),
                     st[0], st[1], st[2], st[3], st[4], L3("time_decay"), L3("faaaa").reshape(-1),
                     L3("ffn_maa_k"), L3("ffn_maa_r")], axis=1)
    ident = np.eye(P, dtype=np.float32)
    pick0 = np.zeros((P, 32), ml_dtypes.bfloat16)
    pick0[:96] = np.tile(np.eye(32), (3, 1))
    pick1 = np.zeros((P, 16), ml_dtypes.bfloat16)
    pick1[:48] = np.tile(np.eye(16), (3, 1))
    gsel = np.repeat(np.eye(16, dtype=np.float32), S3, axis=0)
    srep = np.zeros((16, S3, S3, 16, S3), np.float32)
    for h in range(16):
        for d in range(S3):
            srep[h, d, d, h, :] = 1.0
    arrays = dict(
        x=a["x"], ctx_in=a["ctx_2048"], mask0=a["mask_Bx1xSxS2_ff0"].reshape(B, T, T),
        mask1=a["mask_Bx1x2048_bf1"].view(np.uint8), mask2=a["mask_BxS2_bf1"].view(np.uint8),
        wall=wall, w1=w1, maaw2=L3("maa_w2").reshape(160, D), decw2=L3("decay_w2"), rows=rows, bcast=bcast, cols=cols,
        gate=L2("gate").reshape(1, 1), ident=ident, ident_h=ident.astype(np.float16),
        ident_b=ident.astype(ml_dtypes.bfloat16), pick0=pick0, pick1=pick1, gsel=gsel, srep=srep.reshape(P, S3, P))
    arrays = {k: np.ascontiguousarray(v) for k, v in arrays.items()}
    nc = bacc.Bacc("TRN2", target_bir_lowering=False, num_devices=1)
    args = {k: nc.dram_tensor("in_" + k, v.shape, mybir.dt.from_np(v.dtype), kind="ExternalInput").ap()
            for k, v in arrays.items()}
    out = nc.dram_tensor("out_x", (B, T, D), F32, kind="ExternalOutput").ap()
    build(nc, out=out, **args)
    r = run(nc, [{"in_" + k: v for k, v in arrays.items()}], core_ids=[0])
    return r.results[0]["out_x"]
```

```python
from contextlib import ExitStack


import concourse.bass as bass
from concourse import mybir

F32, F16, BF16, U8 = mybir.dt.float32, mybir.dt.float16, mybir.dt.bfloat16, mybir.dt.uint8
ALU = mybir.AluOpType
ACT = mybir.ActivationFunctionType
X_AXIS = mybir.AxisListType.X

P = 128
B, T, D = 16, 128, 256
NC = D // P
H0, KV0, HD0 = 32, 8, 8
H1, HD1 = 16, 8
H2, HD2 = 16, 16
H3, S3 = 32, 8
QB = 32
QB2 = 64
VB = 32
NEG = 60000.0

W_COLS = {}
_at = 0
for _name, _n in (("q0", 256), ("kv0", 128), ("o0", 256), ("kv2", 512), ("q2", 256), ("o2", 256),
                  ("maa1", 160), ("dec1", 64), ("r3", 256), ("k3", 256), ("v3", 256), ("g3", 256),
                  ("o3", 256), ("fk3", 256), ("fr3", 256), ("fv3", 256)):
    W_COLS[_name] = (_at, _at + _n)
    _at += _n
W_TOTAL = _at
R_COLS = {"bq0": (0, 256), "bkv0": (256, 384), "bo0": (384, 640), "bq1": (640, 768), "bkv1": (768, 1024)}
R_TOTAL = 1024
BC = {"gamma0": 0, "beta0": 1, "gnw": 2, "gnb": 3}
COL = {n: k for k, n in enumerate(("lng2", "lnb2", "ln1w", "ln1b", "ln2w", "ln2b", "maax", "st0", "st1", "st2",
                                   "st3", "st4", "td", "u", "fmk", "fmr"))}


NPAIR = B // 2
AT0, AT1, AT2 = 0, 8, 24

PER = dict(
    dve=14, pool=8,
    xc_t=1, xc_sb=1, proj0=1, hi0=4, lo0=2, packed_t=6, qt_sb=3, kt_sb=3,
    o_raw=3, o_back=3, o_norm=3, o_t=2, ot_sb=2, res=2, var_in=2, rstd=2, x1=1,
    kv1=1, q1=1, hi1=4, hi1q=1, lo1=3, xm1=1, sq1=1, var1=1, std1=1, ms_t=1, xn1=1,
    x2=1, x2_t=1, x2_sb=1, c_hat=1, c_t=1, ct2_sb=2, proj2=1, hi2=4, lo2=3, x3=1,
    x_in=16, c_in=16, m0_in=16, mx_in=16, s0_in=32, out_stored=16,
    max_scores=28, max_read=28, exp_scores=28, exp_done=28, pv_done=28,
    m_split=9, nm=3, m_t=3, m_sb=3, mask_pool=4, mask_parts=1, mx_step=3, st_cols=1,
    dve3=15, act3=3, pool3=3, x3_free=1,
    xh3=2, xh3_t=2, xnt3=4, xm3=1, xxx3=1, xxt3=2, mix3=5, t53=5, x53=5, wd3_ps=1, wd3=1, w3_ps=1, ew3=1, ws3=1,
    k3_ps=1, k3_sb=1, v3_ps=1, v3_sb=1, r3_ps=1, r3_sb=1, g3_ps=1, g3_sb=1, vt3_ps=1, vt3_sb=1, gt3=1,
    vd3=8, a3=8, sc3=8, pr3=8, ruk3=1, att3=1, att3_read=1, d83=1, sq3=1, var3=3, rstd3=3,
    y3=1, y3_t=1, yt3_sb=1, y3_o=1, xkr3=4, ff1=2, kk3=1, tr3=1, ff2=1, s0_read=1, l3_done=1,
)
OF_EACH = list(PER)[:list(PER).index("x_in")]

ORDER = "LALLALALALALALAALAALALALAALALALALALAALAALAALAAALAAALAALAAAAAAAAAAAA"


def build(nc, x, ctx_in, mask0, mask1, mask2, wall, w1, maaw2, decw2, rows, bcast, cols, gate,
          ident, ident_h, ident_b, pick0, pick1, gsel, srep, out):
    with ExitStack() as ctx:
        def sb(name, shape, dt=F32):
            return ctx.enter_context(nc.sbuf_tensor(name, shape, dt))

        W = sb("W", [P, NC, W_TOTAL])
        W1 = sb("W1", [P, 3 * P])
        MAA2 = sb("MAA2", [P, D])
        MAA2b = sb("MAA2b", [32, D])
        DEC2 = sb("DEC2", [64, D])
        ROWS = sb("ROWS", [1, R_TOTAL])
        BCR = sb("BCR", [P, 4, D])
        CV = sb("CV", [P, NC, 16])
        ID = sb("ID", [P, P])
        IDH = sb("IDH", [P, P], F16)
        IDB = sb("IDB", [P, P], BF16)
        PICK0 = sb("PICK0", [P, 32], BF16)
        PICK1 = sb("PICK1", [P, 16], BF16)
        GSEL = sb("GSEL", [P, 16])
        SREP = sb("SREP", [P, 8, P])
        IDLE = sb("IDLE", [P, 2])
        IDLE_DVE = sb("IDLE_DVE", [P, 1])
        GATE = sb("GATE", [P, 1])
        TG = sb("TG", [P, 1])
        ONES = sb("ONES", [1, P])
        NHALF = sb("NHALF", [P, 64])
        MRAW1 = sb("MRAW1", [16, 2 * P], U8)
        MRAW2 = sb("MRAW2", [16, P], U8)
        MF = sb("MF", [16, 3 * P], F16)
        KM1 = sb("KM1", [P, 16, 2], F16)
        KM2 = sb("KM2", [P, 16, 1], F16)
        X = sb("X", [P, 2, D])
        C = sb("C", [P, 2, D])
        M0 = sb("M0", [P, 2, P])
        MXR = sb("MXR", [P, 2, D], U8)
        S0 = sb("S0", [P, 2, NC, S3])
        CXT = sb("CXT", [P, 2, 4, P])
        MP = sb("MP", [P, 3, 2, P], BF16)
        MR = sb("MR", [P, 2, P])
        QN0 = sb("QN0", [P, 2, H0, QB], F16)
        KN0 = sb("KN0", [P, 2, KV0, 4, QB], F16)
        V0 = sb("V0", [P, 2, KV0, VB])
        QN1, KN1 = QN0, KN0[:, :, :, :, :].rearrange("p c a g b -> p c (a g) b")
        V1 = sb("V1", [P, 2, 2 * H1, VB])
        QN2 = sb("QN2", [P, 2, H2, QB2], F16)
        KN2 = sb("KN2", [P, 2, H2, QB2], F16)
        V2 = sb("V2", [P, 2, H2, VB])
        QT = sb("QT", [P, 2, 8, P], F16)
        KT = sb("KT", [P, 2, 8, P], F16)
        NM = sb("NM", [P, 2, 32])
        NR = sb("NR", [P, 2, 32])
        MN = sb("MN", [P, 2, 2, P], BF16)
        MT = sb("MT", [P, 2, 2 * P], BF16)
        PROB = sb("PROB", [P, 8, 512])
        OTT = sb("OTT", [P, 8, P])
        RS = sb("RS", [P, 2, 32])
        ON = sb("ON", [P, 2, D])
        OT = sb("OT", [P, 2, NC, P])
        X1 = sb("X1", [P, 2, D])
        XH = sb("XH", [P, 2, D])
        ST = sb("ST", [P, 2, 6])
        MV = sb("MV", [P, 2, 2])
        VE = sb("VE", [P, 2])
        RSTD = sb("RSTD", [P, 2])
        MXF = sb("MXF", [P, 2, D])
        XM1 = sb("XM1", [P, 2, D])
        SM = sb("SM", [P, 2, 8])
        MEAN = sb("MEAN", [P, 2, 2, P])
        VAR = sb("VAR", [P, 2, 2, P])
        EX2 = sb("EX2", [P, 2, 2, P])
        X3 = sb("X3", [P, 2, D])
        STC3 = sb("STC3", [P, 2, NC, 2])
        STC = sb("STC", [P, 2, NC, 2])
        X3L = sb("X3L", [P, 2, D])
        XH3 = sb("XH3", [P, 2, D])
        ST3 = sb("ST3", [P, 2, 6])
        MV3 = sb("MV3", [P, 2, 2])
        VE3 = sb("VE3", [P, 64])
        RSTD3 = sb("RSTD3", [P, 2])
        XNT = sb("XNT", [P, NC, 2, P + 1])
        SX = sb("SX", [P, NC, 2, P])
        XM = sb("XM", [P, NC, 2, P])
        XXT = sb("XXT", [P, 2 * P])
        XXT4 = sb("XXT4", [32, 2 * P])
        T5 = sb("T5", [P, 2, NC, 2, P])
        WD = sb("WD", [64, 2 * P])
        EW = sb("EW", [P, NC, 2, P])
        WS = sb("WS", [P, NC, 2, P])
        KS = sb("KS", [P, NC, 2, P])
        RR = sb("RR", [P, NC, 2, P])
        VT3 = sb("VT3", [P, NC, 2, P])
        VN3 = sb("VN3", [P, 2 * D])
        A3 = sb("A3", [P, 8, NC, 2, P])
        RUK = sb("RUK", [P, NC, 2, P])
        ATT = sb("ATT", [P, 2 * D])
        DD = sb("DD", [P, 2 * D])
        G8 = sb("G8", [P, 3, 64])
        GT = sb("GT", [P, 2 * D])
        X4 = sb("X4", [P, 2, D])
        OUT = sb("OUT", [P, 2, D])

        X2, XN1, XSQ, CH, X2T, STD = X1, XM1, XH, ON, OT, VAR
        CT2 = XH[:, :, :].rearrange("p c (n t) -> p c n t", n=NC)
        YT, KKR, KK, TR, Y, XKR, X5 = VT3, KS, RR, VN3, DD, T5, A3
        SQ = EW[:, :, :, :].rearrange("p c b t -> p (c b t)")
        PB = ctx.enter_context(nc.psum_tensor("PB", [P, 8, 512], F32))

        sem = {n: ctx.enter_context(nc.semaphore(n)) for n in PER if n not in OF_EACH}
        seq = [{n: ctx.enter_context(nc.semaphore(f"{n}_{c}")) for n in OF_EACH} for c in range(2)]
        w_in = ctx.enter_context(nc.semaphore("w_in"))
        masks_in = ctx.enter_context(nc.semaphore("masks_in"))
        set_dve = ctx.enter_context(nc.semaphore("set_dve"))
        set_act = ctx.enter_context(nc.semaphore("set_act"))
        set_pe = ctx.enter_context(nc.semaphore("set_pe"))
        block = ctx.enter_context(nc.Block())
        N_WEIGHTS = 17
        BOTH = (0, 1)

        def at(j, name, k=None):
            return j * PER[name] + (PER[name] if k is None else k)

        class Count:

            def __init__(self, j):
                self.j, self.given = j, {}

            def __call__(self, name, c=None):
                self.given[name, c] = self.given.get((name, c), 0) + 1
                return at(self.j, name, self.given[name, c])

            def end(self):
                wrong = {n: (k, PER[n[0]]) for n, k in self.given.items() if k != PER[n[0]]}
                assert not wrong, wrong

        def wcol(name, c, a=0, b=None):
            lo, hi = W_COLS[name]
            return W[:, c, lo + a:(hi if b is None else lo + b)]

        def row(name):
            return ROWS[0:1, R_COLS[name][0]:R_COLS[name][1]]

        def vec(name, c):
            return CV[:, c, COL[name]:COL[name] + 1]

        def h16(bank):
            return PB[:, bank, :].bitcast(F16)

        def b16(bank):
            return PB[:, bank, :].bitcast(BF16)

        def turns(eng, attention, layer3):
            for _ in attention(0, True):
                pass
            with eng.Fori(1, NPAIR) as j:
                a, b = attention(j, False), layer3(j - 1, False)
                for step in ORDER:
                    next(a if step == "A" else b)
                assert next(a, None) is None and next(b, None) is None
            for _ in layer3(NPAIR - 1, False):
                pass

        @block.sync
        def _(sp):
            pair = lambda ap: ap.rearrange("(j c) t d -> j t c d", c=2)
            xv, cv, mv, ov = pair(x), pair(ctx_in), pair(mask0), pair(out)
            mxv = mask1.rearrange("(j c) o d -> j o (c d)", c=2)
            sv = ctx_in.rearrange("(j c) t d -> j c t d", c=2)

            def load(j):
                sp.dma_start(X[:, :, :], xv[j]).then_inc(sem["x_in"], 16)
                sp.dma_start(C[:, :, :], cv[j]).then_inc(sem["c_in"], 16)
                sp.dma_start(M0[:, :, :], mv[j]).then_inc(sem["m0_in"], 16)
                sp.dma_start(MXR[:, :, :].rearrange("p c d -> p (c d)"), mxv[j].broadcast_to([P, 2 * D])).then_inc(sem["mx_in"], 16)

            def load_state(j):
                for c in BOTH:
                    last = sp.dma_start(S0[:, c, :, :], sv[j, c, 2:2 + S3, :].rearrange("r (p d) -> (r p) d", d=S3)
                                        .rearrange("(n p) d -> p n d", p=P))
                    last.then_inc(sem["s0_in"], 16)

            sp.sem_inc(sem["out_stored"], 16)
            sp.dma_start(ID[:, :], ident).then_inc(w_in, 16)
            load(0)
            load_state(0)
            wv = wall.rearrange("(c p) n -> p c n", p=P)
            for a, b in ((0, 640), (640, 1664), (1664, W_TOTAL)):
                sp.dma_start(W[:, :, a:b], wv[:, :, a:b]).then_inc(w_in, 16)
            for dst, src in ((W1[:, :], w1), (MAA2[:, :], maaw2[0:P, :]), (MAA2b[:, :], maaw2[P:P + 32, :]),
                             (DEC2[:, :], decw2), (ROWS[:, :], rows),
                             (CV[:, :, :], cols.rearrange("(c p) n -> p c n", p=P)),
                             (IDH[:, :], ident_h), (IDB[:, :], ident_b), (PICK0[:, :], pick0),
                             (PICK1[:, :], pick1), (GSEL[:, :], gsel), (SREP[:, :, :], srep)):
                sp.dma_start(dst, src).then_inc(w_in, 16)
            sp.dma_start(BCR[:, :, :].rearrange("p a b -> p (a b)"), bcast.broadcast_to([P, 4 * D])).then_inc(w_in, 16)
            sp.dma_start(GATE[:, :], gate.broadcast_to([P, 1])).then_inc(masks_in, 16)
            sp.dma_start(MRAW1[:, :], mask1.rearrange("b o d -> (b o) d")).then_inc(masks_in, 16)
            sp.dma_start(MRAW2[:, :], mask2).then_inc(masks_in, 16)

            with sp.Fori(1, NPAIR) as j:
                for c in BOTH:
                    sp.wait_ge(seq[c]["x3"], at(j - 1, "x3"))
                load(j)
                sp.wait_ge(sem["s0_read"], at(j - 1, "s0_read"))
                load_state(j)
                sp.wait_ge(sem["l3_done"], at(j - 1, "l3_done"))
                sp.dma_start(ov[j - 1], OUT[:, :, :]).then_inc(sem["out_stored"], 16)
            sp.wait_ge(sem["l3_done"], NPAIR)
            sp.dma_start(ov[NPAIR - 1], OUT[:, :, :]).then_inc(sem["out_stored"], 16)
            sp.wait_ge(sem["out_stored"], 16 * (NPAIR + 1))

        @block.tensor
        def _(pe):
            mm = pe.matmul
            pe.wait_ge(w_in, 16 * N_WEIGHTS)
            pe.wait_ge(set_dve, 1)
            for k in range(3):
                last = pe.transpose(h16(0)[:, 16 * k:16 * k + 16], MF[:, P * k:P * k + P], IDH[0:16, 0:16])
            last.then_inc(set_pe, 1)
            pe.wait_ge(set_dve, 2)

            def project(dst, lhs, weights, bias=None):
                n = len(lhs)
                for c in range(n):
                    last = mm(dst, lhs[c], weights[c], start=(c == 0), stop=(c == n - 1 and bias is None))
                if bias is not None:
                    last = mm(dst, ONES[0:1, :], bias, start=False, stop=True)
                return last

            def turn_two(bank, src, at_col=0):
                for c in range(NC):
                    last = pe.transpose(PB[:, bank, at_col + P * c:at_col + P * c + P], src[:, P * c:P * c + P], ID[:, :])
                return last

            def turn_packed(bank, src):
                for k in range(8):
                    last = pe.transpose(h16(bank)[:, P * k:P * k + P], src[:, P * k:P * k + P], IDH[:, :])
                return last

            def attention(j, first):
                def packed(n, lo, qn, kn):
                    for c in BOTH:
                        pe.wait_ge(seq[c][lo], at(j, lo))
                        turn_packed(2 + c, qn(c)).then_inc(seq[c]["packed_t"], 1)
                        turn_packed(c, kn(c)).then_inc(seq[c]["packed_t"], 1)

                def maxima(base, n_pairs, unit, units):
                    layer = {AT0: 1, AT1: 2, AT2: 3}[base]
                    for c in BOTH:
                        pe.wait_ge(seq[c]["qt_sb"], at(j, "qt_sb", layer))
                        pe.wait_ge(seq[c]["kt_sb"], at(j, "kt_sb", layer))
                    for c in BOTH:
                        for n in range(n_pairs):
                            m = c * n_pairs + n
                            if m >= 2:
                                pe.wait_ge(sem["max_read"], at(j, "max_read", base + m - 1))
                            for k in range(2):
                                last = unit(2 * (m % 2) + k, c, *units[2 * n + k])
                            last.then_inc(sem["max_scores"], 1)
                        yield

                def turn_maxima(layer, n):
                    pe.wait_ge(sem["nm"], at(j, "nm", layer))
                    for c in BOTH:
                        for a in range(n):
                            last = pe.transpose(b16(4 + c)[:, P * a:P * a + P], MN[:, c, a, :], IDB[:, :])
                    last.then_inc(sem["m_t"], 1)

                def attend(base, n_pairs, score_unit, units, per_product, products, before_product):
                    issued = 0
                    pe.wait_ge(sem["m_sb"], at(j, "m_sb", {AT0: 1, AT1: 2, AT2: 3}[base]))
                    for step in range(2 * n_pairs // per_product):
                        first_of_next = step * per_product == n_pairs
                        ahead = per_product * (step + 1) + 2
                        if base == AT0 and first_of_next:
                            ahead += 1
                        while issued < min(ahead, 2 * n_pairs):
                            c, n = issued // n_pairs, issued % n_pairs
                            if issued >= 2:
                                pe.wait_ge(sem["exp_done"], at(j, "exp_done", base + issued - 1))
                            for k in range(2):
                                last = score_unit(2 * (issued % 2) + k, c, *units[2 * n + k])
                            last.then_inc(sem["exp_scores"], 1)
                            issued += 1
                        m = step * per_product
                        c, n = m // n_pairs, m % n_pairs
                        before_product(c, n)
                        pe.wait_ge(sem["exp_done"], at(j, "exp_done", base + m + per_product))
                        products((2 * (base + m)) % 8, c, n).then_inc(sem["pv_done"], per_product)
                        yield step

                def turn_back(c, layer, bank, pieces):
                    pe.wait_ge(seq[c]["o_raw"], at(j, "o_raw", layer))
                    for n, piece in enumerate(pieces):
                        last = pe.transpose(PB[:, bank + n // 4, P * (n % 4):P * (n % 4) + P], OTT[:, piece, :], ID[:, :])
                    last.then_inc(seq[c]["o_back"], 1)

                def out_turn(c, bank, layer):
                    pe.wait_ge(seq[c]["o_norm"], at(j, "o_norm", layer))
                    turn_two(bank + c, ON[:, c, :]).then_inc(seq[c]["o_t"], 1)

                def out_project(c, bank, k, weights, bias=None):
                    pe.wait_ge(seq[c]["ot_sb"], at(j, "ot_sb", k))
                    project(PB[:, bank + c, D:2 * D], [OT[:, c, n, :] for n in range(NC)],
                            [wcol(weights, n) for n in range(NC)], bias).then_inc(seq[c]["res"], 1)

                pe.wait_ge(sem["c_in"], at(j, "c_in"))
                pe.wait_ge(sem["x_in"], at(j, "x_in"))
                for c in BOTH:
                    turn_two(c, C[:, c, :])
                    turn_two(c, X[:, c, :], D).then_inc(seq[c]["xc_t"], 1)
                yield
                for c in BOTH:
                    pe.wait_ge(seq[c]["xc_sb"], at(j, "xc_sb"))
                    project(PB[:, 2 + c, 0:D], [CXT[:, c, 2 + n, :] for n in range(NC)], [wcol("q0", n) for n in range(NC)], row("bq0"))
                    project(PB[:, 2 + c, D:D + P], [CXT[:, c, n, :] for n in range(NC)],
                            [wcol("kv0", n) for n in range(NC)], row("bkv0")).then_inc(seq[c]["proj0"], 1)
                yield
                packed(1, "lo0", lambda c: QN0[:, c, :, :].rearrange("p a b -> p (a b)"),
                       lambda c: KN0[:, c, :, :, :].rearrange("p a g b -> p (a g b)"))
                yield
                pe.wait_ge(sem["mask_parts"], at(j, "mask_parts"))
                K = 3 * HD0

                def l0_scores(bank, c, half, g, keys_out):
                    for n in range(3):
                        if keys_out:
                            mm(PB[:, bank, :], MP[:, n, c, :], IDB[:, None, :].broadcast_to([P, 4, P]), start=(n == 0), stop=False)
                        else:
                            mm(PB[:, bank, :], IDB[:, :], MP[:, n, c:c + 1, :].broadcast_to([P, 4, P]), start=(n == 0), stop=False)
                    for k in range(4):
                        kv = 4 * half + k
                        dst = PB[:, bank, P * k:P * k + P]
                        q, key = QT[32 * g:32 * g + K, c, kv, :], KT[32 * g:32 * g + K, c, kv, :]
                        if keys_out:
                            mm(dst, key, q, start=False, stop=False)
                        else:
                            last = mm(dst, q, key, start=False, stop=(k == 3))
                    if keys_out:
                        for k in range(4):
                            col = (4 * half + g) * 4 + k
                            last = mm(PB[:, bank, P * k:P * k + P], PICK0[:, col:col + 1].broadcast_to([P, P]), MT[:, c, 0:P],
                                      start=False, stop=(k == 3))
                    return last

                def l0_products(slot, c, n):
                    for k in range(4):
                        last = mm(PB[32 * k:32 * k + 32, 4 + n // 2, D * (n % 2):D * (n % 2) + D], V0[:, c, 4 * (n // 2) + k, :],
                                  PROB[:, slot:slot + 2, P * k:P * k + P], start=True, stop=True)
                    return last

                def l0_before(c, n):
                    if c == 1 and n == 0:
                        turn_back(0, 1, 4, range(8))
                        pe.wait_ge(seq[0]["o_norm"], at(j, "o_norm", 1))

                units0 = [(half, g) for half in range(2) for g in range(4)]
                yield from maxima(AT0, 4, lambda bank, c, half, g: l0_scores(bank, c, half, g, False), units0)
                if not first:
                    for c in BOTH:
                        pe.wait_ge(seq[c]["x3"], at(j - 1, "x3"))
                turn_maxima(1, 1)
                yield
                for m in attend(AT0, 4, lambda bank, c, half, g: l0_scores(bank, c, half, g, True), units0, 1, l0_products, l0_before):
                    if m == 7:
                        out_turn(0, 2, 1)
                    yield
                for c in BOTH:
                    for a in range(2):
                        for k, dst in enumerate((PB[:, c, P * a:P * a + P], PB[:, c, D + P * a:D + P * a + P])):
                            mm(dst, C[:, c, P * a:P * a + P], W1[:, P + P * k:2 * P + P * k], start=True, stop=False)
                            last = mm(dst, ONES[0:1, :], row("bkv1")[:, P * k:P * k + P], start=False, stop=True)
                    last.then_inc(seq[c]["kv1"], 1)
                    if c == 0:
                        turn_back(1, 1, 4, range(8))
                out_project(0, 2, 1, "o0", row("bo0"))
                yield
                out_turn(1, 2, 1)
                yield
                out_project(1, 2, 1, "o0", row("bo0"))
                yield
                for c in BOTH:
                    pe.wait_ge(seq[c]["x1"], at(j, "x1"))
                    for a in range(2):
                        mm(PB[:, 2 + c, P * a:P * a + P], X1[:, c, P * a:P * a + P], W1[:, 0:P], start=True, stop=False)
                        last = mm(PB[:, 2 + c, P * a:P * a + P], ONES[0:1, :], row("bq1"), start=False, stop=True)
                    last.then_inc(seq[c]["q1"], 1)
                yield
                packed(2, "lo1", lambda c: QN1[:, c, :, :].rearrange("p a b -> p (a b)"), lambda c: KN1[:, c, :, :].rearrange("p a b -> p (a b)"))
                yield
                K1 = 3 * HD1 + 1

                def l1_max(bank, c, a, jj, p):
                    rows_ = slice(32 * jj, 32 * jj + K1)
                    for k in range(2):
                        tt = 2 * p + k
                        last = mm(PB[:, bank, D * k:D * k + D], QT[rows_, c, 4 * a + tt, :], KT[rows_, c, tt:8:4, :], start=True, stop=True)
                    return last

                def l1_scores(bank, c, jj, tt):
                    rows_ = slice(32 * jj, 32 * jj + K1)
                    col = 4 * jj + tt
                    for n in range(2):
                        dst = PB[:, bank, D * n:D * n + D]
                        mm(dst, KT[rows_, c, 4 * n + tt, :], QT[rows_, c, tt:8:4, :], start=True, stop=False)
                        last = mm(dst, PICK1[:, col:col + 1].broadcast_to([P, P]), MT[:, c, :], start=False, stop=True)
                    return last

                def l1_products(slot, c, n):
                    tt = n // 2
                    for half in range(2):
                        for jj in range(4):
                            last = mm(PB[32 * jj:32 * jj + 32, 4 + tt // 2, D * (tt % 2):D * (tt % 2) + D], V1[:, c, H1 * half + 4 * tt + jj, :],
                                      PROB[:, slot + jj, D * half:D * half + D], start=(half == 0), stop=(half == 1))
                    return last

                def l1_before(c, n):
                    if c == 1 and n == 0:
                        turn_back(0, 2, 4, [2 * tt + a for a in range(2) for tt in range(4)])
                        pe.wait_ge(seq[0]["o_norm"], at(j, "o_norm", 2))

                yield from maxima(AT1, 8, l1_max, [(a, jj, p) for a in range(2) for jj in range(4) for p in range(2)])
                turn_maxima(2, 2)
                yield
                for m in attend(AT1, 8, l1_scores, [(jj, tt) for tt in range(4) for jj in range(4)], 2, l1_products, l1_before):
                    yield
                turn_back(1, 2, 4, [2 * tt + a for a in range(2) for tt in range(4)])
                for c in BOTH:
                    pe.wait_ge(seq[c]["c_hat"], at(j, "c_hat"))
                    turn_two(2 + c, CH[:, c, :]).then_inc(seq[c]["c_t"], 1)
                for c in BOTH:
                    pe.wait_ge(seq[c]["std1"], at(j, "std1"))
                    for a in range(2):
                        pe.transpose(PB[:, c, P * a:P * a + P], MEAN[:, c, a, :], ID[:, :])
                        last = pe.transpose(PB[:, c, D + P * a:D + P * a + P], STD[:, c, a, :], ID[:, :])
                    last.then_inc(seq[c]["ms_t"], 1)
                yield
                for c in BOTH:
                    pe.wait_ge(seq[c]["ct2_sb"], at(j, "ct2_sb"))
                    pe.wait_ge(seq[c]["x2"], at(j, "x2"))
                    turn_two(2 + c, X2[:, c, :], D).then_inc(seq[c]["x2_t"], 1)
                    project(PB[:, c, :], [CT2[:, c, n, :] for n in range(NC)], [wcol("kv2", n) for n in range(NC)])
                yield
                for c in BOTH:
                    pe.wait_ge(seq[c]["x2_sb"], at(j, "x2_sb"))
                    project(PB[:, 2 + c, 0:D], [X2T[:, c, n, :] for n in range(NC)],
                            [wcol("q2", n) for n in range(NC)]).then_inc(seq[c]["proj2"], 1)
                yield
                packed(3, "lo2", lambda c: QN2[:, c, :, :].rearrange("p a b -> p (a b)"), lambda c: KN2[:, c, :, :].rearrange("p a b -> p (a b)"))
                yield
                K2 = 3 * HD2 + 1

                def l2_scores(bank, c, r, tg, keys_out):
                    rows_ = slice(64 * r, 64 * r + K2)
                    for k in range(4):
                        tt = 4 * tg + k
                        dst = PB[:, bank, P * k:P * k + P]
                        if keys_out:
                            col = 8 * r + tt
                            mm(dst, KT[rows_, c, tt, :], QT[rows_, c, tt, :], start=True, stop=False)
                            last = mm(dst, PICK1[:, col:col + 1].broadcast_to([P, P]), MT[:, c, 0:P], start=False, stop=True)
                        else:
                            last = mm(dst, QT[rows_, c, tt, :], KT[rows_, c, tt, :], start=True, stop=True)
                    return last

                def l2_products(slot, c, n):
                    for tg in range(2):
                        for k in range(4):
                            last = mm(PB[32 * k:32 * k + 32, 4 + c, D * n + P * tg:D * n + P * tg + P], V2[:, c, 2 * (4 * tg + k) + n, :],
                                      PROB[:, slot + tg, P * k:P * k + P], start=True, stop=True)
                    return last

                units2 = [(r, tg) for r in range(2) for tg in range(2)]
                yield from maxima(AT2, 2, lambda bank, c, r, tg: l2_scores(bank, c, r, tg, False), units2)
                turn_maxima(3, 1)
                yield
                for m in attend(AT2, 2, lambda bank, c, r, tg: l2_scores(bank, c, r, tg, True), units2, 1, l2_products, lambda c, n: None):
                    yield
                for c in BOTH:
                    turn_back(c, 3, 4 + c, range(4 * c, 4 * c + 4))
                yield
                for c in BOTH:
                    out_turn(c, 4, 3)
                yield
                for c in BOTH:
                    out_project(c, 4, 2, "o2")
                yield

            def layer3(j, first):
                flat = lambda ap: ap.rearrange("p c b t -> p (c b t)")
                bt = lambda ap: ap.rearrange("p b t -> p (b t)")

                def to_channels(bank, weights, src):
                    for co in range(NC):
                        last = project(PB[:, bank, D * co:D * co + D], [wcol(weights, c, P * co, P * co + P) for c in range(NC)],
                                       [bt(src[:, c, :, :]) for c in range(NC)])
                    return last

                def to_tokens(bank, weights, src):
                    for b in BOTH:
                        last = project(PB[:, bank, D * b:D * b + D], [src[:, c, b, :] for c in range(NC)], [wcol(weights, c) for c in range(NC)])
                    return last

                def turn_pair(bank, src):
                    for b in BOTH:
                        for c in range(NC):
                            last = pe.transpose(PB[:, bank, D * c + P * b:D * c + P * b + P], src(b, c), ID[:, :])
                    return last

                def mix(k, n, bank):
                    for c in range(NC):
                        lhs = MAA2[32 * n:32 * n + 32, P * c:P * c + P] if n < 4 else MAA2b[:, P * c:P * c + P]
                        rhs = XXT[32 * n:32 * n + 32, :] if n < 4 else XXT4[:, :]
                        last = mm(PB[:, bank, D * c:D * c + D], lhs, rhs, start=True, stop=True)
                    last.then_inc(sem["mix3"], 1)

                pe.wait_ge(sem["xh3"], at(j, "xh3", 1))
                turn_pair(6, lambda b, c: XH3[:, b, P * c:P * c + P]).then_inc(sem["xh3_t"], 1)
                yield
                pe.wait_ge(sem["xm3"], at(j, "xm3"))
                project(PB[:, 7, 0:D], [wcol("maa1", c, 0, P) for c in range(NC)], [bt(XM[:, c, :, :]) for c in range(NC)])
                project(PB[0:32, 7, D:2 * D], [wcol("maa1", c, P, P + 32) for c in range(NC)],
                        [bt(XM[:, c, :, :]) for c in range(NC)]).then_inc(sem["xxx3"], 1)
                yield
                pe.wait_ge(sem["xxt3"], at(j, "xxt3"))
                mix(0, 1, 6)
                mix(1, 0, 7)
                yield
                pe.wait_ge(sem["t53"], at(j, "t53", 1))
                mix(2, 2, 6)
                pe.wait_ge(sem["t53"], at(j, "t53", 2))
                mix(3, 3, 7)
                yield
                pe.wait_ge(sem["t53"], at(j, "t53", 3))
                mix(4, 4, 6)
                pe.wait_ge(sem["t53"], at(j, "t53", 4))
                pe.wait_ge(sem["x53"], at(j, "x53", 1))
                project(PB[0:64, 7, 0:D], [wcol("dec1", c) for c in range(NC)], [bt(X5[:, 1, c, :, :]) for c in range(NC)]).then_inc(sem["wd3_ps"], 1)
                yield
                pe.wait_ge(sem["t53"], at(j, "t53", 5))
                pe.wait_ge(sem["wd3"], at(j, "wd3"))
                for c in range(NC):
                    last = mm(PB[:, 6, D * c:D * c + D], DEC2[:, P * c:P * c + P], WD[:, :], start=True, stop=True)
                last.then_inc(sem["w3_ps"], 1)
                pe.wait_ge(sem["x53"], at(j, "x53", 2))
                to_channels(7, "k3", X5[:, 0]).then_inc(sem["k3_ps"], 1)
                yield
                pe.wait_ge(sem["x53"], at(j, "x53", 3))
                pe.wait_ge(sem["ew3"], at(j, "ew3"))
                to_channels(6, "v3", X5[:, 2]).then_inc(sem["vt3_ps"], 1)
                pe.wait_ge(sem["k3_sb"], at(j, "k3_sb"))
                to_tokens(7, "v3", X5[:, 2]).then_inc(sem["v3_ps"], 1)
                yield
                pe.wait_ge(sem["x53"], at(j, "x53", 4))
                pe.wait_ge(sem["vt3_sb"], at(j, "vt3_sb"))
                to_channels(6, "r3", X5[:, 3]).then_inc(sem["r3_ps"], 1)
                pe.wait_ge(sem["x53"], at(j, "x53", 5))
                pe.wait_ge(sem["v3_sb"], at(j, "v3_sb"))
                to_tokens(7, "g3", X5[:, 4]).then_inc(sem["g3_ps"], 1)
                yield
                pe.wait_ge(sem["r3_sb"], at(j, "r3_sb"))
                for d in range(S3):
                    if d == 1:
                        pe.wait_ge(sem["gt3"], at(j, "gt3"))
                    if d >= 2:
                        pe.wait_ge(sem["a3"], at(j, "a3", d - 1))
                    mm(PB[:, 6 + d % 2, :], SREP[:, d, :], flat(VT3[:, :, :, :]), start=True, stop=True).then_inc(sem["vd3"], 1)
                    if d % 2:
                        yield
                pe.wait_ge(sem["a3"], at(j, "a3"))
                pe.wait_ge(sem["ruk3"], at(j, "ruk3"))
                for b in BOTH:
                    for c in range(NC):
                        mm(PB[:, 7, 32 * b + 16 * c:32 * b + 16 * c + 16], RUK[:, c, b, :], GSEL[:, :], start=True, stop=True)
                for d in range(S3):
                    pe.wait_ge(sem["pr3"], at(j, "pr3", d + 1))
                    for b in BOTH:
                        for c in range(NC):
                            at_ = D * b + P * c
                            last = mm(PB[:, 6, at_ + d:at_ + P:S3], A3[:, d, c, b, :], GSEL[:, :], start=True, stop=True)
                    if d == 3:
                        yield
                last.then_inc(sem["att3"], 1)
                yield
                pe.wait_ge(sem["att3_read"], at(j, "att3_read"))
                yield
                yield
                pe.wait_ge(sem["y3"], at(j, "y3"))
                turn_pair(6, lambda b, c: Y[:, D * b + P * c:D * b + P * c + P]).then_inc(sem["y3_t"], 1)
                yield
                pe.wait_ge(sem["yt3_sb"], at(j, "yt3_sb"))
                to_tokens(7, "o3", YT).then_inc(sem["y3_o"], 1)
                yield
                pe.wait_ge(sem["xh3"], at(j, "xh3", 2))
                turn_pair(6, lambda b, c: XH3[:, b, P * c:P * c + P]).then_inc(sem["xh3_t"], 1)
                yield
                yield
                pe.wait_ge(sem["xkr3"], at(j, "xkr3"))
                to_channels(7, "fk3", XKR[:, 0]).then_inc(sem["ff1"], 1)
                to_tokens(6, "fr3", XKR[:, 1]).then_inc(sem["ff1"], 1)
                yield
                pe.wait_ge(sem["kk3"], at(j, "kk3"))
                to_tokens(7, "fv3", KK).then_inc(sem["ff2"], 1)
                yield
                pe.wait_ge(sem["tr3"], at(j, "tr3"))
                pe.wait_ge(sem["l3_done"], at(j, "l3_done"))
                yield

            turns(pe, attention, layer3)

        @block.scalar
        def _(act):
            def copy(o, a, scale=1.0):
                return act.activation(o, a, ACT.Copy, scale=scale)

            act.wait_ge(masks_in, 48)
            act.activation(TG[:, :], GATE[:, :], ACT.Tanh).then_inc(set_act, 1)
            act.wait_ge(w_in, 16 * N_WEIGHTS)
            act.wait_ge(set_act, 1)
            act.wait_ge(set_dve, 2)

            def attention(j, first):
                own = Count(j)
                two = lambda ap: ap.rearrange("p a b -> p (a b)")

                def exp_pair(m):
                    base = AT0 if m < AT1 else AT1 if m < AT2 else AT2
                    act.wait_ge(sem["exp_scores"], at(j, "exp_scores", m + 1))
                    if m >= 4:
                        act.wait_ge(sem["pv_done"], at(j, "pv_done", m - 3))
                    elif not first:
                        act.wait_ge(sem["pv_done"], at(j - 1, "pv_done"))
                    bank, slot = 2 * ((m - base) % 2), (2 * m) % 8
                    act.activation(PROB[:, slot:slot + 2, :], PB[:, bank:bank + 2, :], ACT.Exp).then_inc(sem["exp_done"], 1)

                def keys_turned():
                    for c in BOTH:
                        n = own("kt_sb", c)
                        act.wait_ge(seq[c]["packed_t"], at(j, "packed_t", 2 * (own.given["kt_sb", c])))
                        copy(two(KT[:, c, :, :]), h16(c)).then_inc(seq[c]["kt_sb"], 1)

                def maxima_turned(layer, n):
                    act.wait_ge(sem["m_t"], at(j, "m_t", layer))
                    copy(MT[:, :, 0:n], PB[:, 4:6, :].bitcast(BF16)[:, :, 0:n]).then_inc(sem["m_sb"], 1)

                def products_out(c, m, banks):
                    act.wait_ge(sem["pv_done"], at(j, "pv_done", m))
                    copy(OTT[:, 0:4 * (banks.stop - banks.start), :].rearrange("p (b u) t -> p b (u t)", u=4),
                         PB[:, banks, :]).then_inc(seq[c]["o_raw"], 1)

                def out_turned(c, bank, k):
                    act.wait_ge(seq[c]["o_t"], at(j, "o_t", k))
                    copy(two(OT[:, c, :, :]), PB[:, bank + c, 0:D]).then_inc(seq[c]["ot_sb"], 1)

                for c in BOTH:
                    act.wait_ge(seq[c]["xc_t"], at(j, "xc_t"))
                    copy(two(CXT[:, c, :, :]), PB[:, c, :]).then_inc(seq[c]["xc_sb"], 1)
                yield
                for c in BOTH:
                    act.wait_ge(seq[c]["proj0"], at(j, "proj0"))
                    q = PB[:, 2 + c, 0:D].rearrange("p (h d) -> p h d", d=HD0)
                    k = PB[:, 2 + c, D:D + 64].rearrange("p (h d) -> p h d", d=HD0)
                    v = PB[:, 2 + c, D + 64:D + P].rearrange("p (h d) -> p h d", d=HD0)
                    copy(QN0[:, c, :, 0:16].rearrange("p h (a d) -> p h a d", a=2),
                         q[:, :, None, :].broadcast_to([P, H0, 2, HD0]), float(HD0) ** -0.5).then_inc(seq[c]["hi0"], 1)
                    copy(KN0[:, c, :, :, 0:8], k[:, :, None, :].broadcast_to([P, KV0, 4, HD0])).then_inc(seq[c]["hi0"], 1)
                    copy(KN0[:, c, :, :, 16:24], k[:, :, None, :].broadcast_to([P, KV0, 4, HD0])).then_inc(seq[c]["hi0"], 1)
                    copy(V0[:, c, :, 0:HD0], v).then_inc(seq[c]["hi0"], 1)
                yield
                keys_turned()
                yield
                yield
                yield
                maxima_turned(1, P)
                yield
                for m in range(8):
                    if m != 5:
                        exp_pair(AT0 + m)
                    if m == 4:
                        products_out(0, AT0 + 4, slice(4, 6))
                        exp_pair(AT0 + 5)
                    yield
                products_out(1, AT0 + 8, slice(4, 6))
                for c in BOTH:
                    k = PB[:, c, 0:D].rearrange("p (h d) -> p h d", d=HD1)
                    v = PB[:, c, D:2 * D].rearrange("p (h d) -> p h d", d=HD1)
                    act.wait_ge(seq[c]["kv1"], at(j, "kv1"))
                    copy(KN1[:, c, :, 0:8], k).then_inc(seq[c]["hi1"], 1)
                    copy(KN1[:, c, :, 16:24], k).then_inc(seq[c]["hi1"], 1)
                    copy(V1[:, c, :, 0:HD1], v).then_inc(seq[c]["hi1"], 1)
                    act.activation(V1[:, c, :, HD1:2 * HD1], v, ACT.Square).then_inc(seq[c]["hi1"], 1)
                    if c == 0:
                        out_turned(0, 2, 1)
                yield
                out_turned(1, 2, 1)
                yield
                yield
                for c in BOTH:
                    act.wait_ge(seq[c]["q1"], at(j, "q1"))
                    q = PB[:, 2 + c, 0:D].rearrange("p (h d) -> p h d", d=HD1)
                    copy(QN1[:, c, :, 0:16].rearrange("p h (a d) -> p h a d", a=2),
                         q[:, :, None, :].broadcast_to([P, 2 * H1, 2, HD1]), float(HD1) ** -0.5).then_inc(seq[c]["hi1q"], 1)
                for c in BOTH:
                    act.wait_ge(seq[c]["xm1"], at(j, "xm1"))
                    act.activation(XSQ[:, c, :], XM1[:, c, :], ACT.Square, accum_out=SM[:, c, 1:2]).then_inc(seq[c]["sq1"], 1)
                yield
                keys_turned()
                yield
                yield
                yield
                maxima_turned(2, D)
                yield
                for m in range(16):
                    exp_pair(AT1 + m)
                    if m == 8:
                        products_out(0, AT1 + 8, slice(4, 6))
                    if m % 2:
                        yield
                products_out(1, AT1 + 16, slice(4, 6))
                for c in BOTH:
                    act.wait_ge(seq[c]["var1"], at(j, "var1"))
                    act.activation(STD[:, c, :, :], VAR[:, c, :, :], ACT.Sqrt).then_inc(seq[c]["std1"], 1)
                for c in BOTH:
                    act.wait_ge(seq[c]["c_t"], at(j, "c_t"))
                    for n in range(NC):
                        act.activation(CT2[:, c, n, :], PB[:, 2 + c, P * n:P * n + P], ACT.Identity,
                                       bias=vec("lnb2", n), scale=vec("lng2", n)).then_inc(seq[c]["ct2_sb"], 1)
                yield
                for c in BOTH:
                    act.wait_ge(seq[c]["x2_t"], at(j, "x2_t"))
                    copy(two(X2T[:, c, :, :]), PB[:, 2 + c, D:2 * D]).then_inc(seq[c]["x2_sb"], 1)
                yield
                for c in BOTH:
                    act.wait_ge(seq[c]["proj2"], at(j, "proj2"))
                    q = PB[:, 2 + c, 0:D].rearrange("p (h d) -> p h d", d=HD2)
                    k = PB[:, c, 0:D].rearrange("p (h d) -> p h d", d=HD2)
                    v = PB[:, c, D:2 * D].rearrange("p (h d) -> p h d", d=HD2)
                    copy(QN2[:, c, :, 0:32].rearrange("p h (a d) -> p h a d", a=2),
                         q[:, :, None, :].broadcast_to([P, H2, 2, HD2]), float(HD2) ** -0.5).then_inc(seq[c]["hi2"], 1)
                    copy(KN2[:, c, :, 0:16], k).then_inc(seq[c]["hi2"], 1)
                    copy(KN2[:, c, :, 32:48], k).then_inc(seq[c]["hi2"], 1)
                    copy(V2[:, c, :, 0:HD2], v).then_inc(seq[c]["hi2"], 1)
                yield
                keys_turned()
                yield
                yield
                yield
                maxima_turned(3, P)
                yield
                for m in range(4):
                    exp_pair(AT2 + m)
                    yield
                act.wait_ge(seq[1]["o_back"], at(j, "o_back", 2))
                for c in BOTH:
                    act.wait_ge(sem["pv_done"], at(j, "pv_done", AT2 + 2 * c + 2))
                    copy(OTT[:, 4 * c:4 * c + 4, :].rearrange("p u t -> p (u t)"), PB[:, 4 + c, :]).then_inc(seq[c]["o_raw"], 1)
                yield
                for c in BOTH:
                    out_turned(c, 4, 2)
                yield
                yield

            def layer3(j, first):
                flat = lambda ap: ap.rearrange("p c b t -> p (c b t)")

                def affine(k, w, b):
                    act.wait_ge(sem["xh3_t"], at(j, "xh3_t", k))
                    for c in range(NC):
                        act.activation(XNT[:, c, :, 1:P + 1], PB[:, 6, D * c:D * c + D].rearrange("p (b t) -> p b t", b=2), ACT.Identity,
                                       bias=vec(b, c), scale=vec(w, c)).then_inc(sem["xnt3"], 1)

                affine(1, "ln1w", "ln1b")
                yield
                act.wait_ge(sem["xxx3"], at(j, "xxx3"))
                act.activation(XXT[:, :], PB[:, 7, 0:D], ACT.Tanh).then_inc(sem["xxt3"], 1)
                act.activation(XXT4[:, :], PB[0:32, 7, D:2 * D], ACT.Tanh).then_inc(sem["xxt3"], 1)
                yield
                yield
                yield
                act.wait_ge(sem["wd3_ps"], at(j, "wd3_ps"))
                act.activation(WD[:, :], PB[0:64, 7, 0:D], ACT.Tanh).then_inc(sem["wd3"], 1)
                yield
                act.wait_ge(sem["w3_ps"], at(j, "w3_ps"))
                act.activation(EW[:, 0, :, :].rearrange("p b t -> p (b t)"), PB[:, 6, 0:D], ACT.Exp, bias=vec("td", 0)).then_inc(sem["act3"], 1)
                act.activation(EW[:, 1, :, :].rearrange("p b t -> p (b t)"), PB[:, 6, D:2 * D], ACT.Exp, bias=vec("td", 1)).then_inc(sem["ew3"], 1)
                act.wait_ge(sem["act3"], at(j, "act3", 1))
                act.wait_ge(sem["ew3"], at(j, "ew3"))
                act.activation(WS[:, :, :, 1:P].rearrange("p c b t -> p (c b) t"), EW[:, :, :, 0:P - 1].rearrange("p c b t -> p (c b) t"),
                               ACT.Exp, scale=-1.0).then_inc(sem["ws3"], 1)
                act.wait_ge(sem["k3_ps"], at(j, "k3_ps"))
                copy(flat(KS[:, :, :, :]), PB[:, 7, :]).then_inc(sem["k3_sb"], 1)
                yield
                act.wait_ge(sem["vt3_ps"], at(j, "vt3_ps"))
                copy(flat(VT3[:, :, :, :]), PB[:, 6, :]).then_inc(sem["vt3_sb"], 1)
                act.wait_ge(sem["v3_ps"], at(j, "v3_ps"))
                copy(VN3[:, :], PB[:, 7, :]).then_inc(sem["v3_sb"], 1)
                yield
                act.wait_ge(sem["r3_ps"], at(j, "r3_ps"))
                copy(flat(RR[:, :, :, :]), PB[:, 6, :]).then_inc(sem["r3_sb"], 1)
                act.wait_ge(sem["g3_ps"], at(j, "g3_ps"))
                act.activation(GT[:, :], PB[:, 7, :], ACT.Tanh, scale=0.5).then_inc(sem["g3_sb"], 1)
                yield
                yield
                yield
                yield
                yield
                yield
                yield
                act.wait_ge(sem["d83"], at(j, "d83"))
                act.activation(SQ[:, :], DD[:, :], ACT.Square).then_inc(sem["sq3"], 1)
                yield
                yield
                act.wait_ge(sem["y3_t"], at(j, "y3_t"))
                copy(flat(YT[:, :, :, :]), PB[:, 6, :]).then_inc(sem["yt3_sb"], 1)
                yield
                yield
                affine(2, "ln2w", "ln2b")
                yield
                yield
                act.wait_ge(sem["ff1"], at(j, "ff1", 1))
                act.activation(flat(KKR[:, :, :, :]), PB[:, 7, :], ACT.Relu).then_inc(sem["act3"], 1)
                act.wait_ge(sem["act3"], at(j, "act3", 2))
                act.activation(KK[:, :, :, :], KKR[:, :, :, :], ACT.Square).then_inc(sem["kk3"], 1)
                act.wait_ge(sem["ff1"], at(j, "ff1", 2))
                act.activation(TR[:, :], PB[:, 6, :], ACT.Tanh, scale=0.5).then_inc(sem["tr3"], 1)
                yield
                yield
                act.wait_ge(sem["l3_done"], at(j, "l3_done"))
                act.activation(IDLE[:, 0:1], TG[:, :], ACT.Copy).then_inc(sem["act3"], 1)
                act.wait_ge(sem["act3"], at(j, "act3", 3))
                yield

            turns(act, attention, layer3)

        @block.gpsimd
        def _(pool):
            tt = pool.tensor_tensor
            pool.wait_ge(set_dve, 2)
            SPARE = IDLE[:, 1:2]

            def apart():
                tt(SPARE, NHALF[:, 0:1], NHALF[:, 1:2], ALU.add)

            def attention(j, first):
                own = Count(j)

                def rsqrt(c, k, eps):
                    pool.wait_ge(seq[c]["var_in"], at(j, "var_in", k))
                    apart()
                    pool.tensor_scalar(VE[:, c:c + 1], MV[:, c, 1:2], 1.0, eps, ALU.mult, ALU.add).then_inc(seq[c]["pool"], 1)
                    pool.wait_ge(seq[c]["pool"], own("pool", c))
                    tt(RSTD[:, c:c + 1], VE[:, c:c + 1], NHALF[:, 0:1], ALU.pow).then_inc(seq[c]["rstd"], 1)

                pool.wait_ge(sem["m0_in"], at(j, "m0_in"))
                apart()
                pool.tensor_copy(MP[:, 0, :, :], M0[:, :, :]).then_inc(sem["mask_pool"], 1)
                pool.wait_ge(sem["mask_pool"], own("mask_pool"))
                tt(MR[:, :, :], M0[:, :, :], MP[:, 0, :, :], ALU.subtract).then_inc(sem["mask_pool"], 1)
                pool.wait_ge(sem["mask_pool"], own("mask_pool"))
                apart()
                pool.tensor_copy(MP[:, 1, :, :], MR[:, :, :]).then_inc(sem["mask_pool"], 1)
                pool.wait_ge(sem["mask_pool"], own("mask_pool"))
                tt(MR[:, :, :], MR[:, :, :], MP[:, 1, :, :], ALU.subtract).then_inc(sem["mask_pool"], 1)
                pool.wait_ge(sem["mask_pool"], own("mask_pool"))
                apart()
                pool.tensor_copy(MP[:, 2, :, :], MR[:, :, :]).then_inc(sem["mask_parts"], 1)
                for _ in range(6):
                    yield
                for m in range(8):
                    yield
                rsqrt(0, 1, 1e-6)
                yield
                yield
                rsqrt(1, 1, 1e-6)
                yield
                yield
                for c in BOTH:
                    pool.wait_ge(seq[c]["sq1"], at(j, "sq1"))
                    tt(SM[:, c, 3:4], SM[:, c, 0:1], SM[:, c, 2:3], ALU.mult).then_inc(seq[c]["pool"], 1)
                    pool.wait_ge(seq[c]["pool"], own("pool", c))
                    tt(SM[:, c, 4:5], SM[:, c, 1:2], SM[:, c, 2:3], ALU.mult)
                    tt(SM[:, c, 5:6], SM[:, c, 3:4], SM[:, c, 3:4], ALU.mult).then_inc(seq[c]["pool"], 1)
                    pool.wait_ge(seq[c]["pool"], own("pool", c))
                    tt(SM[:, c, 6:7], SM[:, c, 4:5], SM[:, c, 5:6], ALU.subtract).then_inc(seq[c]["pool"], 1)
                    pool.wait_ge(seq[c]["pool"], own("pool", c))
                    apart()
                    pool.tensor_scalar(SM[:, c, 7:8], SM[:, c, 6:7], 0.0, 1e-5, ALU.max, ALU.add).then_inc(seq[c]["pool"], 1)
                    pool.wait_ge(seq[c]["pool"], own("pool", c))
                    tt(SM[:, c, 4:5], SM[:, c, 7:8], NHALF[:, 0:1], ALU.pow).then_inc(seq[c]["pool"], 1)
                    pool.wait_ge(seq[c]["pool"], own("pool", c))
                    apart()
                    pool.tensor_scalar(XN1[:, c, :], XM1[:, c, :], SM[:, c, 3:4], SM[:, c, 4:5], ALU.subtract, ALU.mult).then_inc(seq[c]["pool"], 1)
                    pool.wait_ge(seq[c]["pool"], own("pool", c))
                    tt(XN1[:, c, :], XN1[:, c, :], MXF[:, c, :], ALU.mult).then_inc(seq[c]["xn1"], 1)
                for c in BOTH:
                    rsqrt(c, 2, 1e-5)
                own.end()
                for _ in range(44 - 18):
                    yield

            def layer3(j, first):
                def rsqrt3(k, eps, n, scale, src, dst):
                    pool.wait_ge(sem["var3"], at(j, "var3", k))
                    apart()
                    pool.tensor_scalar(VE3[:, 0:n], src, scale, eps, ALU.mult, ALU.add).then_inc(sem["pool3"], 1)
                    pool.wait_ge(sem["pool3"], at(j, "pool3", k))
                    tt(dst, VE3[:, 0:n], NHALF[:, 0:n], ALU.pow).then_inc(sem["rstd3"], 1)

                rsqrt3(1, 1e-5, 2, 1.0, MV3[:, :, 1], RSTD3[:, :])
                yield
                yield
                yield
                for k, n in enumerate((1, 0, 2, 3, 4)):
                    pool.wait_ge(sem["t53"], at(j, "t53", k + 1))
                    tt(X5[:, n].rearrange("p c b t -> p (c b) t"), T5[:, k % 2].rearrange("p c b t -> p (c b) t"),
                       XNT[:, :, :, 1:P + 1].rearrange("p c b t -> p (c b) t"), ALU.add).then_inc(sem["x53"], 1)
                    if k in (1, 3):
                        yield
                yield
                yield
                yield
                yield
                for d in range(S3):
                    pool.wait_ge(sem["sc3"], at(j, "sc3", d + 1))
                    tt(A3[:, d], A3[:, d], RR[:, :, :, :], ALU.mult).then_inc(sem["pr3"], 1)
                    if d % 2:
                        yield
                yield
                yield
                yield
                rsqrt3(2, 1e-5, 64, 1.0 / S3, G8[:, 1, :], G8[:, 2, :])
                yield
                yield
                rsqrt3(3, 1e-5, 2, 1.0, MV3[:, :, 1], RSTD3[:, :])
                yield
                yield
                yield
                yield
                yield

            turns(pool, attention, layer3)

        @block.vector
        def _(dve):
            stt, tt, ts = dve.scalar_tensor_tensor, dve.tensor_tensor, dve.tensor_scalar
            for tile in (QN0, KN0, QN2, KN2, WS, MN, V0, V1, V2):
                dve.memset(tile[:], 0.0)
            dve.memset(ONES[:, :], 1.0)
            dve.memset(NHALF[:, :], -0.5)
            dve.wait_ge(masks_in, 48)
            ts(MF[:, 0:2 * P], MRAW1[:, :], 1.0, NEG, ALU.subtract, ALU.mult)
            ts(MF[:, 2 * P:3 * P], MRAW2[:, :], 1.0, NEG, ALU.subtract, ALU.mult).then_inc(set_dve, 1)
            dve.wait_ge(set_dve, 1)
            dve.memset(V0[:, :, :, HD0:HD0 + 1], 1.0)
            dve.memset(V1[:, :, :, 2 * HD1:2 * HD1 + 1], 1.0)
            dve.memset(V2[:, :, :, HD2:HD2 + 1], 1.0)
            dve.memset(QN1[:, :, :, 24:25], NEG)
            dve.memset(QN2[:, :, :, 48:49], NEG)
            dve.wait_ge(set_pe, 1)
            dve.tensor_copy(KM1[:, :, :].rearrange("p b a -> p a b"), h16(0)[:, 0:32].rearrange("p (a b) -> p a b", a=2)).then_inc(masks_in, 16)
            dve.tensor_copy(KM2[:, :, 0], h16(0)[:, 32:48]).then_inc(set_dve, 1)
            dve.wait_ge(masks_in, 64)
            dve.wait_ge(set_dve, 2)
            dve.wait_ge(w_in, 16 * N_WEIGHTS)
            dve.wait_ge(set_act, 1)
            km1 = KM1[:, :, :].rearrange("p (j c) a -> p j c a", c=2)
            km2 = KM2[:, :, :].rearrange("p (j c) a -> p j (c a)", c=2)

            def attention(j, first):
                own = Count(j)
                two = lambda ap: ap.rearrange("p a b -> p (a b)")

                def max_pair(m, dst, width):
                    base = AT0 if m < AT1 else AT1 if m < AT2 else AT2
                    dve.wait_ge(sem["max_scores"], at(j, "max_scores", m + 1))
                    bank = 2 * ((m - base) % 2)
                    dve.tensor_reduce(dst, PB[:, bank:bank + 2, :].rearrange("p b (h s) -> p (b h) s", s=width),
                                      X_AXIS, ALU.max, negate=True).then_inc(sem["max_read"], 1)

                def split_maxima(base, n_pairs, nm, nr, part):
                    dve.wait_ge(sem["max_read"], at(j, "max_read", base + 2 * n_pairs))
                    dve.tensor_copy(part(0), nm).then_inc(sem["m_split"], 1)
                    dve.wait_ge(sem["m_split"], own("m_split"))
                    tt(nr, nm, part(0), ALU.subtract).then_inc(sem["m_split"], 1)
                    dve.wait_ge(sem["m_split"], own("m_split"))
                    dve.tensor_copy(part(1), nr).then_inc(sem["m_split"], 1)
                    dve.wait_ge(sem["m_split"], own("m_split"))
                    tt(part(2), nr, part(1), ALU.subtract).then_inc(sem["nm"], 1)

                def queries_turned():
                    for c in BOTH:
                        own("qt_sb", c)
                        dve.wait_ge(seq[c]["packed_t"], at(j, "packed_t", 2 * own.given["qt_sb", c] - 1))
                        dve.tensor_copy(two(QT[:, c, :, :]), h16(2 + c)).then_inc(seq[c]["qt_sb"], 1)

                def normalise(c, banks, heads, hd, layer):
                    dve.wait_ge(seq[c]["o_back"], at(j, "o_back", layer))
                    o = PB[:, banks, :].rearrange("p a (h d) -> p (a h) d", d=VB)
                    dve.reciprocal(RS[:, c, 0:heads], o[:, :, hd]).then_inc(seq[c]["dve"], 1)
                    dve.wait_ge(seq[c]["dve"], own("dve", c))
                    tt(ON[:, c, :].rearrange("p (h d) -> p h d", d=hd), o[:, :, 0:hd],
                       RS[:, c, 0:heads, None].broadcast_to([P, heads, hd]), ALU.mult).then_inc(seq[c]["o_norm"], 1)

                def add_norm0(c):
                    dve.wait_ge(seq[c]["res"], at(j, "res", 1))
                    tt(XH[:, c, :], PB[:, 2 + c, D:2 * D], X[:, c, :], ALU.add).then_inc(seq[c]["dve"], 1)
                    dve.wait_ge(seq[c]["dve"], own("dve", c))
                    stats(c, XH[:, c, :])

                def stats(c, src):
                    dve.bn_stats(ST[:, c, :], src).then_inc(seq[c]["dve"], 1)
                    dve.wait_ge(seq[c]["dve"], own("dve", c))
                    dve.memset(IDLE_DVE[:, 0:1], 0.0)
                    dve.bn_aggr(MV[:, c, :], ST[:, c, :]).then_inc(seq[c]["var_in"], 1)

                def apply_norm0(c):
                    dve.wait_ge(seq[c]["rstd"], at(j, "rstd", 1))
                    ts(XH[:, c, :], XH[:, c, :], MV[:, c, 0:1], RSTD[:, c:c + 1], ALU.subtract, ALU.mult).then_inc(seq[c]["dve"], 1)
                    dve.wait_ge(seq[c]["dve"], own("dve", c))
                    tt(XH[:, c, :], XH[:, c, :], BCR[:, BC["gamma0"], :], ALU.mult).then_inc(seq[c]["dve"], 1)
                    dve.wait_ge(seq[c]["dve"], own("dve", c))
                    tt(X1[:, c, :], XH[:, c, :], BCR[:, BC["beta0"], :], ALU.add).then_inc(seq[c]["x1"], 1)

                yield
                for c in BOTH:
                    dve.wait_ge(seq[c]["hi0"], at(j, "hi0"))
                    q = PB[:, 2 + c, 0:D].rearrange("p (h d) -> p h d", d=HD0)
                    k = PB[:, 2 + c, D:D + 64].rearrange("p (h d) -> p h d", d=HD0)
                    stt(QN0[:, c, :, 16:24], q, float(HD0) ** -0.5, QN0[:, c, :, 0:8], ALU.mult, ALU.subtract).then_inc(seq[c]["lo0"], 1)
                    tt(KN0[:, c, :, :, 8:16], k[:, :, None, :].broadcast_to([P, KV0, 4, HD0]), KN0[:, c, :, :, 0:8],
                       ALU.subtract).then_inc(seq[c]["lo0"], 1)
                if not first:
                    dve.wait_ge(sem["x3_free"], at(j - 1, "x3_free"))
                dve.tensor_copy(STC[:, :, :, :], CXT[:, :, 0:NC, 0:2]).then_inc(sem["st_cols"], 1)
                yield
                queries_turned()
                yield
                for c in BOTH:
                    for n in range(4):
                        max_pair(4 * c + n, NM[:, c, 8 * n:8 * n + 8], P)
                    yield
                split_maxima(AT0, 4, NM[:, :, :], NR[:, :, :], lambda k: MN[:, :, 0, 32 * k:32 * k + 32])
                dve.wait_ge(sem["mx_in"], at(j, "mx_in"))
                dve.tensor_copy(MXF[:, :, :], MXR[:, :, :]).then_inc(sem["mx_step"], 1)
                for c in BOTH:
                    dve.tensor_copy(KN1[:, c, :, 24].rearrange("p (a h) -> p a h", a=2),
                                    km1[:, j, c, :][:, :, None].broadcast_to([P, 2, H1])).then_inc(seq[c]["lo1"], 1)
                    dve.tensor_copy(KN2[:, c, :, 48], km2[:, j, c:c + 1].broadcast_to([P, H2])).then_inc(seq[c]["lo2"], 1)
                dve.wait_ge(sem["mx_step"], own("mx_step"))
                dve.tensor_reduce(SM[:, :, 2], MXF[:, :, :], X_AXIS, ALU.add).then_inc(sem["mx_step"], 1)
                dve.wait_ge(sem["mx_step"], own("mx_step"))
                dve.reciprocal(SM[:, :, 2], SM[:, :, 2]).then_inc(sem["mx_step"], 1)
                dve.wait_ge(sem["mx_step"], own("mx_step"))
                yield
                for m in range(8):
                    if m == 4:
                        normalise(0, slice(4, 6), H0, HD0, 1)
                    yield
                normalise(1, slice(4, 6), H0, HD0, 1)
                for c in BOTH:
                    dve.wait_ge(seq[c]["hi1"], at(j, "hi1"))
                    k = PB[:, c, 0:D].rearrange("p (h d) -> p h d", d=HD1)
                    tt(KN1[:, c, :, 8:16], k, KN1[:, c, :, 0:8], ALU.subtract).then_inc(seq[c]["lo1"], 1)
                add_norm0(0)
                yield
                apply_norm0(0)
                yield
                add_norm0(1)
                yield
                apply_norm0(1)
                for c in BOTH:
                    dve.wait_ge(seq[c]["x1"], at(j, "x1"))
                    tt(XM1[:, c, :], X1[:, c, :], MXF[:, c, :], ALU.mult).then_inc(seq[c]["dve"], 1)
                for c in BOTH:
                    dve.wait_ge(seq[c]["dve"], own("dve", c))
                    dve.tensor_reduce(SM[:, c, 0:1], XM1[:, c, :], X_AXIS, ALU.add).then_inc(seq[c]["xm1"], 1)
                for c in BOTH:
                    dve.wait_ge(seq[c]["hi1q"], at(j, "hi1q"))
                    q = PB[:, 2 + c, 0:D].rearrange("p (h d) -> p h d", d=HD1)
                    stt(QN1[:, c, :, 16:24], q, float(HD1) ** -0.5, QN1[:, c, :, 0:8], ALU.mult, ALU.subtract).then_inc(seq[c]["lo1"], 1)
                yield
                queries_turned()
                for c in BOTH:
                    dve.wait_ge(seq[c]["x1"], at(j, "x1"))
                    stats(c, C[:, c, :])
                yield
                for c in BOTH:
                    for n in range(8):
                        max_pair(AT1 + 8 * c + n, NM[:, c, 4 * n:4 * n + 4], D)
                    yield
                split_maxima(AT1, 8, NM[:, :, :].rearrange("p c (a h) -> p c a h", a=2), NR[:, :, :].rearrange("p c (a h) -> p c a h", a=2),
                             lambda k: MN[:, :, :, 16 * k:16 * k + 16])
                yield

                def moments(c):
                    dve.wait_ge(seq[c]["o_back"], at(j, "o_back", 2))
                    o = PB[:, 4:6, :].rearrange("p a (h d) -> p a h d", d=VB)
                    rs = RS[:, c, :].rearrange("p (a h) -> p a h", a=2)
                    rsb = rs[:, :, :, None].broadcast_to([P, 2, H1, HD1])
                    v4 = lambda tile: tile[:, c, :, :].rearrange("p a (h d) -> p a h d", d=HD1)
                    v2 = lambda tile: tile[:, c, :, :].rearrange("p a b -> p (a b)")
                    dve.reciprocal(rs, o[:, :, :, 16]).then_inc(seq[c]["dve"], 1)
                    dve.wait_ge(seq[c]["dve"], own("dve", c))
                    tt(v4(MEAN), o[:, :, :, 0:8], rsb, ALU.mult).then_inc(seq[c]["dve"], 1)
                    tt(v4(EX2), o[:, :, :, 8:16], rsb, ALU.mult).then_inc(seq[c]["o_norm"], 1)
                    dve.wait_ge(seq[c]["dve"], own("dve", c))
                    tt(v2(VAR), v2(MEAN), v2(MEAN), ALU.mult).then_inc(seq[c]["dve"], 1)
                    dve.wait_ge(seq[c]["dve"], own("dve", c))
                    dve.wait_ge(seq[c]["o_norm"], at(j, "o_norm", 2))
                    tt(v2(VAR), v2(EX2), v2(VAR), ALU.subtract).then_inc(seq[c]["dve"], 1)
                    dve.wait_ge(seq[c]["dve"], own("dve", c))
                    ts(v2(VAR), v2(VAR), 0.0, None, ALU.max).then_inc(seq[c]["var1"], 1)

                for m in range(16):
                    if m == 2:
                        for c in BOTH:
                            dve.wait_ge(seq[c]["rstd"], at(j, "rstd", 2))
                            ts(CH[:, c, :], C[:, c, :], MV[:, c, 0:1], RSTD[:, c:c + 1], ALU.subtract, ALU.mult).then_inc(seq[c]["c_hat"], 1)
                    if m == 8:
                        moments(0)
                    if m % 2:
                        yield
                moments(1)
                for c in BOTH:
                    dve.wait_ge(seq[c]["ms_t"], at(j, "ms_t"))
                    dve.wait_ge(seq[c]["xn1"], at(j, "xn1"))
                    tt(X2[:, c, :], XN1[:, c, :], PB[:, c, D:2 * D], ALU.mult).then_inc(seq[c]["dve"], 1)
                for c in BOTH:
                    dve.wait_ge(seq[c]["dve"], own("dve", c))
                    tt(X2[:, c, :], X2[:, c, :], PB[:, c, 0:D], ALU.add).then_inc(seq[c]["dve"], 1)
                for c in BOTH:
                    dve.wait_ge(seq[c]["dve"], own("dve", c))
                    tt(X2[:, c, :], X2[:, c, :], MXF[:, c, :], ALU.mult).then_inc(seq[c]["x2"], 1)
                yield
                yield
                for c in BOTH:
                    dve.wait_ge(seq[c]["hi2"], at(j, "hi2"))
                    q = PB[:, 2 + c, 0:D].rearrange("p (h d) -> p h d", d=HD2)
                    k = PB[:, c, 0:D].rearrange("p (h d) -> p h d", d=HD2)
                    stt(QN2[:, c, :, 32:48], q, float(HD2) ** -0.5, QN2[:, c, :, 0:16], ALU.mult, ALU.subtract).then_inc(seq[c]["lo2"], 1)
                    tt(KN2[:, c, :, 16:32], k, KN2[:, c, :, 0:16], ALU.subtract).then_inc(seq[c]["lo2"], 1)
                yield
                queries_turned()
                yield
                for c in BOTH:
                    for r in range(2):
                        max_pair(AT2 + 2 * c + r, NM[:, c, 8 * r:8 * r + 8], P)
                    yield
                split_maxima(AT2, 2, NM[:, :, 0:16], NR[:, :, 0:16], lambda k: MN[:, :, 0, 16 * k:16 * k + 16])
                yield
                for m in range(4):
                    yield
                for c in BOTH:
                    normalise(c, slice(4 + c, 5 + c), H2, HD2, 3)
                yield
                yield
                if not first:
                    dve.wait_ge(sem["x3_free"], at(j - 1, "x3_free"))
                for c in BOTH:
                    dve.wait_ge(seq[c]["res"], at(j, "res", 2))
                    stt(X3[:, c, :], PB[:, 4 + c, D:2 * D], TG[:, 0:1], X2[:, c, :], ALU.mult, ALU.add).then_inc(seq[c]["x3"], 1)
                own.end()
                yield

            def layer3(j, first):
                own = Count(j)

                def stats3(src):
                    for b in BOTH:
                        last = dve.bn_stats(ST3[:, b, :], src[:, b, :])
                    last.then_inc(sem["dve3"], 1)
                    dve.wait_ge(sem["dve3"], own("dve3"))
                    dve.memset(IDLE_DVE[:, 0:1], 0.0)
                    for b in BOTH:
                        last = dve.bn_aggr(MV3[:, b, :], ST3[:, b, :])
                    last.then_inc(sem["var3"], 1)

                def norm3(src, k):
                    dve.wait_ge(sem["rstd3"], at(j, "rstd3", k))
                    for b in BOTH:
                        last = ts(XH3[:, b, :], src[:, b, :], MV3[:, b, 0:1], RSTD3[:, b:b + 1], ALU.subtract, ALU.mult)
                    last.then_inc(sem["xh3"], 1)

                def shift(col, k):
                    dve.tensor_copy(XNT[:, :, :, 0], STC3[:, :, :, col].rearrange("p b c -> p c b")).then_inc(sem["dve3"], 1)
                    dve.wait_ge(sem["dve3"], own("dve3"))
                    dve.wait_ge(sem["xnt3"], at(j, "xnt3", k))
                    tt(SX[:, :, :, :].rearrange("p c b t -> p (c b) t"), XNT[:, :, :, 0:P].rearrange("p c b t -> p (c b) t"),
                       XNT[:, :, :, 1:P + 1].rearrange("p c b t -> p (c b) t"), ALU.subtract).then_inc(sem["dve3"], 1)
                    dve.wait_ge(sem["dve3"], own("dve3"))

                for b in BOTH:
                    dve.wait_ge(seq[b]["x3"], at(j, "x3"))
                dve.tensor_copy(X3L[:, :, :], X3[:, :, :]).then_inc(sem["dve3"], 1)
                dve.wait_ge(sem["dve3"], own("dve3"))
                dve.wait_ge(sem["st_cols"], at(j, "st_cols"))
                dve.tensor_copy(STC3[:, :, :, :], STC[:, :, :, :]).then_inc(sem["x3_free"], 1)
                stats3(X3L)
                norm3(X3L, 1)
                dve.wait_ge(sem["x3_free"], at(j, "x3_free"))
                shift(1, 2)
                for c in range(NC):
                    last = stt(XM[:, c], SX[:, c], vec("maax", c), XNT[:, c, :, 1:P + 1], ALU.mult, ALU.add)
                last.then_inc(sem["xm3"], 1)
                yield
                yield
                for k, n in enumerate((1, 0, 2, 3, 4)):
                    dve.wait_ge(sem["mix3"], at(j, "mix3", k + 1))
                    if k >= 2:
                        dve.wait_ge(sem["x53"], at(j, "x53", k - 1))
                    for c in range(NC):
                        last = stt(T5[:, k % 2, c].rearrange("p b t -> p (b t)"), PB[:, 6 + k % 2, D * c:D * c + D], vec(f"st{n}", c),
                                   SX[:, c].rearrange("p b t -> p (b t)"), ALU.add, ALU.mult)
                    last.then_inc(sem["t53"], 1)
                    if k in (1, 3):
                        yield
                yield
                yield
                yield
                dve.wait_ge(sem["g3_sb"], at(j, "g3_sb"))
                stt(GT[:, :], GT[:, :], 1.0, PB[:, 7, :], ALU.add, ALU.mult).then_inc(sem["gt3"], 1)
                dve.wait_ge(sem["r3_sb"], at(j, "r3_sb"))
                for c in range(NC):
                    last = stt(RUK[:, c], RR[:, c], vec("u", c), KS[:, c], ALU.mult, ALU.mult)
                last.then_inc(sem["ruk3"], 1)
                dve.wait_ge(sem["s0_in"], at(j, "s0_in"))
                for b in BOTH:
                    last = dve.tensor_copy(A3[:, :, :, b, 0], S0[:, b, :, :].rearrange("p c d -> p d c"))
                last.then_inc(sem["s0_read"], 1)
                yield
                dve.wait_ge(sem["ws3"], at(j, "ws3"))
                dve.wait_ge(sem["s0_read"], at(j, "s0_read"))
                for d in range(S3):
                    dve.wait_ge(sem["vd3"], at(j, "vd3", d + 1))
                    vd = PB[:, 6 + d % 2, :].rearrange("p (n t) -> p n t", t=P)
                    tt(A3[:, d, :, :, 1:P].rearrange("p c b t -> p (c b) t"), vd[:, :, 0:P - 1],
                       KS[:, :, :, 0:P - 1].rearrange("p c b t -> p (c b) t"), ALU.mult).then_inc(sem["a3"], 1)
                    dve.wait_ge(sem["a3"], own("a3"))
                    dve.tensor_tensor_scan(A3[:, d].rearrange("p c b t -> p (c b t)"), WS[:, :, :, :].rearrange("p c b t -> p (c b t)"),
                                           A3[:, d].rearrange("p c b t -> p (c b t)"), 0.0, ALU.mult, ALU.add).then_inc(sem["sc3"], 1)
                    if d % 2:
                        yield
                yield
                h3 = lambda ap: ap.rearrange("p (h d) -> p h d", d=S3)
                b8 = lambda ap: ap[:, :, None].broadcast_to([P, 2 * H3, S3])
                dve.wait_ge(sem["att3"], at(j, "att3"))
                tt(h3(ATT[:, :]), h3(VN3[:, :]), b8(PB[:, 7, 0:2 * H3]), ALU.mult).then_inc(sem["dve3"], 1)
                dve.wait_ge(sem["dve3"], own("dve3"))
                tt(ATT[:, :], ATT[:, :], PB[:, 6, :], ALU.add).then_inc(sem["att3_read"], 1)
                dve.wait_ge(sem["att3_read"], at(j, "att3_read"))
                dve.tensor_reduce(G8[:, 0, :], h3(ATT[:, :]), X_AXIS, ALU.add).then_inc(sem["dve3"], 1)
                dve.wait_ge(sem["dve3"], own("dve3"))
                ts(G8[:, 0, :], G8[:, 0, :], 1.0 / S3, None, ALU.mult).then_inc(sem["dve3"], 1)
                dve.wait_ge(sem["dve3"], own("dve3"))
                tt(h3(DD[:, :]), h3(ATT[:, :]), b8(G8[:, 0, :]), ALU.subtract).then_inc(sem["d83"], 1)
                yield
                yield
                dve.wait_ge(sem["sq3"], at(j, "sq3"))
                dve.tensor_reduce(G8[:, 1, :], h3(SQ[:, :]), X_AXIS, ALU.add).then_inc(sem["var3"], 1)
                yield
                dve.wait_ge(sem["rstd3"], at(j, "rstd3", 2))
                tt(h3(Y[:, :]), h3(DD[:, :]), b8(G8[:, 2, :]), ALU.mult).then_inc(sem["dve3"], 1)
                dve.wait_ge(sem["dve3"], own("dve3"))
                y2 = Y[:, :].rearrange("p (b d) -> p b d", b=2)
                tt(y2, y2, BCR[:, BC["gnw"]:BC["gnw"] + 1, :].broadcast_to([P, 2, D]), ALU.mult).then_inc(sem["dve3"], 1)
                dve.wait_ge(sem["dve3"], own("dve3"))
                tt(y2, y2, BCR[:, BC["gnb"]:BC["gnb"] + 1, :].broadcast_to([P, 2, D]), ALU.add).then_inc(sem["dve3"], 1)
                dve.wait_ge(sem["dve3"], own("dve3"))
                stt(Y[:, :], Y[:, :], 0.5, GT[:, :], ALU.mult, ALU.mult).then_inc(sem["y3"], 1)
                yield
                yield
                dve.wait_ge(sem["y3_o"], at(j, "y3_o"))
                tt(X4[:, :, :], PB[:, 7, :].rearrange("p (b d) -> p b d", b=2), X3L[:, :, :], ALU.add).then_inc(sem["dve3"], 1)
                dve.wait_ge(sem["dve3"], own("dve3"))
                stats3(X4)
                norm3(X4, 3)
                yield
                shift(0, 4)
                for n, name in enumerate(("fmk", "fmr")):
                    for c in range(NC):
                        stt(XKR[:, n, c], SX[:, c], vec(name, c), XNT[:, c, :, 1:P + 1], ALU.mult, ALU.add).then_inc(sem["xkr3"], 1)
                yield
                yield
                dve.wait_ge(sem["ff2"], at(j, "ff2"))
                dve.wait_ge(sem["tr3"], at(j, "tr3"))
                stt(TR[:, :], TR[:, :], 1.0, PB[:, 7, :], ALU.add, ALU.mult).then_inc(sem["dve3"], 1)
                dve.wait_ge(sem["dve3"], own("dve3"))
                dve.wait_ge(sem["out_stored"], at(j, "out_stored"))
                stt(OUT[:, :, :], TR[:, :].rearrange("p (b d) -> p b d", b=2), 0.5, X4[:, :, :], ALU.mult, ALU.add).then_inc(sem["l3_done"], 1)
                own.end()
                yield
                yield

            turns(dve, attention, layer3)


def kernel(**inputs):
    import numpy as np
    import ml_dtypes
    import concourse.bacc as bacc
    from concourse.bass_utils import run_bass_kernel_spmd as run

    a = {k: np.asarray(v) for k, v in inputs.items()}
    L0, L1, L2, L3 = (lambda n, p=f"L{k}_xattn_": a[p + n] for k in range(4))
    cat = np.concatenate
    wo0 = L0("Wo").reshape(2, 4, 4, HD0, D).transpose(0, 2, 1, 3, 4).reshape(D, D)
    wo2 = L2("Wo").T.reshape(2, 4, 2, HD2, D).transpose(2, 0, 1, 3, 4).reshape(D, D)
    wall = cat([L0("Wq"), L0("Wk"), L0("Wv"), wo0, L2("Wk").T, L2("Wv").T, L2("Wq").T, wo2,
                L3("maa_w1"), L3("decay_w1"), L3("Wr").T, L3("Wk").T, L3("Wv").T, L3("Wg").T, L3("Wo").T,
                L3("ffn_Wk").T, L3("ffn_Wr").T, L3("ffn_Wv").T], axis=1)
    w1 = cat([L1("Wq").T, L1("Wk").T, L1("Wv").T], axis=1)
    rows = cat([L0("bq"), L0("bk"), L0("bv"), L0("bo"), L1("bq"), L1("bk"), L1("bv")]).reshape(1, -1)
    bcast = cat([L0("gamma"), L0("beta"), L3("gn_w"), L3("gn_b")]).reshape(1, -1)
    st = L3("maa_stack")
    cols = np.stack([L2("ln_gamma"), L2("ln_beta"), L3("ln1_w"), L3("ln1_b"), L3("ln2_w"), L3("ln2_b"), L3("maa_x"),
                     st[0], st[1], st[2], st[3], st[4], L3("time_decay"), L3("faaaa").reshape(-1),
                     L3("ffn_maa_k"), L3("ffn_maa_r")], axis=1)
    ident = np.eye(P, dtype=np.float32)
    pick0 = np.zeros((P, 32), ml_dtypes.bfloat16)
    pick0[:96] = np.tile(np.eye(32), (3, 1))
    pick1 = np.zeros((P, 16), ml_dtypes.bfloat16)
    pick1[:48] = np.tile(np.eye(16), (3, 1))
    gsel = np.repeat(np.eye(16, dtype=np.float32), S3, axis=0)
    srep = np.zeros((16, S3, S3, 16, S3), np.float32)
    for h in range(16):
        for d in range(S3):
            srep[h, d, d, h, :] = 1.0
    arrays = dict(
        x=a["x"], ctx_in=a["ctx_2048"], mask0=a["mask_Bx1xSxS2_ff0"].reshape(B, T, T),
        mask1=a["mask_Bx1x2048_bf1"].view(np.uint8), mask2=a["mask_BxS2_bf1"].view(np.uint8),
        wall=wall, w1=w1, maaw2=L3("maa_w2").reshape(160, D), decw2=L3("decay_w2"), rows=rows, bcast=bcast, cols=cols,
        gate=L2("gate").reshape(1, 1), ident=ident, ident_h=ident.astype(np.float16),
        ident_b=ident.astype(ml_dtypes.bfloat16), pick0=pick0, pick1=pick1, gsel=gsel, srep=srep.reshape(P, S3, P))
    arrays = {k: np.ascontiguousarray(v) for k, v in arrays.items()}
    nc = bacc.Bacc("TRN2", target_bir_lowering=False, num_devices=1)
    args = {k: nc.dram_tensor("in_" + k, v.shape, mybir.dt.from_np(v.dtype), kind="ExternalInput").ap()
            for k, v in arrays.items()}
    out = nc.dram_tensor("out_x", (B, T, D), F32, kind="ExternalOutput").ap()
    build(nc, out=out, **args)
    r = run(nc, [{"in_" + k: v for k, v in arrays.items()}], core_ids=[0])
    return r.results[0]["out_x"]
```

```python
from contextlib import ExitStack

import concourse.bass as bass
from concourse import mybir

F32, F16, BF16, U8 = mybir.dt.float32, mybir.dt.float16, mybir.dt.bfloat16, mybir.dt.uint8
ALU = mybir.AluOpType
ACT = mybir.ActivationFunctionType
X_AXIS = mybir.AxisListType.X

P = 128
B, T, D = 16, 128, 256
NC = D // P
H0, KV0, HD0 = 32, 8, 8
H1, HD1 = 16, 8
H2, HD2 = 16, 16
H3, S3 = 32, 8
QB = 32
QB2 = 64
VB = 32
M_UNIT = 256.0
NEG = 60000.0

W_COLS = {}
_at = 0
for _name, _n in (("q0", 256), ("kv0", 128), ("o0", 256), ("kv2", 512), ("q2", 256), ("o2", 256),
                  ("maa1", 160), ("dec1", 64), ("r3", 256), ("k3", 256), ("v3", 256), ("g3", 256),
                  ("o3", 256), ("fk3", 256), ("fr3", 256), ("fv3", 256)):
    W_COLS[_name] = (_at, _at + _n)
    _at += _n
W_TOTAL = _at
R_COLS = {"bq0": (0, 256), "bkv0": (256, 384), "bo0": (384, 640), "bq1": (640, 768), "bkv1": (768, 1024)}
R_TOTAL = 1024
BC = {"gamma0": 0, "beta0": 1, "gnw": 2, "gnb": 3}
COL = {n: k for k, n in enumerate(("lng2", "lnb2", "ln1w", "ln1b", "ln2w", "ln2b", "maax", "st0", "st1", "st2",
                                   "st3", "st4", "td", "u", "fmk", "fmr"))}


NPAIR = B // 2
AT0, AT1, AT2 = 0, 8, 24

PER = dict(
    dve=15, pool=6,
    xc_t=1, xc_sb=1, proj0=1, hi0=3, lo0=2, packed_t=6, qt_sb=3, kt_sb=3,
    o_raw=3, o_back=3, o_norm=3, o_t=2, ot_sb=2, res=2, var_in=2, rstd=2, x1=1,
    kv1=1, q1=1, hi1=3, hi1q=1, lo1=3, xm1=1, sq1=1, var1=1, std1=1, ms_t=1, xn1=1,
    x2=1, x2_t=1, x2_sb=1, c_hat=1, c_t=1, ct2_sb=2, proj2=1, hi2=3, lo2=3, x3=1,
    x_in=16, c_in=16, m0_in=16, mx_in=16, s0_in=32, out_stored=16,
    max_scores=28, max_read=28, exp_scores=28, exp_done=28, pv_done=28,
    m_split=7, nm=3, m_t=3, m_sb=4, mask_pool=4, mask_parts=1, mx_step=3, st_cols=1,
    dve3=18, act3=3, x3_free=1,
    xh3=2, xh3_t=2, xnt3=4, xm3=1, xxx3=1, xxt3=2, mix3=5, t53=5, x53=5, wd3_ps=1, wd3=1, w3_ps=1, ew3=1, ws3=1,
    k3_ps=1, k3_sb=1, v3_ps=1, v3_sb=1, r3_ps=1, r3_sb=1, g3_ps=1, g3_sb=1, vt3_ps=1, vt3_sb=1, gt3=1,
    vd3=8, a3=8, sc3=8, pr3=8, ruk3=1, att3=2, att3_sb=1, att3_read=1, d83=1, sq3=1, var3=3, rstd3=3,
    y3=1, y3_t=1, yt3_sb=1, y3_o=1, xkr3=4, ff1=2, kk3=1, tr3=1, ff2=1, s0_read=1, l3_done=1,
)
OF_EACH = list(PER)[:list(PER).index("x_in")]

ORDER = "LALALALLALALALLAALALAAAALALAAALALAALAALALAALALAAALAAALALAALAALAAAAAAAAA"


def build(nc, x, ctx_in, mask0, mask1, mask2, wall, w1, maaw2, decw2, rows, bcast, cols, gate,
          ident, ident_h, ident_b, pick0, pick1, gsel, srep, out):
    with ExitStack() as ctx:
        def sb(name, shape, dt=F32):
            return ctx.enter_context(nc.sbuf_tensor(name, shape, dt))

        W = sb("W", [P, NC, W_TOTAL])
        W1 = sb("W1", [P, 3 * P])
        MAA2 = sb("MAA2", [P, D])
        MAA2b = sb("MAA2b", [32, D])
        DEC2 = sb("DEC2", [64, D])
        ROWS = sb("ROWS", [3, R_TOTAL])
        ROWP = sb("ROWP", [3, 3, R_TOTAL], BF16)
        BCR = sb("BCR", [P, 4, D])
        CV = sb("CV", [P, NC, 16])
        ID = sb("ID", [P, P])
        IDH = sb("IDH", [P, P], F16)
        IDB = sb("IDB", [P, P], BF16)
        PICK0 = sb("PICK0", [P, 32], BF16)
        PICK1 = sb("PICK1", [P, 16], BF16)
        GSEL = sb("GSEL", [P, 32])
        SREP = sb("SREP", [P, 8, P])
        IDLE = sb("IDLE", [P, 2])
        IDLE_DVE = sb("IDLE_DVE", [P, 1])
        GATE = sb("GATE", [P, 1])
        TG = sb("TG", [P, 1])
        ONES = sb("ONES", [3, P], BF16)
        EPS3 = sb("EPS3", [P, 1])
        NHALF = sb("NHALF", [P, 64])
        MRAW1 = sb("MRAW1", [16, 2 * P], U8)
        MRAW2 = sb("MRAW2", [16, P], U8)
        MF = sb("MF", [16, 3 * P], F16)
        KM1 = sb("KM1", [P, 16, 2], F16)
        KM2 = sb("KM2", [P, 16, 1], F16)
        X = sb("X", [P, 2, D])
        C = sb("C", [P, 2, D])
        M0 = sb("M0", [P, 2, P])
        MXR = sb("MXR", [P, 2, D], U8)
        S0 = sb("S0", [P, 2, NC, S3])
        CXT = sb("CXT", [P, 2, 4, P])
        MP = sb("MP", [P, 3, 2, P], BF16)
        MR = sb("MR", [P, 2, P])
        QN0 = sb("QN0", [P, 2, H0, QB], F16)
        KN0 = sb("KN0", [P, 2, KV0, 4, QB], F16)
        V0 = sb("V0", [P, 2, KV0, VB])
        QN1, KN1 = QN0, KN0[:, :, :, :, :].rearrange("p c a g b -> p c (a g) b")
        V1 = sb("V1", [P, 2, 2 * H1, VB])
        QN2 = sb("QN2", [P, 2, H2, QB2], F16)
        KN2 = sb("KN2", [P, 2, H2, QB2], F16)
        V2 = sb("V2", [P, 2, H2, VB])
        QT = sb("QT", [P, 2, 8, P], F16)
        KT = sb("KT", [P, 2, 8, P], F16)
        NM = sb("NM", [P, 2, 32])
        NR = sb("NR", [P, 2, 32])
        MN = sb("MN", [P, 2, 2, P], BF16)
        MT = sb("MT", [P, 2, 2 * P], BF16)
        PROB = sb("PROB", [P, 8, 512])
        OTT = sb("OTT", [P, 8, P])
        RS = sb("RS", [P, 2, 32])
        ON = sb("ON", [P, 2, D])
        OT = sb("OT", [P, 2, NC, P])
        X1 = sb("X1", [P, 2, D])
        XH = sb("XH", [P, 2, D])
        ST = sb("ST", [P, 2, 6])
        MV = sb("MV", [P, 2, 2])
        VE = sb("VE", [P, 2])
        RSTD = sb("RSTD", [P, 2])
        MXF = sb("MXF", [P, 2, D])
        XM1 = sb("XM1", [P, 2, D])
        SM = sb("SM", [P, 2, 8])
        MEAN = sb("MEAN", [P, 2, 2, P])
        VAR = sb("VAR", [P, 2, 2, P])
        EX2 = sb("EX2", [P, 2, 2, P])
        X3 = sb("X3", [P, 2, D])
        STC3 = sb("STC3", [P, 2, NC, 2])
        STC = sb("STC", [P, 2, NC, 2])
        X3L = sb("X3L", [P, 2, D])
        XH3 = sb("XH3", [P, 2, D])
        ST3 = sb("ST3", [P, 2, 6])
        MV3 = sb("MV3", [P, 2, 2])
        VE3 = sb("VE3", [P, 2])
        RSTD3 = sb("RSTD3", [P, 2])
        XNT = sb("XNT", [P, NC, 2, P + 1])
        SX = sb("SX", [P, NC, 2, P])
        XM = sb("XM", [P, NC, 2, P])
        XXT = sb("XXT", [P, 2 * P])
        XXT4 = sb("XXT4", [32, 2 * P])
        T5 = sb("T5", [P, 2, NC, 2, P])
        WD = sb("WD", [64, 2 * P])
        EW = sb("EW", [P, NC, 2, P])
        WS = sb("WS", [P, NC, 2, P])
        KS = sb("KS", [P, NC, 2, P])
        RR = sb("RR", [P, NC, 2, P])
        VT3 = sb("VT3", [P, NC, 2, P])
        VN3 = sb("VN3", [P, 2 * D])
        A3 = sb("A3", [P, 8, NC, 2, P])
        RUK = sb("RUK", [P, NC, 2, P])
        ATT = sb("ATT", [P, 2 * D])
        DD = sb("DD", [P, 2 * D])
        G8 = sb("G8", [P, 3, 64])
        GT = sb("GT", [P, 2 * D])
        X4 = sb("X4", [P, 2, D])
        OUT = sb("OUT", [P, 2, D])

        X2, XN1, XSQ, CH, X2T, STD = X1, XM1, XH, ON, OT, VAR
        CT2 = XH[:, :, :].rearrange("p c (n t) -> p c n t", n=NC)
        YT, KKR, KK, TR, Y, XKR, X5 = VT3, KS, RR, VN3, DD, T5, A3
        ATR = T5
        GB = RUK[:, :, :, :].rearrange("p c b t -> p (c b t)")
        SQ = EW[:, :, :, :].rearrange("p c b t -> p (c b t)")
        PB = ctx.enter_context(nc.psum_tensor("PB", [P, 8, 512], F32))

        sem = {n: ctx.enter_context(nc.semaphore(n)) for n in PER if n not in OF_EACH}
        seq = [{n: ctx.enter_context(nc.semaphore(f"{n}_{c}")) for n in OF_EACH} for c in range(2)]
        w_in = ctx.enter_context(nc.semaphore("w_in"))
        w3_in = ctx.enter_context(nc.semaphore("w3_in"))
        masks_in = ctx.enter_context(nc.semaphore("masks_in"))
        set_dve = ctx.enter_context(nc.semaphore("set_dve"))
        set_act = ctx.enter_context(nc.semaphore("set_act"))
        set_pe = ctx.enter_context(nc.semaphore("set_pe"))
        block = ctx.enter_context(nc.Block())
        N_MASKS, N_WEIGHTS, N_WEIGHTS3 = 6, 8, 6
        BOTH = (0, 1)

        def at(j, name, k=None):
            return j * PER[name] + (PER[name] if k is None else k)

        class Count:

            def __init__(self, j):
                self.j, self.given = j, {}

            def __call__(self, name, c=None):
                self.given[name, c] = self.given.get((name, c), 0) + 1
                return at(self.j, name, self.given[name, c])

            def end(self):
                wrong = {n: (k, PER[n[0]]) for n, k in self.given.items() if k != PER[n[0]]}
                assert not wrong, wrong

        def wcol(name, c, a=0, b=None):
            lo, hi = W_COLS[name]
            return W[:, c, lo + a:(hi if b is None else lo + b)]

        def row(name):
            return ROWP[:, 0, R_COLS[name][0]:R_COLS[name][1]]

        def vec(name, c):
            return CV[:, c, COL[name]:COL[name] + 1]

        def h16(bank):
            return PB[:, bank, :].bitcast(F16)

        def b16(bank):
            return PB[:, bank, :].bitcast(BF16)

        def turns(eng, attention, layer3):
            for _ in attention(0, True):
                pass
            eng.wait_ge(w3_in, 16 * N_WEIGHTS3)
            with eng.Fori(1, NPAIR) as j:
                a, b = attention(j, False), layer3(j - 1, False)
                for step in ORDER:
                    next(a if step == "A" else b)
                assert next(a, None) is None and next(b, None) is None
            for _ in layer3(NPAIR - 1, False):
                pass

        @block.sync
        def _(sp):
            pair = lambda ap: ap.rearrange("(j c) t d -> j t c d", c=2)
            xv, cv, mv, ov = pair(x), pair(ctx_in), pair(mask0), pair(out)
            mxv = mask1.rearrange("(j c) o d -> j o (c d)", c=2)
            sv = ctx_in.rearrange("(j c) t d -> j c t d", c=2)

            def load(j, j_free):
                if j_free is not None:
                    sp.wait_ge(sem["mask_parts"], at(j_free, "mask_parts"))
                sp.dma_start(M0[:, :, :], mv[j]).then_inc(sem["m0_in"], 16)
                if j_free is not None:
                    sp.wait_ge(seq[0]["x1"], at(j_free, "x1"))
                    sp.wait_ge(seq[1]["x1"], at(j_free, "x1"))
                sp.dma_start(X[:, :, :], xv[j]).then_inc(sem["x_in"], 16)
                sp.dma_start(MXR[:, :, :].rearrange("p c d -> p (c d)"), mxv[j].broadcast_to([P, 2 * D])).then_inc(sem["mx_in"], 16)
                if j_free is not None:
                    sp.wait_ge(seq[0]["c_hat"], at(j_free, "c_hat"))
                    sp.wait_ge(seq[1]["c_hat"], at(j_free, "c_hat"))
                sp.dma_start(C[:, :, :], cv[j]).then_inc(sem["c_in"], 16)

            def load_state(j):
                for c in BOTH:
                    last = sp.dma_start(S0[:, c, :, :], sv[j, c, 2:2 + S3, :].rearrange("r (p d) -> (r p) d", d=S3)
                                        .rearrange("(n p) d -> p n d", p=P))
                    last.then_inc(sem["s0_in"], 16)

            sp.sem_inc(sem["out_stored"], 16)
            for dst, src in ((GATE[:, :], gate.broadcast_to([P, 1])), (MRAW1[:, :], mask1.rearrange("b o d -> (b o) d")),
                             (MRAW2[:, :], mask2), (IDH[:, :], ident_h), (ROWS[:, :], rows.broadcast_to([3, R_TOTAL])), (ID[:, :], ident)):
                sp.dma_start(dst, src).then_inc(masks_in, 16)
            load(0, None)
            wv = wall.rearrange("(c p) n -> p c n", p=P)
            W_L3 = W_COLS["maa1"][0]
            for a, b in ((0, 640), (640, W_L3)):
                sp.dma_start(W[:, :, a:b], wv[:, :, a:b]).then_inc(w_in, 16)
            for dst, src in ((IDB[:, :], ident_b), (W1[:, :], w1), (PICK0[:, :], pick0), (PICK1[:, :], pick1),
                             (CV[:, :, :], cols.rearrange("(c p) n -> p c n", p=P))):
                sp.dma_start(dst, src).then_inc(w_in, 16)
            sp.dma_start(BCR[:, :, :].rearrange("p a b -> p (a b)"), bcast.broadcast_to([P, 4 * D])).then_inc(w_in, 16)
            load_state(0)
            sp.dma_start(W[:, :, W_L3:W_TOTAL], wv[:, :, W_L3:W_TOTAL]).then_inc(w3_in, 16)
            for dst, src in ((MAA2[:, :], maaw2[0:P, :]), (MAA2b[:, :], maaw2[P:P + 32, :]), (DEC2[:, :], decw2),
                             (GSEL[:, :], gsel), (SREP[:, :, :], srep)):
                sp.dma_start(dst, src).then_inc(w3_in, 16)

            def state_and_store(j):
                sp.wait_ge(sem["s0_read"], at(j - 1, "s0_read"))
                load_state(j)
                sp.wait_ge(sem["l3_done"], at(j - 1, "l3_done"))
                sp.dma_start(ov[j - 1], OUT[:, :, :]).then_inc(sem["out_stored"], 16)

            load(1, 0)
            with sp.Fori(2, NPAIR) as j:
                load(j, j - 1)
                state_and_store(j - 1)
            state_and_store(NPAIR - 1)
            sp.wait_ge(sem["l3_done"], NPAIR)
            sp.dma_start(ov[NPAIR - 1], OUT[:, :, :]).then_inc(sem["out_stored"], 16)
            sp.wait_ge(sem["out_stored"], 16 * (NPAIR + 1))

        @block.tensor
        def _(pe):
            mm = pe.matmul
            pe.wait_ge(masks_in, 16 * N_MASKS)
            pe.wait_ge(set_dve, 1)
            for k in range(3):
                last = pe.transpose(h16(0)[:, 16 * k:16 * k + 16], MF[:, P * k:P * k + P], IDH[0:16, 0:16])
            last.then_inc(set_pe, 1)
            pe.wait_ge(set_dve, 9)
            pe.wait_ge(w_in, 16 * N_WEIGHTS)

            def project(dst, lhs, weights, bias=None):
                n = len(lhs)
                for c in range(n):
                    last = mm(dst, lhs[c], weights[c], start=(c == 0), stop=(c == n - 1 and bias is None))
                if bias is not None:
                    last = mm(dst, ONES[:, :], bias, start=False, stop=True)
                return last

            def turn_two(bank, src, at_col=0):
                for c in range(NC):
                    last = pe.transpose(PB[:, bank, at_col + P * c:at_col + P * c + P], src[:, P * c:P * c + P], ID[:, :])
                return last

            def turn_packed(bank, src):
                for k in range(8):
                    last = pe.transpose(h16(bank)[:, P * k:P * k + P], src[:, P * k:P * k + P], IDH[:, :])
                return last

            def attention(j, first):
                def packed(n, lo, qn, kn):
                    for c in BOTH:
                        pe.wait_ge(seq[c][lo], at(j, lo))
                        turn_packed(2 + c, qn(c)).then_inc(seq[c]["packed_t"], 1)
                        turn_packed(c, kn(c)).then_inc(seq[c]["packed_t"], 1)

                def maxima(base, n_pairs, unit, units):
                    layer = {AT0: 1, AT1: 2, AT2: 3}[base]
                    for c in BOTH:
                        pe.wait_ge(seq[c]["qt_sb"], at(j, "qt_sb", layer))
                        pe.wait_ge(seq[c]["kt_sb"], at(j, "kt_sb", layer))
                    for c in BOTH:
                        for n in range(n_pairs):
                            m = c * n_pairs + n
                            if m >= 2:
                                pe.wait_ge(sem["max_read"], at(j, "max_read", base + m - 1))
                            for k in range(2):
                                last = unit(2 * (m % 2) + k, c, *units[2 * n + k])
                            last.then_inc(sem["max_scores"], 1)
                            if n % 4 == 3 or n == n_pairs - 1:
                                yield

                def turn_maxima(layer, n):
                    pe.wait_ge(sem["nm"], at(j, "nm", layer))
                    for c in BOTH:
                        for a in range(n):
                            last = pe.transpose(b16(4 + c)[:, P * a:P * a + P], MN[:, c, a, :], IDB[:, :])
                    last.then_inc(sem["m_t"], 1)

                def attend(base, n_pairs, score_unit, units, per_product, products, before_product):
                    issued = 0
                    pe.wait_ge(sem["m_sb"], at(j, "m_sb", {AT0: 1, AT1: 2, AT2: 4}[base]))
                    for step in range(2 * n_pairs // per_product):
                        first_of_next = step * per_product == n_pairs
                        ahead = per_product * (step + 1) + 2
                        if base == AT0 and first_of_next:
                            ahead += 1
                        while issued < min(ahead, 2 * n_pairs):
                            c, n = issued // n_pairs, issued % n_pairs
                            if base == AT1 and issued == n_pairs:
                                pe.wait_ge(sem["m_sb"], at(j, "m_sb", 3))
                            if issued >= 2:
                                pe.wait_ge(sem["exp_done"], at(j, "exp_done", base + issued - 1))
                            for k in range(2):
                                last = score_unit(2 * (issued % 2) + k, c, *units[2 * n + k])
                            last.then_inc(sem["exp_scores"], 1)
                            issued += 1
                        m = step * per_product
                        c, n = m // n_pairs, m % n_pairs
                        before_product(c, n)
                        pe.wait_ge(sem["exp_done"], at(j, "exp_done", base + m + per_product))
                        products((2 * (base + m)) % 8, c, n).then_inc(sem["pv_done"], per_product)
                        yield step

                def turn_back(c, layer, bank, pieces):
                    pe.wait_ge(seq[c]["o_raw"], at(j, "o_raw", layer))
                    for n, piece in enumerate(pieces):
                        last = pe.transpose(PB[:, bank + n // 4, P * (n % 4):P * (n % 4) + P], OTT[:, piece, :], ID[:, :])
                    last.then_inc(seq[c]["o_back"], 1)

                def out_turn(c, bank, layer):
                    pe.wait_ge(seq[c]["o_norm"], at(j, "o_norm", layer))
                    turn_two(bank + c, ON[:, c, :]).then_inc(seq[c]["o_t"], 1)

                def out_project(c, bank, k, weights, bias=None):
                    pe.wait_ge(seq[c]["ot_sb"], at(j, "ot_sb", k))
                    project(PB[:, bank + c, D:2 * D], [OT[:, c, n, :] for n in range(NC)],
                            [wcol(weights, n) for n in range(NC)], bias).then_inc(seq[c]["res"], 1)

                pe.wait_ge(sem["c_in"], at(j, "c_in"))
                pe.wait_ge(sem["x_in"], at(j, "x_in"))
                for c in BOTH:
                    turn_two(c, C[:, c, :])
                    turn_two(c, X[:, c, :], D).then_inc(seq[c]["xc_t"], 1)
                yield
                for c in BOTH:
                    pe.wait_ge(seq[c]["xc_sb"], at(j, "xc_sb"))
                    project(PB[:, 2 + c, 0:D], [CXT[:, c, 2 + n, :] for n in range(NC)], [wcol("q0", n) for n in range(NC)], row("bq0"))
                    project(PB[:, 2 + c, D:D + P], [CXT[:, c, n, :] for n in range(NC)],
                            [wcol("kv0", n) for n in range(NC)], row("bkv0")).then_inc(seq[c]["proj0"], 1)
                yield
                packed(1, "lo0", lambda c: QN0[:, c, :, :].rearrange("p a b -> p (a b)"),
                       lambda c: KN0[:, c, :, :, :].rearrange("p a g b -> p (a g b)"))
                yield
                pe.wait_ge(sem["mask_parts"], at(j, "mask_parts"))
                K = 3 * HD0

                def l0_scores(bank, c, half, g, keys_out):
                    for n in range(3):
                        if keys_out:
                            mm(PB[:, bank, :], MP[:, n, c, :], IDB[:, None, :].broadcast_to([P, 4, P]), start=(n == 0), stop=False)
                        else:
                            mm(PB[:, bank, :], IDB[:, :], MP[:, n, c:c + 1, :].broadcast_to([P, 4, P]), start=(n == 0), stop=False)
                    for k in range(4):
                        kv = 4 * half + k
                        dst = PB[:, bank, P * k:P * k + P]
                        q, key = QT[32 * g:32 * g + K, c, kv, :], KT[32 * g:32 * g + K, c, kv, :]
                        if keys_out:
                            mm(dst, key, q, start=False, stop=False)
                        else:
                            last = mm(dst, q, key, start=False, stop=(k == 3))
                    if keys_out:
                        for k in range(4):
                            col = (4 * half + g) * 4 + k
                            last = mm(PB[:, bank, P * k:P * k + P], PICK0[:, col:col + 1].broadcast_to([P, P]), MT[:, c, 0:P],
                                      start=False, stop=(k == 3))
                    return last

                def l0_products(slot, c, n):
                    for k in range(4):
                        last = mm(PB[32 * k:32 * k + 32, 4 + n // 2, D * (n % 2):D * (n % 2) + D], V0[:, c, 4 * (n // 2) + k, :],
                                  PROB[:, slot:slot + 2, P * k:P * k + P], start=True, stop=True)
                    return last

                def l0_before(c, n):
                    if c == 1 and n == 0:
                        turn_back(0, 1, 4, range(8))
                        pe.wait_ge(seq[0]["o_norm"], at(j, "o_norm", 1))

                units0 = [(half, g) for half in range(2) for g in range(4)]
                yield from maxima(AT0, 4, lambda bank, c, half, g: l0_scores(bank, c, half, g, False), units0)
                if not first:
                    for c in BOTH:
                        pe.wait_ge(seq[c]["x3"], at(j - 1, "x3"))
                turn_maxima(1, 1)
                yield
                for m in attend(AT0, 4, lambda bank, c, half, g: l0_scores(bank, c, half, g, True), units0, 1, l0_products, l0_before):
                    if m == 7:
                        out_turn(0, 2, 1)
                    yield
                for c in BOTH:
                    for a in range(2):
                        for k, dst in enumerate((PB[:, c, P * a:P * a + P], PB[:, c, D + P * a:D + P * a + P])):
                            mm(dst, C[:, c, P * a:P * a + P], W1[:, P + P * k:2 * P + P * k], start=True, stop=False)
                            last = mm(dst, ONES[:, :], row("bkv1")[:, P * k:P * k + P], start=False, stop=True)
                    last.then_inc(seq[c]["kv1"], 1)
                    if c == 0:
                        turn_back(1, 1, 4, range(8))
                out_project(0, 2, 1, "o0", row("bo0"))
                yield
                out_turn(1, 2, 1)
                yield
                out_project(1, 2, 1, "o0", row("bo0"))
                for c in BOTH:
                    if c == 1:
                        yield
                    pe.wait_ge(seq[c]["x1"], at(j, "x1"))
                    for a in range(2):
                        mm(PB[:, 2 + c, P * a:P * a + P], X1[:, c, P * a:P * a + P], W1[:, 0:P], start=True, stop=False)
                        last = mm(PB[:, 2 + c, P * a:P * a + P], ONES[:, :], row("bq1"), start=False, stop=True)
                    last.then_inc(seq[c]["q1"], 1)
                yield
                packed(2, "lo1", lambda c: QN1[:, c, :, :].rearrange("p a b -> p (a b)"), lambda c: KN1[:, c, :, :].rearrange("p a b -> p (a b)"))
                yield
                K1 = 3 * HD1 + 1

                def l1_max(bank, c, a, jj, p):
                    rows_ = slice(32 * jj, 32 * jj + K1)
                    for k in range(2):
                        tt = 2 * p + k
                        last = mm(PB[:, bank, D * k:D * k + D], QT[rows_, c, 4 * a + tt, :], KT[rows_, c, tt:8:4, :], start=True, stop=True)
                    return last

                def l1_scores(bank, c, jj, tt):
                    rows_ = slice(32 * jj, 32 * jj + K1 + 2)
                    for n in range(2):
                        last = mm(PB[:, bank, D * n:D * n + D], KT[rows_, c, 4 * n + tt, :], QT[rows_, c, tt:8:4, :], start=True, stop=True)
                    return last

                def l1_products(slot, c, n):
                    tt = n // 2
                    for half in range(2):
                        for jj in range(4):
                            last = mm(PB[32 * jj:32 * jj + 32, 4 + tt // 2, D * (tt % 2):D * (tt % 2) + D], V1[:, c, H1 * half + 4 * tt + jj, :],
                                      PROB[:, slot + jj, D * half:D * half + D], start=(half == 0), stop=(half == 1))
                    return last

                def l1_before(c, n):
                    if c == 1 and n == 0:
                        turn_back(0, 2, 4, [2 * tt + a for a in range(2) for tt in range(4)])
                        pe.wait_ge(seq[0]["o_norm"], at(j, "o_norm", 2))

                yield from maxima(AT1, 8, l1_max, [(a, jj, p) for a in range(2) for jj in range(4) for p in range(2)])
                pe.wait_ge(sem["nm"], at(j, "nm", 2))
                for c in BOTH:
                    last = turn_packed(4 + c, QN1[:, c, :, :].rearrange("p a b -> p (a b)"))
                last.then_inc(sem["m_t"], 1)
                yield
                for m in attend(AT1, 8, l1_scores, [(jj, tt) for tt in range(4) for jj in range(4)], 2, l1_products, l1_before):
                    yield
                turn_back(1, 2, 4, [2 * tt + a for a in range(2) for tt in range(4)])
                for c in BOTH:
                    pe.wait_ge(seq[c]["c_hat"], at(j, "c_hat"))
                    turn_two(2 + c, CH[:, c, :]).then_inc(seq[c]["c_t"], 1)
                for c in BOTH:
                    pe.wait_ge(seq[c]["std1"], at(j, "std1"))
                    for a in range(2):
                        pe.transpose(PB[:, c, P * a:P * a + P], MEAN[:, c, a, :], ID[:, :])
                        last = pe.transpose(PB[:, c, D + P * a:D + P * a + P], STD[:, c, a, :], ID[:, :])
                    last.then_inc(seq[c]["ms_t"], 1)
                yield
                for c in BOTH:
                    pe.wait_ge(seq[c]["ct2_sb"], at(j, "ct2_sb"))
                    pe.wait_ge(seq[c]["x2"], at(j, "x2"))
                    turn_two(2 + c, X2[:, c, :], D).then_inc(seq[c]["x2_t"], 1)
                    project(PB[:, c, :], [CT2[:, c, n, :] for n in range(NC)], [wcol("kv2", n) for n in range(NC)])
                yield
                for c in BOTH:
                    pe.wait_ge(seq[c]["x2_sb"], at(j, "x2_sb"))
                    project(PB[:, 2 + c, 0:D], [X2T[:, c, n, :] for n in range(NC)],
                            [wcol("q2", n) for n in range(NC)]).then_inc(seq[c]["proj2"], 1)
                yield
                packed(3, "lo2", lambda c: QN2[:, c, :, :].rearrange("p a b -> p (a b)"), lambda c: KN2[:, c, :, :].rearrange("p a b -> p (a b)"))
                yield
                K2 = 3 * HD2 + 1

                def l2_scores(bank, c, r, tg, keys_out):
                    rows_ = slice(64 * r, 64 * r + K2)
                    for k in range(4):
                        tt = 4 * tg + k
                        dst = PB[:, bank, P * k:P * k + P]
                        if keys_out:
                            col = 8 * r + tt
                            mm(dst, KT[rows_, c, tt, :], QT[rows_, c, tt, :], start=True, stop=False)
                            last = mm(dst, PICK1[:, col:col + 1].broadcast_to([P, P]), MT[:, c, 0:P], start=False, stop=True)
                        else:
                            last = mm(dst, QT[rows_, c, tt, :], KT[rows_, c, tt, :], start=True, stop=True)
                    return last

                def l2_products(slot, c, n):
                    for tg in range(2):
                        for k in range(4):
                            last = mm(PB[32 * k:32 * k + 32, 4 + c, D * n + P * tg:D * n + P * tg + P], V2[:, c, 2 * (4 * tg + k) + n, :],
                                      PROB[:, slot + tg, P * k:P * k + P], start=True, stop=True)
                    return last

                units2 = [(r, tg) for r in range(2) for tg in range(2)]
                yield from maxima(AT2, 2, lambda bank, c, r, tg: l2_scores(bank, c, r, tg, False), units2)
                turn_maxima(3, 1)
                yield
                for m in attend(AT2, 2, lambda bank, c, r, tg: l2_scores(bank, c, r, tg, True), units2, 1, l2_products, lambda c, n: None):
                    yield
                for c in BOTH:
                    turn_back(c, 3, 4 + c, range(4 * c, 4 * c + 4))
                yield
                for c in BOTH:
                    out_turn(c, 4, 3)
                yield
                for c in BOTH:
                    out_project(c, 4, 2, "o2")
                yield

            def layer3(j, first):
                flat = lambda ap: ap.rearrange("p c b t -> p (c b t)")
                bt = lambda ap: ap.rearrange("p b t -> p (b t)")

                def to_channels(bank, weights, src):
                    for co in range(NC):
                        last = project(PB[:, bank, D * co:D * co + D], [wcol(weights, c, P * co, P * co + P) for c in range(NC)],
                                       [bt(src[:, c, :, :]) for c in range(NC)])
                    return last

                def to_tokens(bank, weights, src):
                    for b in BOTH:
                        last = project(PB[:, bank, D * b:D * b + D], [src[:, c, b, :] for c in range(NC)], [wcol(weights, c) for c in range(NC)])
                    return last

                def turn_pair(bank, src):
                    for b in BOTH:
                        for c in range(NC):
                            last = pe.transpose(PB[:, bank, D * c + P * b:D * c + P * b + P], src(b, c), ID[:, :])
                    return last

                def mix(k, n, bank):
                    for c in range(NC):
                        lhs = MAA2[32 * n:32 * n + 32, P * c:P * c + P] if n < 4 else MAA2b[:, P * c:P * c + P]
                        rhs = XXT[32 * n:32 * n + 32, :] if n < 4 else XXT4[:, :]
                        last = mm(PB[:, bank, D * c:D * c + D], lhs, rhs, start=True, stop=True)
                    last.then_inc(sem["mix3"], 1)

                yield
                pe.wait_ge(sem["xh3"], at(j, "xh3", 1))
                turn_pair(6, lambda b, c: XH3[:, b, P * c:P * c + P]).then_inc(sem["xh3_t"], 1)
                yield
                pe.wait_ge(sem["xm3"], at(j, "xm3"))
                project(PB[:, 7, 0:D], [wcol("maa1", c, 0, P) for c in range(NC)], [bt(XM[:, c, :, :]) for c in range(NC)])
                project(PB[0:32, 7, D:2 * D], [wcol("maa1", c, P, P + 32) for c in range(NC)],
                        [bt(XM[:, c, :, :]) for c in range(NC)]).then_inc(sem["xxx3"], 1)
                yield
                pe.wait_ge(sem["xxt3"], at(j, "xxt3"))
                mix(0, 1, 6)
                mix(1, 0, 7)
                yield
                pe.wait_ge(sem["t53"], at(j, "t53", 1))
                mix(2, 2, 6)
                pe.wait_ge(sem["t53"], at(j, "t53", 2))
                mix(3, 3, 7)
                yield
                pe.wait_ge(sem["t53"], at(j, "t53", 3))
                mix(4, 4, 6)
                pe.wait_ge(sem["t53"], at(j, "t53", 4))
                pe.wait_ge(sem["x53"], at(j, "x53", 1))
                project(PB[0:64, 7, 0:D], [wcol("dec1", c) for c in range(NC)], [bt(X5[:, 1, c, :, :]) for c in range(NC)]).then_inc(sem["wd3_ps"], 1)
                yield
                pe.wait_ge(sem["t53"], at(j, "t53", 5))
                pe.wait_ge(sem["wd3"], at(j, "wd3"))
                for c in range(NC):
                    last = mm(PB[:, 6, D * c:D * c + D], DEC2[:, P * c:P * c + P], WD[:, :], start=True, stop=True)
                last.then_inc(sem["w3_ps"], 1)
                pe.wait_ge(sem["x53"], at(j, "x53", 2))
                to_channels(7, "k3", X5[:, 0]).then_inc(sem["k3_ps"], 1)
                yield
                pe.wait_ge(sem["x53"], at(j, "x53", 3))
                pe.wait_ge(sem["ew3"], at(j, "ew3"))
                to_channels(6, "v3", X5[:, 2]).then_inc(sem["vt3_ps"], 1)
                yield
                pe.wait_ge(sem["k3_sb"], at(j, "k3_sb"))
                pe.wait_ge(sem["vt3_sb"], at(j, "vt3_sb"))
                for b in BOTH:
                    for c in range(NC):
                        last = pe.transpose(PB[:, 7, D * b + P * c:D * b + P * c + P], VT3[:, c, b, :], ID[:, :])
                last.then_inc(sem["v3_ps"], 1)
                pe.wait_ge(sem["x53"], at(j, "x53", 4))
                to_channels(6, "r3", X5[:, 3]).then_inc(sem["r3_ps"], 1)
                pe.wait_ge(sem["x53"], at(j, "x53", 5))
                pe.wait_ge(sem["v3_sb"], at(j, "v3_sb"))
                to_tokens(7, "g3", X5[:, 4]).then_inc(sem["g3_ps"], 1)
                yield
                pe.wait_ge(sem["r3_sb"], at(j, "r3_sb"))
                for d in range(S3):
                    if d == 1:
                        pe.wait_ge(sem["gt3"], at(j, "gt3"))
                    if d >= 2:
                        pe.wait_ge(sem["a3"], at(j, "a3", d - 1))
                    mm(PB[:, 6 + d % 2, :], SREP[:, d, :], flat(VT3[:, :, :, :]), start=True, stop=True).then_inc(sem["vd3"], 1)
                    if d % 2:
                        yield
                pe.wait_ge(sem["a3"], at(j, "a3"))
                pe.wait_ge(sem["ruk3"], at(j, "ruk3"))
                pe.wait_ge(sem["a3"], at(j, "a3"))
                pe.wait_ge(sem["ruk3"], at(j, "ruk3"))
                for d in range(S3):
                    pe.wait_ge(sem["pr3"], at(j, "pr3", d + 1))
                    last = mm(PB[32 * (d % 4):32 * (d % 4) + 32, 6 + d // 4, :], GSEL[:, :], flat(A3[:, d]), start=True, stop=True)
                last.then_inc(sem["att3"], 1)
                yield
                pe.wait_ge(sem["att3_sb"], at(j, "att3_sb"))
                for b in BOTH:
                    for c in range(NC):
                        for half in range(2):
                            k = 2 * c + half
                            pe.transpose(PB[:, 6 + b, P * k:P * k + P], ATR[:, half, c, b, :], ID[:, :])
                for b in BOTH:
                    for c in range(NC):
                        last = mm(PB[:, 6 + b, D * c + 16:D * c + 32], RUK[:, c, b, :], GSEL[:, 0:16], start=True, stop=True)
                last.then_inc(sem["att3"], 1)
                yield
                pe.wait_ge(sem["att3_read"], at(j, "att3_read"))
                yield
                yield
                pe.wait_ge(sem["y3"], at(j, "y3"))
                turn_pair(6, lambda b, c: Y[:, D * b + P * c:D * b + P * c + P]).then_inc(sem["y3_t"], 1)
                yield
                pe.wait_ge(sem["yt3_sb"], at(j, "yt3_sb"))
                to_tokens(7, "o3", YT).then_inc(sem["y3_o"], 1)
                yield
                yield
                pe.wait_ge(sem["xh3"], at(j, "xh3", 2))
                turn_pair(6, lambda b, c: XH3[:, b, P * c:P * c + P]).then_inc(sem["xh3_t"], 1)
                yield
                yield
                pe.wait_ge(sem["xkr3"], at(j, "xkr3"))
                to_channels(7, "fk3", XKR[:, 0]).then_inc(sem["ff1"], 1)
                to_tokens(6, "fr3", XKR[:, 1]).then_inc(sem["ff1"], 1)
                yield
                pe.wait_ge(sem["kk3"], at(j, "kk3"))
                to_tokens(7, "fv3", KK).then_inc(sem["ff2"], 1)
                yield
                pe.wait_ge(sem["tr3"], at(j, "tr3"))
                pe.wait_ge(sem["l3_done"], at(j, "l3_done"))
                yield

            turns(pe, attention, layer3)

        @block.scalar
        def _(act):
            def copy(o, a, scale=1.0):
                return act.activation(o, a, ACT.Copy, scale=scale)

            act.wait_ge(masks_in, 16 * N_MASKS)
            act.activation(TG[:, :], GATE[:, :], ACT.Tanh).then_inc(set_act, 1)
            act.wait_ge(w_in, 16 * N_WEIGHTS)
            act.wait_ge(set_act, 1)
            act.wait_ge(set_dve, 9)

            def attention(j, first):
                own = Count(j)
                two = lambda ap: ap.rearrange("p a b -> p (a b)")

                def exp_pair(m):
                    base = AT0 if m < AT1 else AT1 if m < AT2 else AT2
                    act.wait_ge(sem["exp_scores"], at(j, "exp_scores", m + 1))
                    if m >= 4:
                        act.wait_ge(sem["pv_done"], at(j, "pv_done", m - 3))
                    elif not first:
                        act.wait_ge(sem["pv_done"], at(j - 1, "pv_done"))
                    bank, slot = 2 * ((m - base) % 2), (2 * m) % 8
                    act.activation(PROB[:, slot:slot + 2, :], PB[:, bank:bank + 2, :], ACT.Exp).then_inc(sem["exp_done"], 1)

                def keys_turned():
                    for c in BOTH:
                        own("kt_sb", c)
                        act.wait_ge(seq[c]["packed_t"], at(j, "packed_t", 2 * own.given["kt_sb", c]))
                        copy(two(KT[:, c, :, :]), h16(c)).then_inc(seq[c]["kt_sb"], 1)

                def maxima_turned(layer, n):
                    act.wait_ge(sem["m_t"], at(j, "m_t", layer))
                    copy(MT[:, :, 0:n], PB[:, 4:6, :].bitcast(BF16)[:, :, 0:n]).then_inc(sem["m_sb"], 1)

                def products_out(c, m):
                    act.wait_ge(sem["pv_done"], at(j, "pv_done", m))
                    copy(OTT[:, :, :].rearrange("p (b u) t -> p b (u t)", u=4), PB[:, 4:6, :]).then_inc(seq[c]["o_raw"], 1)

                def out_turned(c, bank, k):
                    act.wait_ge(seq[c]["o_t"], at(j, "o_t", k))
                    copy(two(OT[:, c, :, :]), PB[:, bank + c, 0:D]).then_inc(seq[c]["ot_sb"], 1)

                for c in BOTH:
                    act.wait_ge(seq[c]["xc_t"], at(j, "xc_t"))
                    copy(two(CXT[:, c, :, :]), PB[:, c, :]).then_inc(seq[c]["xc_sb"], 1)
                yield
                for c in BOTH:
                    act.wait_ge(seq[c]["proj0"], at(j, "proj0"))
                    q = PB[:, 2 + c, 0:D].rearrange("p (h d) -> p h d", d=HD0)
                    k = PB[:, 2 + c, D:D + 64].rearrange("p (h d) -> p h d", d=HD0)
                    v = PB[:, 2 + c, D + 64:D + P].rearrange("p (h d) -> p h d", d=HD0)
                    copy(QN0[:, c, :, 0:16].rearrange("p h (a d) -> p h a d", a=2),
                         q[:, :, None, :].broadcast_to([P, H0, 2, HD0]), float(HD0) ** -0.5).then_inc(seq[c]["hi0"], 1)
                    copy(KN0[:, c, :, :, :].rearrange("p k g (a d) -> p k (g a) d", a=2)[:, :, :, 0:8],
                         k[:, :, None, :].broadcast_to([P, KV0, 8, HD0])).then_inc(seq[c]["hi0"], 1)
                    copy(V0[:, c, :, 0:HD0], v).then_inc(seq[c]["hi0"], 1)
                yield
                keys_turned()
                yield
                yield
                yield
                maxima_turned(1, P)
                yield
                for m in range(8):
                    if m != 5:
                        exp_pair(AT0 + m)
                    if m == 4:
                        exp_pair(AT0 + 5)
                    yield
                products_out(1, AT0 + 8)
                for c in BOTH:
                    k = PB[:, c, 0:D].rearrange("p (h d) -> p h d", d=HD1)
                    v = PB[:, c, D:2 * D].rearrange("p (h d) -> p h d", d=HD1)
                    act.wait_ge(seq[c]["kv1"], at(j, "kv1"))
                    copy(KN1[:, c, :, :].rearrange("p h (a d) -> p h a d", a=2)[:, :, :, 0:8],
                         k[:, :, None, :].broadcast_to([P, 2 * H1, 2, HD1])).then_inc(seq[c]["hi1"], 1)
                    copy(V1[:, c, :, 0:HD1], v).then_inc(seq[c]["hi1"], 1)
                    act.activation(V1[:, c, :, HD1:2 * HD1], v, ACT.Square).then_inc(seq[c]["hi1"], 1)
                    if c == 0:
                        out_turned(0, 2, 1)
                yield
                out_turned(1, 2, 1)
                yield
                for c in BOTH:
                    act.wait_ge(seq[c]["q1"], at(j, "q1"))
                    q = PB[:, 2 + c, 0:D].rearrange("p (h d) -> p h d", d=HD1)
                    copy(QN1[:, c, :, 0:16].rearrange("p h (a d) -> p h a d", a=2),
                         q[:, :, None, :].broadcast_to([P, 2 * H1, 2, HD1]), float(HD1) ** -0.5).then_inc(seq[c]["hi1q"], 1)
                    act.wait_ge(seq[c]["xm1"], at(j, "xm1"))
                    act.activation(XSQ[:, c, :], XM1[:, c, :], ACT.Square, accum_out=SM[:, c, 1:2]).then_inc(seq[c]["sq1"], 1)
                    if c == 0:
                        yield
                yield
                keys_turned()
                yield
                yield
                yield
                yield
                yield
                act.wait_ge(sem["m_t"], at(j, "m_t", 2))
                for c in BOTH:
                    copy(two(QT[:, c, :, :]), h16(4 + c)).then_inc(sem["m_sb"], 1)
                yield
                for m in range(16):
                    exp_pair(AT1 + m)
                    if m % 2:
                        yield
                products_out(1, AT1 + 16)
                for c in BOTH:
                    act.wait_ge(seq[c]["var1"], at(j, "var1"))
                    act.activation(STD[:, c, :, :], VAR[:, c, :, :], ACT.Sqrt).then_inc(seq[c]["std1"], 1)
                for c in BOTH:
                    act.wait_ge(seq[c]["c_t"], at(j, "c_t"))
                    for n in range(NC):
                        act.activation(CT2[:, c, n, :], PB[:, 2 + c, P * n:P * n + P], ACT.Identity,
                                       bias=vec("lnb2", n), scale=vec("lng2", n)).then_inc(seq[c]["ct2_sb"], 1)
                yield
                for c in BOTH:
                    act.wait_ge(seq[c]["x2_t"], at(j, "x2_t"))
                    copy(two(X2T[:, c, :, :]), PB[:, 2 + c, D:2 * D]).then_inc(seq[c]["x2_sb"], 1)
                yield
                for c in BOTH:
                    act.wait_ge(seq[c]["proj2"], at(j, "proj2"))
                    q = PB[:, 2 + c, 0:D].rearrange("p (h d) -> p h d", d=HD2)
                    k = PB[:, c, 0:D].rearrange("p (h d) -> p h d", d=HD2)
                    v = PB[:, c, D:2 * D].rearrange("p (h d) -> p h d", d=HD2)
                    copy(QN2[:, c, :, 0:32].rearrange("p h (a d) -> p h a d", a=2),
                         q[:, :, None, :].broadcast_to([P, H2, 2, HD2]), float(HD2) ** -0.5).then_inc(seq[c]["hi2"], 1)
                    copy(KN2[:, c, :, :].rearrange("p h (a d) -> p h a d", a=2)[:, :, :, 0:16],
                         k[:, :, None, :].broadcast_to([P, H2, 2, HD2])).then_inc(seq[c]["hi2"], 1)
                    copy(V2[:, c, :, 0:HD2], v).then_inc(seq[c]["hi2"], 1)
                yield
                keys_turned()
                yield
                yield
                yield
                maxima_turned(3, P)
                yield
                for m in range(4):
                    exp_pair(AT2 + m)
                    yield
                act.wait_ge(seq[1]["o_back"], at(j, "o_back", 2))
                for c in BOTH:
                    act.wait_ge(sem["pv_done"], at(j, "pv_done", AT2 + 2 * c + 2))
                    copy(OTT[:, 4 * c:4 * c + 4, :].rearrange("p u t -> p (u t)"), PB[:, 4 + c, :]).then_inc(seq[c]["o_raw"], 1)
                yield
                for c in BOTH:
                    out_turned(c, 4, 2)
                yield
                yield

            def layer3(j, first):
                flat = lambda ap: ap.rearrange("p c b t -> p (c b t)")

                def affine(k, w, b):
                    act.wait_ge(sem["xh3_t"], at(j, "xh3_t", k))
                    for c in range(NC):
                        act.activation(XNT[:, c, :, 1:P + 1], PB[:, 6, D * c:D * c + D].rearrange("p (b t) -> p b t", b=2), ACT.Identity,
                                       bias=vec(b, c), scale=vec(w, c)).then_inc(sem["xnt3"], 1)

                yield
                affine(1, "ln1w", "ln1b")
                yield
                act.wait_ge(sem["xxx3"], at(j, "xxx3"))
                act.activation(XXT[:, :], PB[:, 7, 0:D], ACT.Tanh).then_inc(sem["xxt3"], 1)
                act.activation(XXT4[:, :], PB[0:32, 7, D:2 * D], ACT.Tanh).then_inc(sem["xxt3"], 1)
                yield
                yield
                yield
                act.wait_ge(sem["wd3_ps"], at(j, "wd3_ps"))
                act.activation(WD[:, :], PB[0:64, 7, 0:D], ACT.Tanh).then_inc(sem["wd3"], 1)
                yield
                act.wait_ge(sem["w3_ps"], at(j, "w3_ps"))
                act.activation(EW[:, 0, :, :].rearrange("p b t -> p (b t)"), PB[:, 6, 0:D], ACT.Exp, bias=vec("td", 0)).then_inc(sem["act3"], 1)
                act.activation(EW[:, 1, :, :].rearrange("p b t -> p (b t)"), PB[:, 6, D:2 * D], ACT.Exp, bias=vec("td", 1)).then_inc(sem["ew3"], 1)
                act.wait_ge(sem["act3"], at(j, "act3", 1))
                act.wait_ge(sem["ew3"], at(j, "ew3"))
                act.activation(WS[:, :, :, 1:P].rearrange("p c b t -> p (c b) t"), EW[:, :, :, 0:P - 1].rearrange("p c b t -> p (c b) t"),
                               ACT.Exp, scale=-1.0).then_inc(sem["ws3"], 1)
                act.wait_ge(sem["k3_ps"], at(j, "k3_ps"))
                copy(flat(KS[:, :, :, :]), PB[:, 7, :]).then_inc(sem["k3_sb"], 1)
                yield
                act.wait_ge(sem["vt3_ps"], at(j, "vt3_ps"))
                copy(flat(VT3[:, :, :, :]), PB[:, 6, :]).then_inc(sem["vt3_sb"], 1)
                yield
                act.wait_ge(sem["v3_ps"], at(j, "v3_ps"))
                copy(VN3[:, :], PB[:, 7, :]).then_inc(sem["v3_sb"], 1)
                act.wait_ge(sem["r3_ps"], at(j, "r3_ps"))
                copy(flat(RR[:, :, :, :]), PB[:, 6, :]).then_inc(sem["r3_sb"], 1)
                act.wait_ge(sem["g3_ps"], at(j, "g3_ps"))
                act.activation(GT[:, :], PB[:, 7, :], ACT.Tanh, scale=0.5).then_inc(sem["g3_sb"], 1)
                yield
                yield
                yield
                yield
                yield
                yield
                act.wait_ge(sem["att3"], at(j, "att3", 1))
                copy(ATR[:, :].rearrange("p a c b t -> p a (c b t)"), PB[:, 6:8, :]).then_inc(sem["att3_sb"], 1)
                yield
                act.wait_ge(sem["d83"], at(j, "d83"))
                act.activation(SQ[:, :], DD[:, :], ACT.Square).then_inc(sem["sq3"], 1)
                yield
                act.wait_ge(sem["var3"], at(j, "var3", 2))
                act.activation(G8[:, 2, :], G8[:, 1, :], ACT.Sqrt, bias=EPS3[:, :], scale=1.0 / S3).then_inc(sem["rstd3"], 1)
                yield
                act.wait_ge(sem["y3_t"], at(j, "y3_t"))
                copy(flat(YT[:, :, :, :]), PB[:, 6, :]).then_inc(sem["yt3_sb"], 1)
                yield
                yield
                yield
                affine(2, "ln2w", "ln2b")
                yield
                yield
                act.wait_ge(sem["ff1"], at(j, "ff1", 1))
                act.activation(flat(KKR[:, :, :, :]), PB[:, 7, :], ACT.Relu).then_inc(sem["act3"], 1)
                act.wait_ge(sem["act3"], at(j, "act3", 2))
                act.activation(KK[:, :, :, :], KKR[:, :, :, :], ACT.Square).then_inc(sem["kk3"], 1)
                act.wait_ge(sem["ff1"], at(j, "ff1", 2))
                act.activation(TR[:, :], PB[:, 6, :], ACT.Tanh, scale=0.5).then_inc(sem["tr3"], 1)
                yield
                yield
                act.wait_ge(sem["l3_done"], at(j, "l3_done"))
                act.activation(IDLE[:, 0:1], TG[:, :], ACT.Copy).then_inc(sem["act3"], 1)
                act.wait_ge(sem["act3"], at(j, "act3", 3))
                yield

            turns(act, attention, layer3)

        @block.gpsimd
        def _(pool):
            tt = pool.tensor_tensor
            pool.wait_ge(set_dve, 9)
            SPARE = IDLE[:, 1:2]

            def apart():
                tt(SPARE, NHALF[:, 0:1], NHALF[:, 1:2], ALU.add)

            def attention(j, first):
                own = Count(j)

                def rsqrt(c, k):
                    pool.wait_ge(seq[c]["var_in"], at(j, "var_in", k))
                    tt(RSTD[:, c:c + 1], VE[:, c:c + 1], NHALF[:, 0:1], ALU.pow).then_inc(seq[c]["rstd"], 1)

                pool.wait_ge(sem["m0_in"], at(j, "m0_in"))
                apart()
                pool.tensor_copy(MP[:, 0, :, :], M0[:, :, :]).then_inc(sem["mask_pool"], 1)
                pool.wait_ge(sem["mask_pool"], own("mask_pool"))
                tt(MR[:, :, :], M0[:, :, :], MP[:, 0, :, :], ALU.subtract).then_inc(sem["mask_pool"], 1)
                pool.wait_ge(sem["mask_pool"], own("mask_pool"))
                apart()
                pool.tensor_copy(MP[:, 1, :, :], MR[:, :, :]).then_inc(sem["mask_pool"], 1)
                pool.wait_ge(sem["mask_pool"], own("mask_pool"))
                tt(MR[:, :, :], MR[:, :, :], MP[:, 1, :, :], ALU.subtract).then_inc(sem["mask_pool"], 1)
                pool.wait_ge(sem["mask_pool"], own("mask_pool"))
                apart()
                pool.tensor_copy(MP[:, 2, :, :], MR[:, :, :]).then_inc(sem["mask_parts"], 1)
                for _ in range(6):
                    yield
                for m in range(8):
                    yield
                rsqrt(0, 1)
                yield
                yield
                rsqrt(1, 1)
                yield
                yield
                for c in BOTH:
                    pool.wait_ge(seq[c]["sq1"], at(j, "sq1"))
                    tt(SM[:, c, 3:4], SM[:, c, 0:1], SM[:, c, 2:3], ALU.mult).then_inc(seq[c]["pool"], 1)
                    pool.wait_ge(seq[c]["pool"], own("pool", c))
                    tt(SM[:, c, 4:5], SM[:, c, 1:2], SM[:, c, 2:3], ALU.mult)
                    tt(SM[:, c, 5:6], SM[:, c, 3:4], SM[:, c, 3:4], ALU.mult).then_inc(seq[c]["pool"], 1)
                    pool.wait_ge(seq[c]["pool"], own("pool", c))
                    tt(SM[:, c, 6:7], SM[:, c, 4:5], SM[:, c, 5:6], ALU.subtract).then_inc(seq[c]["pool"], 1)
                    pool.wait_ge(seq[c]["pool"], own("pool", c))
                    apart()
                    pool.tensor_scalar(SM[:, c, 7:8], SM[:, c, 6:7], 0.0, 1e-5, ALU.max, ALU.add).then_inc(seq[c]["pool"], 1)
                    pool.wait_ge(seq[c]["pool"], own("pool", c))
                    tt(SM[:, c, 4:5], SM[:, c, 7:8], NHALF[:, 0:1], ALU.pow).then_inc(seq[c]["pool"], 1)
                    pool.wait_ge(seq[c]["pool"], own("pool", c))
                    apart()
                    pool.tensor_scalar(XN1[:, c, :], XM1[:, c, :], SM[:, c, 3:4], SM[:, c, 4:5], ALU.subtract, ALU.mult).then_inc(seq[c]["pool"], 1)
                    pool.wait_ge(seq[c]["pool"], own("pool", c))
                    tt(XN1[:, c, :], XN1[:, c, :], MXF[:, c, :], ALU.mult).then_inc(seq[c]["xn1"], 1)
                for c in BOTH:
                    rsqrt(c, 2)
                own.end()
                for _ in range(46 - 18):
                    yield

            def layer3(j, first):
                def rsqrt3(k):
                    pool.wait_ge(sem["var3"], at(j, "var3", k))
                    tt(RSTD3[:, :], VE3[:, :], NHALF[:, 0:2], ALU.pow).then_inc(sem["rstd3"], 1)

                rsqrt3(1)
                yield
                yield
                yield
                yield
                for k, n in enumerate((1, 0, 2, 3, 4)):
                    pool.wait_ge(sem["t53"], at(j, "t53", k + 1))
                    tt(X5[:, n].rearrange("p c b t -> p (c b) t"), T5[:, k % 2].rearrange("p c b t -> p (c b) t"),
                       XNT[:, :, :, 1:P + 1].rearrange("p c b t -> p (c b) t"), ALU.add).then_inc(sem["x53"], 1)
                    if k in (1, 3):
                        yield
                yield
                yield
                yield
                yield
                for d in range(S3):
                    pool.wait_ge(sem["sc3"], at(j, "sc3", d + 1))
                    tt(A3[:, d], A3[:, d], RR[:, :, :, :], ALU.mult).then_inc(sem["pr3"], 1)
                    if d % 2:
                        yield
                yield
                yield
                yield
                yield
                yield
                rsqrt3(3)
                yield
                yield
                yield
                yield
                yield
                yield

            turns(pool, attention, layer3)

        @block.vector
        def _(dve):
            stt, tt, ts = dve.scalar_tensor_tensor, dve.tensor_tensor, dve.tensor_scalar
            for tile in (QN0, KN0, QN2, KN2, WS, MN, V0, V1, V2):
                dve.memset(tile[:], 0.0)
            dve.memset(ONES[:, :], 1.0)
            dve.memset(NHALF[:, :], -0.5)
            dve.memset(EPS3[:, :], 1e-5)
            dve.wait_ge(masks_in, 16 * N_MASKS)
            ts(MF[:, 0:2 * P], MRAW1[:, :], 1.0, NEG, ALU.subtract, ALU.mult)
            ts(MF[:, 2 * P:3 * P], MRAW2[:, :], 1.0, NEG, ALU.subtract, ALU.mult).then_inc(set_dve, 1)
            dve.wait_ge(set_dve, 1)
            dve.memset(V0[:, :, :, HD0:HD0 + 1], 1.0)
            dve.memset(V1[:, :, :, 2 * HD1:2 * HD1 + 1], 1.0)
            dve.memset(V2[:, :, :, HD2:HD2 + 1], 1.0)
            dve.memset(QN1[:, :, :, 24:25], NEG)
            dve.memset(KN1[:, :, :, 25:27], M_UNIT)
            dve.memset(QN2[:, :, :, 48:49], NEG)
            dve.tensor_copy(ROWP[:, 0, :], ROWS[:, :]).then_inc(set_dve, 1)
            dve.wait_ge(set_dve, 2)
            tt(ROWS[:, :], ROWS[:, :], ROWP[:, 0, :], ALU.subtract).then_inc(set_dve, 1)
            dve.wait_ge(set_dve, 3)
            dve.tensor_copy(ROWP[:, 1, :], ROWS[:, :]).then_inc(set_dve, 1)
            dve.wait_ge(set_dve, 4)
            tt(ROWP[:, 2, :], ROWS[:, :], ROWP[:, 1, :], ALU.subtract).then_inc(set_dve, 1)
            dve.wait_ge(set_dve, 5)
            ts(ROWP[:, 0, :], ROWP[:, 0, :], ID[0:3, 0:1], None, ALU.mult).then_inc(set_dve, 1)
            dve.wait_ge(set_dve, 6)
            stt(ROWP[:, 0, :], ROWP[:, 1, :], ID[0:3, 1:2], ROWP[:, 0, :], ALU.mult, ALU.add).then_inc(set_dve, 1)
            dve.wait_ge(set_dve, 7)
            stt(ROWP[:, 0, :], ROWP[:, 2, :], ID[0:3, 2:3], ROWP[:, 0, :], ALU.mult, ALU.add).then_inc(set_dve, 1)
            dve.wait_ge(set_dve, 8)
            dve.wait_ge(set_pe, 1)
            dve.tensor_copy(KM1[:, :, :].rearrange("p b a -> p a b"), h16(0)[:, 0:32].rearrange("p (a b) -> p a b", a=2)).then_inc(masks_in, 16)
            dve.tensor_copy(KM2[:, :, 0], h16(0)[:, 32:48]).then_inc(set_dve, 1)
            dve.wait_ge(masks_in, 16 * (N_MASKS + 1))
            dve.wait_ge(set_dve, 9)
            dve.wait_ge(w_in, 16 * N_WEIGHTS)
            dve.wait_ge(set_act, 1)
            km1 = KM1[:, :, :].rearrange("p (j c) a -> p j c a", c=2)
            km2 = KM2[:, :, :].rearrange("p (j c) a -> p j (c a)", c=2)

            def attention(j, first):
                own = Count(j)
                two = lambda ap: ap.rearrange("p a b -> p (a b)")

                def max_pair(m, dst, width):
                    base = AT0 if m < AT1 else AT1 if m < AT2 else AT2
                    dve.wait_ge(sem["max_scores"], at(j, "max_scores", m + 1))
                    bank = 2 * ((m - base) % 2)
                    dve.tensor_reduce(dst, PB[:, bank:bank + 2, :].rearrange("p b (h s) -> p (b h) s", s=width),
                                      X_AXIS, ALU.max, negate=True).then_inc(sem["max_read"], 1)

                def split_maxima(base, n_pairs, nm, nr, part):
                    dve.wait_ge(sem["max_read"], at(j, "max_read", base + 2 * n_pairs))
                    dve.tensor_copy(part(0), nm).then_inc(sem["m_split"], 1)
                    dve.wait_ge(sem["m_split"], own("m_split"))
                    tt(nr, nm, part(0), ALU.subtract).then_inc(sem["m_split"], 1)
                    dve.wait_ge(sem["m_split"], own("m_split"))
                    dve.tensor_copy(part(1), nr).then_inc(sem["m_split"], 1)
                    dve.wait_ge(sem["m_split"], own("m_split"))
                    tt(part(2), nr, part(1), ALU.subtract).then_inc(sem["nm"], 1)

                def queries_turned():
                    for c in BOTH:
                        own("qt_sb", c)
                        dve.wait_ge(seq[c]["packed_t"], at(j, "packed_t", 2 * own.given["qt_sb", c] - 1))
                        dve.tensor_copy(two(QT[:, c, :, :]), h16(2 + c)).then_inc(seq[c]["qt_sb"], 1)

                def products_out(c, m):
                    dve.wait_ge(sem["pv_done"], at(j, "pv_done", m))
                    dve.tensor_copy(OTT[:, :, :].rearrange("p (b u) t -> p b (u t)", u=4), PB[:, 4:6, :]).then_inc(seq[c]["o_raw"], 1)

                def normalise(c, banks, heads, hd, layer):
                    dve.wait_ge(seq[c]["o_back"], at(j, "o_back", layer))
                    o = PB[:, banks, :].rearrange("p a (h d) -> p (a h) d", d=VB)
                    dve.reciprocal(RS[:, c, 0:heads], o[:, :, hd]).then_inc(seq[c]["dve"], 1)
                    dve.wait_ge(seq[c]["dve"], own("dve", c))
                    tt(ON[:, c, :].rearrange("p (h d) -> p h d", d=hd), o[:, :, 0:hd],
                       RS[:, c, 0:heads, None].broadcast_to([P, heads, hd]), ALU.mult).then_inc(seq[c]["o_norm"], 1)

                def add_norm0(c):
                    dve.wait_ge(seq[c]["res"], at(j, "res", 1))
                    tt(XH[:, c, :], PB[:, 2 + c, D:2 * D], X[:, c, :], ALU.add).then_inc(seq[c]["dve"], 1)
                    dve.wait_ge(seq[c]["dve"], own("dve", c))
                    stats(c, XH[:, c, :], 1e-6)

                def stats(c, src, eps):
                    dve.bn_stats(ST[:, c, :], src).then_inc(seq[c]["dve"], 1)
                    dve.wait_ge(seq[c]["dve"], own("dve", c))
                    dve.memset(IDLE_DVE[:, 0:1], 0.0)
                    dve.bn_aggr(MV[:, c, :], ST[:, c, :]).then_inc(seq[c]["dve"], 1)
                    dve.wait_ge(seq[c]["dve"], own("dve", c))
                    ts(VE[:, c:c + 1], MV[:, c, 1:2], eps, None, ALU.add).then_inc(seq[c]["var_in"], 1)

                def apply_norm0(c):
                    dve.wait_ge(seq[c]["rstd"], at(j, "rstd", 1))
                    stt(XH[:, c, :], XH[:, c, :], MV[:, c, 0:1], BCR[:, BC["gamma0"], :], ALU.subtract, ALU.mult).then_inc(seq[c]["dve"], 1)
                    dve.wait_ge(seq[c]["dve"], own("dve", c))
                    stt(X1[:, c, :], XH[:, c, :], RSTD[:, c:c + 1], BCR[:, BC["beta0"], :], ALU.mult, ALU.add).then_inc(seq[c]["x1"], 1)

                yield
                for c in BOTH:
                    dve.wait_ge(seq[c]["hi0"], at(j, "hi0"))
                    q = PB[:, 2 + c, 0:D].rearrange("p (h d) -> p h d", d=HD0)
                    k = PB[:, 2 + c, D:D + 64].rearrange("p (h d) -> p h d", d=HD0)
                    stt(QN0[:, c, :, 16:24], q, float(HD0) ** -0.5, QN0[:, c, :, 0:8], ALU.mult, ALU.subtract).then_inc(seq[c]["lo0"], 1)
                    tt(KN0[:, c, :, :, 8:16], k[:, :, None, :].broadcast_to([P, KV0, 4, HD0]), KN0[:, c, :, :, 0:8],
                       ALU.subtract).then_inc(seq[c]["lo0"], 1)
                yield
                queries_turned()
                yield
                for c in BOTH:
                    for n in range(4):
                        max_pair(4 * c + n, NM[:, c, 8 * n:8 * n + 8], P)
                    yield
                split_maxima(AT0, 4, NM[:, :, :], NR[:, :, :], lambda k: MN[:, :, 0, 32 * k:32 * k + 32])
                if not first:
                    dve.wait_ge(sem["x3_free"], at(j - 1, "x3_free"))
                dve.tensor_copy(STC[:, :, :, :], CXT[:, :, 0:NC, 0:2]).then_inc(sem["st_cols"], 1)
                dve.wait_ge(sem["mx_in"], at(j, "mx_in"))
                dve.tensor_copy(MXF[:, :, :], MXR[:, :, :]).then_inc(sem["mx_step"], 1)
                for c in BOTH:
                    dve.tensor_copy(KN1[:, c, :, 24].rearrange("p (a h) -> p a h", a=2),
                                    km1[:, j, c, :][:, :, None].broadcast_to([P, 2, H1])).then_inc(seq[c]["lo1"], 1)
                    dve.tensor_copy(KN2[:, c, :, 48], km2[:, j, c:c + 1].broadcast_to([P, H2])).then_inc(seq[c]["lo2"], 1)
                dve.wait_ge(sem["mx_step"], own("mx_step"))
                dve.tensor_reduce(SM[:, :, 2], MXF[:, :, :], X_AXIS, ALU.add).then_inc(sem["mx_step"], 1)
                dve.wait_ge(sem["mx_step"], own("mx_step"))
                dve.reciprocal(SM[:, :, 2], SM[:, :, 2]).then_inc(sem["mx_step"], 1)
                dve.wait_ge(sem["mx_step"], own("mx_step"))
                yield
                for m in range(8):
                    if m == 4:
                        products_out(0, AT0 + 4)
                        normalise(0, slice(4, 6), H0, HD0, 1)
                    yield
                normalise(1, slice(4, 6), H0, HD0, 1)
                for c in BOTH:
                    dve.wait_ge(seq[c]["hi1"], at(j, "hi1"))
                    k = PB[:, c, 0:D].rearrange("p (h d) -> p h d", d=HD1)
                    tt(KN1[:, c, :, 8:16], k, KN1[:, c, :, 0:8], ALU.subtract).then_inc(seq[c]["lo1"], 1)
                add_norm0(0)
                yield
                apply_norm0(0)
                yield
                add_norm0(1)
                for c in BOTH:
                    if c == 1:
                        yield
                        apply_norm0(1)
                    dve.wait_ge(seq[c]["x1"], at(j, "x1"))
                    tt(XM1[:, c, :], X1[:, c, :], MXF[:, c, :], ALU.mult).then_inc(seq[c]["dve"], 1)
                    dve.wait_ge(seq[c]["dve"], own("dve", c))
                    dve.tensor_reduce(SM[:, c, 0:1], XM1[:, c, :], X_AXIS, ALU.add).then_inc(seq[c]["xm1"], 1)
                    dve.wait_ge(seq[c]["hi1q"], at(j, "hi1q"))
                    q = PB[:, 2 + c, 0:D].rearrange("p (h d) -> p h d", d=HD1)
                    stt(QN1[:, c, :, 16:24], q, float(HD1) ** -0.5, QN1[:, c, :, 0:8], ALU.mult, ALU.subtract).then_inc(seq[c]["lo1"], 1)
                yield
                queries_turned()
                for c in BOTH:
                    dve.wait_ge(seq[c]["x1"], at(j, "x1"))
                    stats(c, C[:, c, :], 1e-5)
                yield
                for c in BOTH:
                    for n in range(8):
                        max_pair(AT1 + 8 * c + n, NM[:, c, 16 * (n // 4) + n % 4:16 * (n // 4) + 16:4], D)
                        if n % 4 == 3:
                            yield
                dve.wait_ge(sem["max_read"], at(j, "max_read", AT1 + 16))
                nm = NM[:, :, :].rearrange("p c h -> p (c h)")
                hi, lo = (QN1[:, :, :, n].rearrange("p c h -> p (c h)") for n in (25, 26))
                ts(hi, nm, 1.0 / M_UNIT, None, ALU.mult).then_inc(sem["m_split"], 1)
                dve.wait_ge(sem["m_split"], own("m_split"))
                stt(lo, nm, 1.0 / M_UNIT, hi, ALU.mult, ALU.subtract).then_inc(sem["nm"], 1)
                yield

                def moments(c):
                    dve.wait_ge(seq[c]["o_back"], at(j, "o_back", 2))
                    o = PB[:, 4:6, :].rearrange("p a (h d) -> p a h d", d=VB)
                    rs = RS[:, c, :].rearrange("p (a h) -> p a h", a=2)
                    rsb = rs[:, :, :, None].broadcast_to([P, 2, H1, HD1])
                    v4 = lambda tile: tile[:, c, :, :].rearrange("p a (h d) -> p a h d", d=HD1)
                    v2 = lambda tile: tile[:, c, :, :].rearrange("p a b -> p (a b)")
                    dve.reciprocal(rs, o[:, :, :, 16]).then_inc(seq[c]["dve"], 1)
                    dve.wait_ge(seq[c]["dve"], own("dve", c))
                    tt(v4(MEAN), o[:, :, :, 0:8], rsb, ALU.mult).then_inc(seq[c]["dve"], 1)
                    tt(v4(EX2), o[:, :, :, 8:16], rsb, ALU.mult).then_inc(seq[c]["o_norm"], 1)
                    dve.wait_ge(seq[c]["dve"], own("dve", c))
                    tt(v2(VAR), v2(MEAN), v2(MEAN), ALU.mult).then_inc(seq[c]["dve"], 1)
                    dve.wait_ge(seq[c]["dve"], own("dve", c))
                    dve.wait_ge(seq[c]["o_norm"], at(j, "o_norm", 2))
                    tt(v2(VAR), v2(EX2), v2(VAR), ALU.subtract).then_inc(seq[c]["dve"], 1)
                    dve.wait_ge(seq[c]["dve"], own("dve", c))
                    ts(v2(VAR), v2(VAR), 0.0, None, ALU.max).then_inc(seq[c]["var1"], 1)

                for m in range(16):
                    if m == 2:
                        for c in BOTH:
                            dve.wait_ge(seq[c]["rstd"], at(j, "rstd", 2))
                            ts(CH[:, c, :], C[:, c, :], MV[:, c, 0:1], RSTD[:, c:c + 1], ALU.subtract, ALU.mult).then_inc(seq[c]["c_hat"], 1)
                    if m == 8:
                        products_out(0, AT1 + 8)
                        moments(0)
                    if m % 2:
                        yield
                moments(1)
                for c in BOTH:
                    dve.wait_ge(seq[c]["ms_t"], at(j, "ms_t"))
                    dve.wait_ge(seq[c]["xn1"], at(j, "xn1"))
                    tt(X2[:, c, :], XN1[:, c, :], PB[:, c, D:2 * D], ALU.mult).then_inc(seq[c]["dve"], 1)
                for c in BOTH:
                    dve.wait_ge(seq[c]["dve"], own("dve", c))
                    tt(X2[:, c, :], X2[:, c, :], PB[:, c, 0:D], ALU.add).then_inc(seq[c]["dve"], 1)
                for c in BOTH:
                    dve.wait_ge(seq[c]["dve"], own("dve", c))
                    tt(X2[:, c, :], X2[:, c, :], MXF[:, c, :], ALU.mult).then_inc(seq[c]["x2"], 1)
                yield
                yield
                for c in BOTH:
                    dve.wait_ge(seq[c]["hi2"], at(j, "hi2"))
                    q = PB[:, 2 + c, 0:D].rearrange("p (h d) -> p h d", d=HD2)
                    k = PB[:, c, 0:D].rearrange("p (h d) -> p h d", d=HD2)
                    stt(QN2[:, c, :, 32:48], q, float(HD2) ** -0.5, QN2[:, c, :, 0:16], ALU.mult, ALU.subtract).then_inc(seq[c]["lo2"], 1)
                    tt(KN2[:, c, :, 16:32], k, KN2[:, c, :, 0:16], ALU.subtract).then_inc(seq[c]["lo2"], 1)
                yield
                queries_turned()
                yield
                for c in BOTH:
                    for r in range(2):
                        max_pair(AT2 + 2 * c + r, NM[:, c, 8 * r:8 * r + 8], P)
                    yield
                split_maxima(AT2, 2, NM[:, :, 0:16], NR[:, :, 0:16], lambda k: MN[:, :, 0, 16 * k:16 * k + 16])
                yield
                for m in range(4):
                    yield
                for c in BOTH:
                    normalise(c, slice(4 + c, 5 + c), H2, HD2, 3)
                yield
                yield
                if not first:
                    dve.wait_ge(sem["x3_free"], at(j - 1, "x3_free"))
                for c in BOTH:
                    dve.wait_ge(seq[c]["res"], at(j, "res", 2))
                    stt(X3[:, c, :], PB[:, 4 + c, D:2 * D], TG[:, 0:1], X2[:, c, :], ALU.mult, ALU.add).then_inc(seq[c]["x3"], 1)
                own.end()
                yield

            def layer3(j, first):
                own = Count(j)

                def stats3(src):
                    for b in BOTH:
                        last = dve.bn_stats(ST3[:, b, :], src[:, b, :])
                    last.then_inc(sem["dve3"], 1)
                    dve.wait_ge(sem["dve3"], own("dve3"))
                    dve.memset(IDLE_DVE[:, 0:1], 0.0)
                    for b in BOTH:
                        last = dve.bn_aggr(MV3[:, b, :], ST3[:, b, :])
                    last.then_inc(sem["dve3"], 1)
                    dve.wait_ge(sem["dve3"], own("dve3"))
                    ts(VE3[:, :], MV3[:, :, 1], 1e-5, None, ALU.add).then_inc(sem["var3"], 1)

                def norm3(src, k):
                    dve.wait_ge(sem["rstd3"], at(j, "rstd3", k))
                    for b in BOTH:
                        last = ts(XH3[:, b, :], src[:, b, :], MV3[:, b, 0:1], RSTD3[:, b:b + 1], ALU.subtract, ALU.mult)
                    last.then_inc(sem["xh3"], 1)

                def shift(col, k):
                    dve.tensor_copy(XNT[:, :, :, 0], STC3[:, :, :, col].rearrange("p b c -> p c b")).then_inc(sem["dve3"], 1)
                    dve.wait_ge(sem["dve3"], own("dve3"))
                    dve.wait_ge(sem["xnt3"], at(j, "xnt3", k))
                    tt(SX[:, :, :, :].rearrange("p c b t -> p (c b) t"), XNT[:, :, :, 0:P].rearrange("p c b t -> p (c b) t"),
                       XNT[:, :, :, 1:P + 1].rearrange("p c b t -> p (c b) t"), ALU.subtract).then_inc(sem["dve3"], 1)
                    dve.wait_ge(sem["dve3"], own("dve3"))

                for b in BOTH:
                    dve.wait_ge(seq[b]["x3"], at(j, "x3"))
                stats3(X3)
                dve.tensor_copy(X3L[:, :, :], X3[:, :, :]).then_inc(sem["dve3"], 1)
                dve.wait_ge(sem["dve3"], own("dve3"))
                dve.wait_ge(sem["st_cols"], at(j, "st_cols"))
                dve.tensor_copy(STC3[:, :, :, :], STC[:, :, :, :]).then_inc(sem["x3_free"], 1)
                yield
                norm3(X3L, 1)
                dve.wait_ge(sem["x3_free"], at(j, "x3_free"))
                shift(1, 2)
                for c in range(NC):
                    last = stt(XM[:, c], SX[:, c], vec("maax", c), XNT[:, c, :, 1:P + 1], ALU.mult, ALU.add)
                last.then_inc(sem["xm3"], 1)
                yield
                yield
                for k, n in enumerate((1, 0, 2, 3, 4)):
                    dve.wait_ge(sem["mix3"], at(j, "mix3", k + 1))
                    if k >= 2:
                        dve.wait_ge(sem["x53"], at(j, "x53", k - 1))
                    for c in range(NC):
                        last = stt(T5[:, k % 2, c].rearrange("p b t -> p (b t)"), PB[:, 6 + k % 2, D * c:D * c + D], vec(f"st{n}", c),
                                   SX[:, c].rearrange("p b t -> p (b t)"), ALU.add, ALU.mult)
                    last.then_inc(sem["t53"], 1)
                    if k in (1, 3):
                        yield
                yield
                yield
                yield
                dve.wait_ge(sem["g3_sb"], at(j, "g3_sb"))
                stt(GT[:, :], GT[:, :], 1.0, PB[:, 7, :], ALU.add, ALU.mult).then_inc(sem["gt3"], 1)
                dve.wait_ge(sem["r3_sb"], at(j, "r3_sb"))
                for c in range(NC):
                    last = stt(RUK[:, c], RR[:, c], vec("u", c), KS[:, c], ALU.mult, ALU.mult)
                last.then_inc(sem["ruk3"], 1)
                dve.wait_ge(sem["s0_in"], at(j, "s0_in"))
                for b in BOTH:
                    last = dve.tensor_copy(A3[:, :, :, b, 0], S0[:, b, :, :].rearrange("p c d -> p d c"))
                last.then_inc(sem["s0_read"], 1)
                yield
                dve.wait_ge(sem["ws3"], at(j, "ws3"))
                dve.wait_ge(sem["s0_read"], at(j, "s0_read"))
                for d in range(S3):
                    dve.wait_ge(sem["vd3"], at(j, "vd3", d + 1))
                    vd = PB[:, 6 + d % 2, :].rearrange("p (n t) -> p n t", t=P)
                    tt(A3[:, d, :, :, 1:P].rearrange("p c b t -> p (c b) t"), vd[:, :, 0:P - 1],
                       KS[:, :, :, 0:P - 1].rearrange("p c b t -> p (c b) t"), ALU.mult).then_inc(sem["a3"], 1)
                    dve.wait_ge(sem["a3"], own("a3"))
                    dve.tensor_tensor_scan(A3[:, d].rearrange("p c b t -> p (c b t)"), WS[:, :, :, :].rearrange("p c b t -> p (c b t)"),
                                           A3[:, d].rearrange("p c b t -> p (c b t)"), 0.0, ALU.mult, ALU.add).then_inc(sem["sc3"], 1)
                    if d % 2:
                        yield
                yield
                h3 = lambda ap: ap.rearrange("p (h d) -> p h d", d=S3)
                b8 = lambda ap: ap[:, :, None].broadcast_to([P, 2 * H3, S3])
                dve.wait_ge(sem["att3"], at(j, "att3"))
                sums = PB[:, 6:8, :].rearrange("p b (c d h) -> p (b c) h d", c=NC, h=32)
                att = ATT[:, :].rearrange("p (n h d) -> p n h d", h=16, d=S3)
                tt(att, VN3[:, :].rearrange("p (n h d) -> p n h d", h=16, d=S3),
                   sums[:, :, 16:32, 0:1].broadcast_to([P, 2 * NC, 16, S3]), ALU.mult).then_inc(sem["dve3"], 1)
                dve.wait_ge(sem["dve3"], own("dve3"))
                tt(att, att, sums[:, :, 0:16, :], ALU.add).then_inc(sem["att3_read"], 1)
                dve.wait_ge(sem["att3_read"], at(j, "att3_read"))
                dve.tensor_reduce(G8[:, 0, :], h3(ATT[:, :]), X_AXIS, ALU.add).then_inc(sem["dve3"], 1)
                dve.wait_ge(sem["dve3"], own("dve3"))
                stt(h3(DD[:, :]), b8(G8[:, 0, :]), -1.0 / S3, h3(ATT[:, :]), ALU.mult, ALU.add).then_inc(sem["d83"], 1)
                yield
                two_seqs = lambda ap: ap.rearrange("p (b d) -> p b d", b=2)
                of_both = lambda name: BCR[:, BC[name]:BC[name] + 1, :].broadcast_to([P, 2, D])
                stt(two_seqs(GB), two_seqs(GT[:, :]), 0.5, of_both("gnb"), ALU.mult, ALU.mult).then_inc(sem["dve3"], 1)
                dve.wait_ge(sem["dve3"], own("dve3"))
                stt(two_seqs(GT[:, :]), two_seqs(GT[:, :]), 0.5, of_both("gnw"), ALU.mult, ALU.mult).then_inc(sem["dve3"], 1)
                dve.wait_ge(sem["dve3"], own("dve3"))
                dve.wait_ge(sem["d83"], at(j, "d83"))
                tt(ATT[:, :], DD[:, :], GT[:, :], ALU.mult).then_inc(sem["dve3"], 1)
                dve.wait_ge(sem["dve3"], own("dve3"))
                yield
                dve.wait_ge(sem["sq3"], at(j, "sq3"))
                dve.tensor_reduce(G8[:, 1, :], h3(SQ[:, :]), X_AXIS, ALU.add).then_inc(sem["var3"], 1)
                yield
                dve.wait_ge(sem["rstd3"], at(j, "rstd3", 2))
                dve.reciprocal(G8[:, 2, :], G8[:, 2, :]).then_inc(sem["dve3"], 1)
                dve.wait_ge(sem["dve3"], own("dve3"))
                tt(h3(Y[:, :]), h3(ATT[:, :]), b8(G8[:, 2, :]), ALU.mult).then_inc(sem["dve3"], 1)
                dve.wait_ge(sem["dve3"], own("dve3"))
                tt(Y[:, :], Y[:, :], GB, ALU.add).then_inc(sem["y3"], 1)
                yield
                yield
                dve.wait_ge(sem["y3_o"], at(j, "y3_o"))
                tt(X4[:, :, :], PB[:, 7, :].rearrange("p (b d) -> p b d", b=2), X3L[:, :, :], ALU.add).then_inc(sem["dve3"], 1)
                dve.wait_ge(sem["dve3"], own("dve3"))
                stats3(X4)
                yield
                norm3(X4, 3)
                yield
                shift(0, 4)
                for n, name in enumerate(("fmk", "fmr")):
                    for c in range(NC):
                        stt(XKR[:, n, c], SX[:, c], vec(name, c), XNT[:, c, :, 1:P + 1], ALU.mult, ALU.add).then_inc(sem["xkr3"], 1)
                yield
                yield
                dve.wait_ge(sem["ff2"], at(j, "ff2"))
                dve.wait_ge(sem["tr3"], at(j, "tr3"))
                stt(TR[:, :], TR[:, :], 1.0, PB[:, 7, :], ALU.add, ALU.mult).then_inc(sem["dve3"], 1)
                dve.wait_ge(sem["dve3"], own("dve3"))
                dve.wait_ge(sem["out_stored"], at(j, "out_stored"))
                stt(OUT[:, :, :], TR[:, :].rearrange("p (b d) -> p b d", b=2), 0.5, X4[:, :, :], ALU.mult, ALU.add).then_inc(sem["l3_done"], 1)
                own.end()
                yield
                yield

            turns(dve, attention, layer3)


def kernel(**inputs):
    import numpy as np
    import ml_dtypes
    import concourse.bacc as bacc
    from concourse.bass_utils import run_bass_kernel_spmd as run

    a = {k: np.asarray(v) for k, v in inputs.items()}
    L0, L1, L2, L3 = (lambda n, p=f"L{k}_xattn_": a[p + n] for k in range(4))
    cat = np.concatenate
    wo0 = L0("Wo").reshape(2, 4, 4, HD0, D).transpose(0, 2, 1, 3, 4).reshape(D, D)
    wo2 = L2("Wo").T.reshape(2, 4, 2, HD2, D).transpose(2, 0, 1, 3, 4).reshape(D, D)
    wall = cat([L0("Wq"), L0("Wk"), L0("Wv"), wo0, L2("Wk").T, L2("Wv").T, L2("Wq").T, wo2,
                L3("maa_w1"), L3("decay_w1"), L3("Wr").T, L3("Wk").T, L3("Wv").T, L3("Wg").T, L3("Wo").T,
                L3("ffn_Wk").T, L3("ffn_Wr").T, L3("ffn_Wv").T], axis=1)
    w1 = cat([L1("Wq").T, L1("Wk").T, L1("Wv").T], axis=1)
    rows = cat([L0("bq"), L0("bk"), L0("bv"), L0("bo"), L1("bq"), L1("bk"), L1("bv")]).reshape(1, -1)
    bcast = cat([L0("gamma"), L0("beta"), L3("gn_w"), L3("gn_b")]).reshape(1, -1)
    st = L3("maa_stack")
    cols = np.stack([L2("ln_gamma"), L2("ln_beta"), L3("ln1_w"), L3("ln1_b"), L3("ln2_w"), L3("ln2_b"), L3("maa_x"),
                     st[0], st[1], st[2], st[3], st[4], L3("time_decay"), L3("faaaa").reshape(-1),
                     L3("ffn_maa_k"), L3("ffn_maa_r")], axis=1)
    ident = np.eye(P, dtype=np.float32)
    pick0 = np.zeros((P, 32), ml_dtypes.bfloat16)
    pick0[:96] = np.tile(np.eye(32), (3, 1))
    pick1 = np.zeros((P, 16), ml_dtypes.bfloat16)
    pick1[:48] = np.tile(np.eye(16), (3, 1))
    gsel = np.repeat(np.eye(16, 32, dtype=np.float32), S3, axis=0)
    srep = np.zeros((16, S3, S3, 16, S3), np.float32)
    for h in range(16):
        for d in range(S3):
            srep[h, d, d, h, :] = 1.0
    arrays = dict(
        x=a["x"], ctx_in=a["ctx_2048"], mask0=a["mask_Bx1xSxS2_ff0"].reshape(B, T, T),
        mask1=a["mask_Bx1x2048_bf1"].view(np.uint8), mask2=a["mask_BxS2_bf1"].view(np.uint8),
        wall=wall, w1=w1, maaw2=L3("maa_w2").reshape(160, D), decw2=L3("decay_w2"), rows=rows, bcast=bcast, cols=cols,
        gate=L2("gate").reshape(1, 1), ident=ident, ident_h=ident.astype(np.float16),
        ident_b=ident.astype(ml_dtypes.bfloat16), pick0=pick0, pick1=pick1, gsel=gsel, srep=srep.reshape(P, S3, P))
    arrays = {k: np.ascontiguousarray(v) for k, v in arrays.items()}
    nc = bacc.Bacc("TRN2", target_bir_lowering=False, num_devices=1)
    args = {k: nc.dram_tensor("in_" + k, v.shape, mybir.dt.from_np(v.dtype), kind="ExternalInput").ap()
            for k, v in arrays.items()}
    out = nc.dram_tensor("out_x", (B, T, D), F32, kind="ExternalOutput").ap()
    build(nc, out=out, **args)
    r = run(nc, [{"in_" + k: v for k, v in arrays.items()}], core_ids=[0])
    return r.results[0]["out_x"]
```
